# Optimizing a Trainium2 kernel written in Bass

```python
import numpy as np
import jax
import jax.numpy as jnp

def _softmax(x, axis=-1):
    return jax.nn.softmax(x, axis=axis)

def _gelu(x):
    return jax.nn.gelu(x, approximate=True)

def _silu(x):
    return jax.nn.silu(x)

def _sigmoid(x):
    return jax.nn.sigmoid(x)

def _layernorm(x, axis=-1, eps=1e-05):
    m = jnp.mean(x, axis=axis, keepdims=True)
    v = jnp.var(x, axis=axis, keepdims=True)
    return (x - m) / jnp.sqrt(v + eps)

def _scatter_add(tgt, idx, src, axis=0):
    return tgt.at[idx].add(src)

def _segment_sum(src, seg, n):
    return jax.ops.segment_sum(src, seg, n)
kernel_name = 'mk_decoder_postln_d2_seqx_r8_44b737'

def setup_inputs(seed: int=0):
    np.random.seed(seed)
    _w = jnp.asarray

    def _rec_inputs():
        import jax
        import jax.numpy as jnp
        _rk = jax.random.key(seed)
        x = -0.0003929 + 0.9999 * jax.random.normal(jax.random.fold_in(_rk, 1), (32, 64, 256), jnp.float32)
        _lenS = 64 - jax.random.randint(jax.random.fold_in(_rk, 7), (32,), 0, max(1, 64 // 4) + 1, jnp.int32)
        _lenS2 = 64 - jax.random.randint(jax.random.fold_in(_rk, 8), (32,), 0, max(1, 64 // 4) + 1, jnp.int32)
        _ctx_1024P = jax.random.normal(jax.random.fold_in(_rk, 11), (32, 16, 128), jnp.float32)
        _ctx_1024c = jax.random.dirichlet(jax.random.fold_in(_rk, 511), 0.3 * jnp.ones((16,), jnp.float32), (32, 64))
        _ctx_1024t = jnp.einsum('bsk,bkd->bsd', _ctx_1024c, _ctx_1024P)
        _ctx_1024t = _ctx_1024t * jax.lax.rsqrt(jnp.mean(jnp.square(_ctx_1024t)) + 1e-12) * 0.953939
        ctx_1024 = 0.000227908 + 0.99994 * (_ctx_1024t + 0.3 * jax.random.normal(jax.random.fold_in(_rk, 611), (32, 64, 128), jnp.float32))
        _validS = jnp.arange(64)[None, :] < _lenS[:, None]
        _validS2 = jnp.arange(64)[None, :] < _lenS2[:, None]
        _causal = jnp.tril(jnp.ones((64, 64), dtype=bool))
        mask_BxS2_bf1 = jnp.ones((32, 64), dtype=bool)
        return (x, ctx_1024, mask_BxS2_bf1)
    x, ctx_1024, mask_BxS2_bf1 = _rec_inputs()

    def _L0_attn_setup():
        import jax, jax.numpy as jnp
        import numpy as np
        B, T, HID, H = (2, 256, 256, 16)
        D = HID // H

        def apply_rope(x):
            b, t, h, d = x.shape
            half = d // 2
            x1, x2 = (x[..., :half], x[..., half:])
            theta = 1.0 / 10000.0 ** (jnp.arange(0, half, 2, dtype=jnp.float32) / half)
            pos = jnp.arange(t, dtype=jnp.float32)
            freq = pos[:, None] * theta[None, :]
            sin = jnp.sin(freq)[None, :, None, :]
            cos = jnp.cos(freq)[None, :, None, :]
            x1e, x1o = (x1[..., ::2], x1[..., 1::2])
            x2e, x2o = (x2[..., ::2], x2[..., 1::2])
            x1r = jnp.concatenate([x1e * cos - x1o * sin, x1e * sin + x1o * cos], axis=-1)
            x2r = jnp.concatenate([x2e * cos - x2o * sin, x2e * sin + x2o * cos], axis=-1)
            return jnp.concatenate([x1r, x2r], axis=-1)
        key = jax.random.key(seed)
        ks = jax.random.split(key, 5)
        s = 0.02
        return {'hidden_states': jax.random.normal(ks[0], (B, T, HID), dtype=jnp.float32), 'Wq': jax.random.normal(ks[1], (HID, HID), dtype=jnp.float32) * s, 'Wk': jax.random.normal(ks[2], (D, HID), dtype=jnp.float32) * s, 'Wv': jax.random.normal(ks[3], (D, HID), dtype=jnp.float32) * s, 'Wo': jax.random.normal(ks[4], (HID, HID), dtype=jnp.float32) * s}
    _L0_attn_all = _L0_attn_setup()
    _L0_attn_in = {k: v for k, v in _L0_attn_all.items() if k in ('Wq', 'Wk', 'Wv', 'Wo')}
    del _L0_attn_all

    def _L0_xattn_setup():
        import jax, jax.numpy as jnp
        import numpy as np
        EPS = 1e-05

        def rmsnorm(x, g, eps=EPS):
            var = jnp.mean(jnp.square(x), axis=-1, keepdims=True)
            return x * jax.lax.rsqrt(var + eps) * g
        key = jax.random.key(seed)
        ks = jax.random.split(key, 8)
        B, Sq, Skv = (2, 512, 64)
        dim, cdim, H, D = (256, 128, 16, 128)
        inner = H * D
        s = lambda f: 1.0 / np.sqrt(f)
        return {'hidden_states': jax.random.normal(ks[0], (B, Sq, dim), jnp.float32), 'encoder_hidden_states': jax.random.normal(ks[1], (B, Skv, cdim), jnp.float32), 'Wq': jax.random.normal(ks[2], (dim, inner), jnp.float32) * s(dim), 'Wk': jax.random.normal(ks[3], (cdim, inner), jnp.float32) * s(cdim), 'Wv': jax.random.normal(ks[4], (cdim, inner), jnp.float32) * s(cdim), 'Wo': jax.random.normal(ks[5], (inner, dim), jnp.float32) * s(inner), 'gq': jnp.ones((D,), jnp.float32), 'gk': jnp.ones((D,), jnp.float32)}
    _L0_xattn_all = _L0_xattn_setup()
    _L0_xattn_in = {k: v for k, v in _L0_xattn_all.items() if k in ('Wq', 'Wk', 'Wv', 'Wo', 'gq', 'gk')}
    del _L0_xattn_all

    def _L0_ffn_setup():
        import jax, jax.numpy as jnp
        import numpy as np
        HIDDEN = 256
        INTER = 1024
        B, S = (4, 128)

        def _qmatmul(x, w_int8, scale):
            y = jnp.einsum('bsh,ho->bso', x, w_int8.astype(x.dtype))
            return y * scale
        key = jax.random.key(seed)
        ks = jax.random.split(key, 7)
        x = jax.random.normal(ks[0], (B, S, HIDDEN), dtype=jnp.float32)
        w_gate = jax.random.randint(ks[1], (HIDDEN, INTER), -128, 128, dtype=jnp.int32).astype(jnp.int8)
        w_up = jax.random.randint(ks[2], (HIDDEN, INTER), -128, 128, dtype=jnp.int32).astype(jnp.int8)
        w_down = jax.random.randint(ks[3], (INTER, HIDDEN), -128, 128, dtype=jnp.int32).astype(jnp.int8)
        s_gate = jax.random.uniform(ks[4], (INTER,), dtype=jnp.float32) * 0.02 + 0.001
        s_up = jax.random.uniform(ks[5], (INTER,), dtype=jnp.float32) * 0.02 + 0.001
        s_down = jax.random.uniform(ks[6], (HIDDEN,), dtype=jnp.float32) * 0.02 + 0.001
        return {'x': x, 'w_gate': w_gate, 'w_up': w_up, 'w_down': w_down, 's_gate': s_gate, 's_up': s_up, 's_down': s_down}
    _L0_ffn_all = _L0_ffn_setup()
    _L0_ffn_in = {k: v for k, v in _L0_ffn_all.items() if k in ('w_gate', 'w_up', 'w_down', 's_gate', 's_up', 's_down')}
    del _L0_ffn_all

    def _L1_attn_setup():
        import jax, jax.numpy as jnp
        import numpy as np
        H = 16
        D = 128
        M = 16
        ROPE = 64
        THETA = 10000.0
        WIN = 64
        CAP = 50.0
        G = 4
        HID = 256
        QC = 64
        INTER = 256

        def rope_cache(t):
            inv = 1.0 / THETA ** (jnp.arange(0, ROPE, 2, dtype=jnp.float32) / ROPE)
            ang = jnp.arange(t, dtype=jnp.float32)[:, None] * inv[None, :]
            return (jnp.cos(ang), jnp.sin(ang))

        def apply_partial_rope(x, cos, sin):
            x1 = x[..., :ROPE // 2]
            x2 = x[..., ROPE // 2:ROPE]
            rest = x[..., ROPE:]
            return jnp.concatenate([x1 * cos - x2 * sin, x1 * sin + x2 * cos, rest], axis=-1)

        def rmsnorm(x, w, eps=1e-06):
            return x * jax.lax.rsqrt(jnp.mean(x * x, axis=-1, keepdims=True) + eps) * w

        def attend(scores, mask, sink, v, sub):
            b, h, t, _ = scores.shape
            logits = jnp.where(mask, scores, jnp.float32(-1e+30))
            sink_col = jnp.broadcast_to(sink[None, :, None, None], (b, h, t, 1))
            probs = jax.nn.softmax(jnp.concatenate([logits, sink_col], axis=-1), axis=-1)[..., :-1]
            return jnp.einsum(sub, probs, v)
        key = jax.random.key(seed)
        ks = jax.random.split(key, 12)
        s = 0.02
        return {'h': jax.random.normal(ks[0], (2, 256, HID), dtype=jnp.float32), 'Wq_c': jax.random.normal(ks[1], (HID, QC), dtype=jnp.float32) * s, 'Wq_up': jax.random.normal(ks[2], (QC, H * D), dtype=jnp.float32) * s, 'Wk': jax.random.normal(ks[3], (HID, D), dtype=jnp.float32) * s, 'Wv': jax.random.normal(ks[4], (HID, D), dtype=jnp.float32) * s, 'W_comp': jax.random.normal(ks[5], (M * HID, D), dtype=jnp.float32) * s, 'q_norm_w': jnp.ones((D,), dtype=jnp.float32), 'k_norm_w': jnp.ones((D,), dtype=jnp.float32), 'sink': jnp.zeros((H,), dtype=jnp.float32), 'Wg': jax.random.normal(ks[6], (G, H // G * D, INTER), dtype=jnp.float32) * s, 'Wo': jax.random.normal(ks[7], (G * INTER, HID), dtype=jnp.float32) * s}
    _L1_attn_all = _L1_attn_setup()
    _L1_attn_in = {k: v for k, v in _L1_attn_all.items() if k in ('Wq_c', 'Wq_up', 'Wk', 'Wv', 'W_comp', 'q_norm_w', 'k_norm_w', 'sink', 'Wg', 'Wo')}
    del _L1_attn_all

    def _L1_xattn_setup():
        import jax, jax.numpy as jnp
        import numpy as np
        N_HEADS = 16
        N_KV_HEADS = 8
        HEAD_DIM = 128
        D_TEXT = 256
        D_VISION = 128
        GROUPS = N_HEADS // N_KV_HEADS
        key = jax.random.key(seed)
        ks = jax.random.split(key, 6)
        B, T_text, T_vis = (4, 256, 72)
        text_hidden = jax.random.normal(ks[0], (B, T_text, D_TEXT), dtype=jnp.float32)
        vision_tokens = jax.random.normal(ks[1], (B, T_vis, D_VISION), dtype=jnp.float32)
        vision_mask = jnp.ones((B, T_vis), dtype=bool)
        s = 0.02
        Wq = jax.random.normal(ks[2], (D_TEXT, N_HEADS * HEAD_DIM), dtype=jnp.float32) * s
        Wk = jax.random.normal(ks[3], (D_VISION, N_KV_HEADS * HEAD_DIM), dtype=jnp.float32) * s
        Wv = jax.random.normal(ks[4], (D_VISION, N_KV_HEADS * HEAD_DIM), dtype=jnp.float32) * s
        Wo = jax.random.normal(ks[5], (N_HEADS * HEAD_DIM, D_TEXT), dtype=jnp.float32) * s
        return {'text_hidden': text_hidden, 'vision_tokens': vision_tokens, 'vision_mask': vision_mask, 'Wq': Wq, 'Wk': Wk, 'Wv': Wv, 'Wo': Wo}
    _L1_xattn_all = _L1_xattn_setup()
    _L1_xattn_in = {k: v for k, v in _L1_xattn_all.items() if k in ('Wq', 'Wk', 'Wv', 'Wo')}
    del _L1_xattn_all

    def _L1_ffn_setup():
        import jax, jax.numpy as jnp
        import numpy as np
        DIM = 256
        HID = 704
        ZERO_POINT = 128.0

        def _qlinear(x, wq, scale):
            W = (wq.astype(jnp.float32) - ZERO_POINT) * scale[:, None]
            return jnp.einsum('bsd,hd->bsh', x, W)
        key = jax.random.key(seed)
        ks = jax.random.split(key, 7)
        B, S = (4, 256)
        sg = jax.random.uniform(ks[1], (HID,)) * (0.02 / np.sqrt(DIM)) + 0.0001
        su = jax.random.uniform(ks[3], (HID,)) * (0.02 / np.sqrt(DIM)) + 0.0001
        sd = jax.random.uniform(ks[5], (DIM,)) * (0.02 / np.sqrt(HID)) + 0.0001
        return {'x': jax.random.normal(ks[0], (B, S, DIM), dtype=jnp.float32), 'wq_gate': jax.random.randint(ks[2], (HID, DIM), 0, 32, dtype=jnp.int32), 's_gate': sg, 'wq_up': jax.random.randint(ks[4], (HID, DIM), 0, 32, dtype=jnp.int32), 's_up': su, 'wq_down': jax.random.randint(ks[6], (DIM, HID), 0, 32, dtype=jnp.int32), 's_down': sd}
    _L1_ffn_all = _L1_ffn_setup()
    _L1_ffn_in = {k: v for k, v in _L1_ffn_all.items() if k in ('wq_gate', 's_gate', 'wq_up', 's_up', 'wq_down', 's_down')}
    del _L1_ffn_all
    return {'x': x, 'ctx_1024': ctx_1024, 'mask_BxS2_bf1': mask_BxS2_bf1, 'L0_attn_Wq': _L0_attn_in['Wq'], 'L0_attn_Wk': _L0_attn_in['Wk'], 'L0_attn_Wv': _L0_attn_in['Wv'], 'L0_attn_Wo': _L0_attn_in['Wo'], 'L0_xattn_Wq': _L0_xattn_in['Wq'], 'L0_xattn_Wk': _L0_xattn_in['Wk'], 'L0_xattn_Wv': _L0_xattn_in['Wv'], 'L0_xattn_Wo': _L0_xattn_in['Wo'], 'L0_xattn_gq': _L0_xattn_in['gq'], 'L0_xattn_gk': _L0_xattn_in['gk'], 'L0_ffn_w_gate': _L0_ffn_in['w_gate'], 'L0_ffn_w_up': _L0_ffn_in['w_up'], 'L0_ffn_w_down': _L0_ffn_in['w_down'], 'L0_ffn_s_gate': _L0_ffn_in['s_gate'], 'L0_ffn_s_up': _L0_ffn_in['s_up'], 'L0_ffn_s_down': _L0_ffn_in['s_down'], 'L1_attn_Wq_c': _L1_attn_in['Wq_c'], 'L1_attn_Wq_up': _L1_attn_in['Wq_up'], 'L1_attn_Wk': _L1_attn_in['Wk'], 'L1_attn_Wv': _L1_attn_in['Wv'], 'L1_attn_W_comp': _L1_attn_in['W_comp'], 'L1_attn_q_norm_w': _L1_attn_in['q_norm_w'], 'L1_attn_k_norm_w': _L1_attn_in['k_norm_w'], 'L1_attn_sink': _L1_attn_in['sink'], 'L1_attn_Wg': _L1_attn_in['Wg'], 'L1_attn_Wo': _L1_attn_in['Wo'], 'L1_xattn_Wq': _L1_xattn_in['Wq'], 'L1_xattn_Wk': _L1_xattn_in['Wk'], 'L1_xattn_Wv': _L1_xattn_in['Wv'], 'L1_xattn_Wo': _L1_xattn_in['Wo'], 'L1_ffn_wq_gate': _L1_ffn_in['wq_gate'], 'L1_ffn_s_gate': _L1_ffn_in['s_gate'], 'L1_ffn_wq_up': _L1_ffn_in['wq_up'], 'L1_ffn_s_up': _L1_ffn_in['s_up'], 'L1_ffn_wq_down': _L1_ffn_in['wq_down'], 'L1_ffn_s_down': _L1_ffn_in['s_down']}

def reference(x, ctx_1024, mask_BxS2_bf1, L0_attn_Wq, L0_attn_Wk, L0_attn_Wv, L0_attn_Wo, L0_xattn_Wq, L0_xattn_Wk, L0_xattn_Wv, L0_xattn_Wo, L0_xattn_gq, L0_xattn_gk, L0_ffn_w_gate, L0_ffn_w_up, L0_ffn_w_down, L0_ffn_s_gate, L0_ffn_s_up, L0_ffn_s_down, L1_attn_Wq_c, L1_attn_Wq_up, L1_attn_Wk, L1_attn_Wv, L1_attn_W_comp, L1_attn_q_norm_w, L1_attn_k_norm_w, L1_attn_sink, L1_attn_Wg, L1_attn_Wo, L1_xattn_Wq, L1_xattn_Wk, L1_xattn_Wv, L1_xattn_Wo, L1_ffn_wq_gate, L1_ffn_s_gate, L1_ffn_wq_up, L1_ffn_s_up, L1_ffn_wq_down, L1_ffn_s_down):
    import jax
    import jax.numpy as jnp

    def _L0_attn_ref(hidden_states, Wq, Wk, Wv, Wo):
        import jax, jax.numpy as jnp
        import numpy as np
        B, T, HID, H = (2, 256, 256, 16)
        D = HID // H

        def apply_rope(x):
            b, t, h, d = x.shape
            half = d // 2
            x1, x2 = (x[..., :half], x[..., half:])
            theta = 1.0 / 10000.0 ** (jnp.arange(0, half, 2, dtype=jnp.float32) / half)
            pos = jnp.arange(t, dtype=jnp.float32)
            freq = pos[:, None] * theta[None, :]
            sin = jnp.sin(freq)[None, :, None, :]
            cos = jnp.cos(freq)[None, :, None, :]
            x1e, x1o = (x1[..., ::2], x1[..., 1::2])
            x2e, x2o = (x2[..., ::2], x2[..., 1::2])
            x1r = jnp.concatenate([x1e * cos - x1o * sin, x1e * sin + x1o * cos], axis=-1)
            x2r = jnp.concatenate([x2e * cos - x2o * sin, x2e * sin + x2o * cos], axis=-1)
            return jnp.concatenate([x1r, x2r], axis=-1)
        b, t, _ = hidden_states.shape
        scaling = D ** (-0.5)
        q = (hidden_states @ Wq.T).reshape(b, t, H, D).transpose(0, 2, 1, 3)
        k = hidden_states @ Wk.T
        v = hidden_states @ Wv.T
        q = apply_rope(q)
        k = apply_rope(k[:, None])
        v = v[:, None]
        scores = jnp.einsum('bhqd,bokd->bhqk', q, k) * scaling
        causal = jnp.tril(jnp.ones((t, t), dtype=bool))
        scores = jnp.where(causal[None, None], scores, -jnp.inf)
        probs = jax.nn.softmax(scores, axis=-1)
        attn = jnp.einsum('bhqk,bokd->bhqd', probs, v)
        attn = attn.transpose(0, 2, 1, 3).reshape(b, t, HID)
        return attn @ Wo.T

    def _L0_xattn_ref(hidden_states, encoder_hidden_states, Wq, Wk, Wv, Wo, gq, gk):
        import jax, jax.numpy as jnp
        import numpy as np
        EPS = 1e-05

        def rmsnorm(x, g, eps=EPS):
            var = jnp.mean(jnp.square(x), axis=-1, keepdims=True)
            return x * jax.lax.rsqrt(var + eps) * g
        B, Sq, _ = hidden_states.shape
        Skv = encoder_hidden_states.shape[1]
        D = gq.shape[0]
        H = Wq.shape[1] // D
        scale = 1.0 / np.sqrt(D)
        q = (hidden_states @ Wq).reshape(B, Sq, H, D)
        k = (encoder_hidden_states @ Wk).reshape(B, Skv, H, D)
        v = (encoder_hidden_states @ Wv).reshape(B, Skv, H, D)
        q = rmsnorm(q, gq)
        k = rmsnorm(k, gk)
        scores = jnp.einsum('bqhd,bkhd->bhqk', q, k) * scale
        attn = jax.nn.softmax(scores, axis=-1)
        out = jnp.einsum('bhqk,bkhd->bqhd', attn, v)
        out = out.reshape(B, Sq, H * D)
        return out @ Wo

    def _L0_ffn_ref(x, w_gate, w_up, w_down, s_gate, s_up, s_down):
        import jax, jax.numpy as jnp
        import numpy as np
        HIDDEN = 256
        INTER = 1024
        B, S = (4, 128)

        def _qmatmul(x, w_int8, scale):
            y = jnp.einsum('bsh,ho->bso', x, w_int8.astype(x.dtype))
            return y * scale
        gate = jax.nn.silu(_qmatmul(x, w_gate, s_gate))
        up = _qmatmul(x, w_up, s_up)
        fuse = gate * up
        return _qmatmul(fuse, w_down, s_down)

    def _L1_attn_ref(h, Wq_c, Wq_up, Wk, Wv, W_comp, q_norm_w, k_norm_w, sink, Wg, Wo):
        import jax, jax.numpy as jnp
        import numpy as np
        H = 16
        D = 128
        M = 16
        ROPE = 64
        THETA = 10000.0
        WIN = 64
        CAP = 50.0
        G = 4
        HID = 256
        QC = 64
        INTER = 256

        def rope_cache(t):
            inv = 1.0 / THETA ** (jnp.arange(0, ROPE, 2, dtype=jnp.float32) / ROPE)
            ang = jnp.arange(t, dtype=jnp.float32)[:, None] * inv[None, :]
            return (jnp.cos(ang), jnp.sin(ang))

        def apply_partial_rope(x, cos, sin):
            x1 = x[..., :ROPE // 2]
            x2 = x[..., ROPE // 2:ROPE]
            rest = x[..., ROPE:]
            return jnp.concatenate([x1 * cos - x2 * sin, x1 * sin + x2 * cos, rest], axis=-1)

        def rmsnorm(x, w, eps=1e-06):
            return x * jax.lax.rsqrt(jnp.mean(x * x, axis=-1, keepdims=True) + eps) * w

        def attend(scores, mask, sink, v, sub):
            b, h, t, _ = scores.shape
            logits = jnp.where(mask, scores, jnp.float32(-1e+30))
            sink_col = jnp.broadcast_to(sink[None, :, None, None], (b, h, t, 1))
            probs = jax.nn.softmax(jnp.concatenate([logits, sink_col], axis=-1), axis=-1)[..., :-1]
            return jnp.einsum(sub, probs, v)
        b, t, _ = h.shape
        cos, sin = rope_cache(t)
        q = (h @ Wq_c @ Wq_up).reshape(b, t, H, D).transpose(0, 2, 1, 3)
        q = rmsnorm(apply_partial_rope(q, cos, sin), q_norm_w)
        k_sw = rmsnorm(apply_partial_rope(h @ Wk, cos, sin), k_norm_w)
        v_sw = h @ Wv
        nb = t // M
        ck = rmsnorm(h.reshape(b, nb, M * HID) @ W_comp, k_norm_w)
        scale = 1.0 / jnp.sqrt(jnp.float32(D))
        pos = jnp.arange(t)
        blk_end = jnp.arange(nb) * M + (M - 1)
        valid = blk_end[None, :] < pos[:, None]
        c_scores = jnp.einsum('bhtd,bnd->bhtn', q, ck) * scale
        c_out = attend(c_scores, valid[None, None], sink, ck, 'bhtn,bnd->bhtd')
        sw_scores = jnp.einsum('bhtd,bsd->bhts', q, k_sw) * scale
        sw_scores = CAP * jnp.tanh(sw_scores / CAP)
        sw_mask = (pos[None, :] <= pos[:, None]) & (pos[:, None] - pos[None, :] < WIN)
        sw_out = attend(sw_scores, sw_mask[None, None], sink, v_sw, 'bhts,bsd->bhtd')
        ao = (c_out + sw_out).transpose(0, 2, 1, 3).reshape(b, t, G, H // G * D)
        inter = jnp.einsum('btgf,gfi->btgi', ao, Wg)
        return inter.reshape(b, t, G * INTER) @ Wo

    def _L1_xattn_ref(text_hidden, vision_tokens, vision_mask, Wq, Wk, Wv, Wo):
        import jax, jax.numpy as jnp
        import numpy as np
        N_HEADS = 16
        N_KV_HEADS = 8
        HEAD_DIM = 128
        D_TEXT = 256
        D_VISION = 128
        GROUPS = N_HEADS // N_KV_HEADS
        B, T_text, _ = text_hidden.shape
        T_vis = vision_tokens.shape[1]
        scale = jnp.float32(np.sqrt(HEAD_DIM))
        q = (text_hidden @ Wq).reshape(B, T_text, N_HEADS, HEAD_DIM).transpose(0, 2, 1, 3)
        k = (vision_tokens @ Wk).reshape(B, T_vis, N_KV_HEADS, HEAD_DIM).transpose(0, 2, 1, 3)
        v = (vision_tokens @ Wv).reshape(B, T_vis, N_KV_HEADS, HEAD_DIM).transpose(0, 2, 1, 3)
        k = jnp.repeat(k, GROUPS, axis=1)
        v = jnp.repeat(v, GROUPS, axis=1)
        scores = jnp.einsum('bhtd,bhsd->bhts', q, k) / scale
        mask = vision_mask[:, None, None, :]
        scores = jnp.where(mask, scores, -jnp.inf)
        attn = jax.nn.softmax(scores, axis=-1)
        attn = jnp.nan_to_num(attn, nan=0.0)
        out = jnp.einsum('bhts,bhsd->bhtd', attn, v)
        out = out.transpose(0, 2, 1, 3).reshape(B, T_text, N_HEADS * HEAD_DIM)
        return out @ Wo

    def _L1_ffn_ref(x, wq_gate, s_gate, wq_up, s_up, wq_down, s_down):
        import jax, jax.numpy as jnp
        import numpy as np
        DIM = 256
        HID = 704
        ZERO_POINT = 128.0

        def _qlinear(x, wq, scale):
            W = (wq.astype(jnp.float32) - ZERO_POINT) * scale[:, None]
            return jnp.einsum('bsd,hd->bsh', x, W)
        gate = _qlinear(x, wq_gate, s_gate)
        gate = jax.nn.silu(gate)
        up = _qlinear(x, wq_up, s_up)
        return _qlinear(gate * up, wq_down, s_down)
    x = _layernorm(x + _L0_attn_ref(x, L0_attn_Wq, L0_attn_Wk, L0_attn_Wv, L0_attn_Wo), axis=-1)
    x = _layernorm(x + _L0_xattn_ref(x, ctx_1024, L0_xattn_Wq, L0_xattn_Wk, L0_xattn_Wv, L0_xattn_Wo, L0_xattn_gq, L0_xattn_gk), axis=-1)
    x = _layernorm(x + _L0_ffn_ref(x, L0_ffn_w_gate, L0_ffn_w_up, L0_ffn_w_down, L0_ffn_s_gate, L0_ffn_s_up, L0_ffn_s_down), axis=-1)
    x = _layernorm(x + _L1_attn_ref(x, L1_attn_Wq_c, L1_attn_Wq_up, L1_attn_Wk, L1_attn_Wv, L1_attn_W_comp, L1_attn_q_norm_w, L1_attn_k_norm_w, L1_attn_sink, L1_attn_Wg, L1_attn_Wo), axis=-1)
    x = _layernorm(x + _L1_xattn_ref(x, ctx_1024, mask_BxS2_bf1, L1_xattn_Wq, L1_xattn_Wk, L1_xattn_Wv, L1_xattn_Wo), axis=-1)
    x = _layernorm(x + _L1_ffn_ref(x, L1_ffn_wq_gate, L1_ffn_s_gate, L1_ffn_wq_up, L1_ffn_s_up, L1_ffn_wq_down, L1_ffn_s_down), axis=-1)
    return x

_drawn_inputs = setup_inputs


def setup_inputs(seed=0):
    import zlib

    import numpy as np

    out = dict(_drawn_inputs(seed))
    spreads = {'L0_xattn_gq': (1.0, 0.2),
     'L0_xattn_gk': (1.0, 0.2),
     'L1_attn_q_norm_w': (1.0, 0.6),
     'L1_attn_k_norm_w': (1.0, 0.2),
     'L1_attn_sink': (0.0, 0.8)}
    factors = {'L0_attn_Wq': 8.0,
     'L0_attn_Wk': 8.0,
     'L1_xattn_Wq': 8.0,
     'L1_xattn_Wk': 8.0,
     'L1_ffn_s_gate': 8.0,
     'L1_ffn_s_up': 8.0,
     'L1_ffn_s_down': 8.0}
    for name, (base, spread) in spreads.items():
        noise = np.random.default_rng([zlib.crc32(name.encode()), seed]).standard_normal(out[name].shape)
        drawn = base * np.exp(spread * noise) if base else spread * noise
        out[name] = jnp.asarray(drawn.astype(out[name].dtype))
    for name, factor in factors.items():
        out[name] = (out[name] * factor).astype(out[name].dtype)
    return out
```

```python
from contextlib import ExitStack

import concourse.bass as bass
from concourse import mybir

F32 = mybir.dt.float32
BF16 = mybir.dt.bfloat16
I32 = mybir.dt.int32
I8 = mybir.dt.int8
U8 = mybir.dt.uint8
ALU = mybir.AluOpType
ACT = mybir.ActivationFunctionType
AX = mybir.AxisListType

P = 128
B, T, D = 32, 64, 256
NT = B * T // P
NC = 4
CT = NT // NC
CN = CT * P
CB = CN // T
KD = D // P
H = 16
HD = 128
NU = H // 2
NB = 4
W1 = T + NB
NEG = -1e30
LN_EPS = 1e-5
FF0 = 1024 // P
FF1_SIZES = [128] * 5 + [64]
FF1N = 704


class Order:

    def __init__(self, eng, sem):
        self.eng, self.sem, self.base, self.n, self.it, self.per = eng, sem, 0, 0, None, 0

    def enter(self, it, per):
        self.it, self.per, self.n = it, per, 0

    def leave(self, trips):
        assert self.n == self.per, (self.n, self.per)
        self.base += trips * self.per
        self.it, self.n = None, 0

    def then(self, ins):
        ins.then_inc(self.sem, 1)
        if self.it is None:
            self.base += 1
            self.eng.wait_ge(self.sem, self.base)
        else:
            self.n += 1
            self.eng.wait_ge(self.sem, self.it * self.per + (self.base + self.n))


def build(nc, a, out):
    ctx = ExitStack()
    with ctx:
        def sb(name, shape, dt=F32):
            return ctx.enter_context(nc.sbuf_tensor(name, shape, dt))

        def sem(name):
            return ctx.enter_context(nc.semaphore(name))

        X = sb("X", [P, NT, D])
        Xc = sb("Xc", [P, CT, D])
        XT = sb("XT", [P, KD, CN])
        ctxT = sb("ctxT", [P, CN])
        ctxN = sb("ctxN", [P, 4, P])
        R1 = sb("R1", [P, 12032])
        R2 = sb("R2", [P, 8224])
        WL = sb("WL", [P, 8192])
        WU = sb("WU", [P, 8192])
        Eflat = sb("E", [P, 2 * 2 * CT * W1])
        PT = sb("PT", [P, 2 * CN])
        OT = sb("OT", [P, 2, 2 * CN])
        Y = sb("Y", [P, CT, D])
        ident = sb("ident", [P, P])
        identb = sb("identb", [P, P], BF16)
        causal = sb("causal", [P, T])
        causalb = sb("causalb", [P, 8, T], BF16)
        keep = sb("keep", [P, T])
        blockmask = sb("blockmask", [P, NB])
        rot0 = sb("rot0", [P, 2, D])
        cos1 = sb("cos1", [64, T])
        sin1 = sb("sin1", [64, T])
        headmask = sb("headmask", [P, 8])
        ones = sb("ones", [P, P])
        onehot = sb("onehot", [P, H, H])
        vmaskb = sb("vmaskb", [P, NT, T], BF16)
        anykey = sb("anykey", [P, NT])
        cols = sb("cols", [P, 40])
        rowsB = sb("rowsB", [P, 2, D])
        kwB = sb("kwB", [32, HD])
        sinkB = sb("sinkB", [P, H])
        sinkneg = sb("sinkneg", [P, H])
        sinkexp = sb("sinkexp", [P, H])
        rrow = sb("rrow", [H, CN])
        rq = sb("rq", [P, CT, H])
        mx = sb("mx", [P, 8])
        sm = sb("sm", [P, 8])
        rs = sb("rs", [P, 8])
        cb = sb("cb", [P, 2, CT, NB + 1])
        bst = sb("bst", [P, CT, 6])
        mv = sb("mv", [P, CT, 2])
        std = sb("std", [P, CT])
        rstd = sb("rstd", [P, CT])
        ckv = sb("ckv", [32, HD])
        ckt = sb("ckt", [32, HD])
        cks = sb("cks", [32, 4])
        eps5, eps6, eps6b = sb("eps5", [P, 1]), sb("eps6", [P, 1]), sb("eps6b", [P, 1])
        ps = ctx.enter_context(nc.psum_tensor("ps", [P, 8, CN], F32))

        gq_c, gk_c, gqk_c = cols[:, 0:1], cols[:, 1:2], cols[:, 2:3]
        qw_c, kw_c, qkw_c = cols[:, 3:4], cols[:, 4:5], cols[:, 5:6]
        sg0, su0 = cols[:, 6:14], cols[:, 14:22]
        sg1, su1 = cols[:, 22:28], cols[:, 28:34]

        def view(region, at, *shape):
            n = 1
            for s in shape:
                n *= s
            v = region[:, at:at + n]
            if len(shape) == 2:
                v = v.rearrange("p (a b) -> p a b", b=shape[1])
            if len(shape) == 3:
                v = v.rearrange("p (a b c) -> p a b c", b=shape[1], c=shape[2])
            return v

        xq_w = view(R1, 0, KD, H * HD)
        xk_w = view(R1, 4096, H * HD)
        xvo_w = view(R1, 6144, H, D)
        cq_w = view(R1, 0, KD, 64)
        up_w = view(R1, 128, H, HD)
        k1_w = view(R1, 3200, KD, HD)
        v1_w = view(R1, 3584, KD, HD)
        comp_w = view(R1, 3840, 16 * KD, HD)
        go_w = view(R1, 7936, H, D)
        f1g_w = view(R1, 0, KD, FF1N)
        f1u_w = view(R1, 1408, KD, FF1N)
        f1d_w = view(R1, 2816, 6, D)
        a0q_w = view(R2, 0, 2 * KD, D)
        a0k_w = view(R2, 1024, KD, P)
        a0v_w = view(R2, 1536, KD, 16)
        a0o_w = view(R2, 1568, KD, D)
        f0g_w = view(R2, 2080, KD, 1024)
        f0u_w = view(R2, 4128, KD, 1024)
        f0d_w = view(R2, 6176, FF0, D)
        x1a_w = view(R2, 0, H * KD, HD)
        x1vo_w = view(R2, 4096, H, D)
        x0_vT, x0_o = view(WU, 0, H, P), view(WU, 2048, H, D)
        g_wgT, g_wo = view(WU, 0, 8, CN), view(WU, 4096, 8, D)
        x1_qT, x1_kT = view(WU, 0, H, D), view(WL, 4352, 8, P)
        x1_vT, x1_o = view(WL, 5376, 8, P), view(WU, 4096, H, D)
        raw0 = view(WU, 6144, 1536).bitcast(I32)
        vmask8 = view(WU, 7680, 256).bitcast(U8).rearrange("p (t k) -> p t k", k=T)
        raw1 = view(WL, 0, 4352).bitcast(I32)
        q0T = view(WL, 0, 2, CN)
        k0T = view(WL, 1024, CN)
        v0bd = view(WL, 2560, CB, 32)
        kbd = view(WL, 3840, CB, 8 * T)
        qT = view(WL, 0, H, CN)
        kT = view(WU, 0, H, CN)
        krms, krs = PT[:, 0:CN], PT[:, CN:2 * CN]
        SQ, KSQ = (OT[:, j, :].rearrange("p (s m) -> p s m", s=2) for j in range(2))
        qcT = view(WU, 0, CN)
        keysT = view(WU, 512, CB, W1)
        E = Eflat[:].rearrange("p (r h t k) -> p r h t k", r=2, h=2, t=CT)
        E64 = Eflat[:, 0:4 * CT * T].rearrange("p (r h t k) -> p r h t k", r=2, h=2, t=CT)
        vals = view(WU, 1056, CB, HD)
        l1t1, l1t2, l1k = (view(WU, 2080 + CN * j, CN) for j in range(3))
        q1T = view(WU, 0, 2, 2 * CN)
        e0 = view(WL, 2816, 2, CN)
        SQr = [l1t1, l1t2]
        silu_b = view(WL, 0, 2, CN)
        hidT = view(WL, 1024, 2, CN)

        d_x, d_const, d_a0, d_x0, d_x0o, d_f0 = (sem(n) for n in ("d_x", "d_const", "d_a0", "d_x0", "d_x0o", "d_f0"))
        d_l1, d_l1o, d_x1o, d_f1, d_ctx, d_ck, d_out = (
            sem(n) for n in ("d_l1", "d_l1o", "d_x1o", "d_f1", "d_ctx", "d_ck", "d_out"))
        v_own, a_own, g_own = sem("v_own"), sem("a_own"), sem("g_own")
        const_v, const_g, const_a = sem("const_v"), sem("const_g"), sem("const_a")
        xc_ready, xt_psum, xt_ready = (sem(n) for n in ("xc_ready", "xt_psum", "xt_ready"))
        y_done, y_read, ln_var, ln_log, ln_std, ln_done = (sem(n) for n in ("y_done", "y_read", "ln_var", "ln_log", "ln_std", "ln_done"))
        fuse_mm, fuse_cp = sem("fuse_mm"), sem("fuse_cp")
        f0_cvt, f1_cvt = sem("f0_cvt"), sem("f1_cvt")

        class Unit:

            def __init__(s, n):
                s.q_mm, s.q_ready, s.s_done, s.s_free, s.sub, s.tanh, s.exp, s.cexp = (
                    sem(f"{n}_{w}") for w in ("q_mm", "q_ready", "s_done", "s_free", "sub", "tanh", "exp", "cexp"))
                s.p_ready, s.t_done, s.pt_ready, s.v_done, s.ot_ready, s.o_done = (
                    sem(f"{n}_{w}") for w in ("p_ready", "t_done", "pt_ready", "v_done", "ot_ready", "o_done"))
                s.ot_ready2 = sem(f"{n}_ot_ready2")

        U0, U1, U3, U4 = Unit("sa0"), Unit("xa0"), Unit("sa1"), Unit("xa1")
        a0_w, a0_mm, a0_q, a0_k, a0_v, a0_vbd, a0_kbd = (
            sem(f"a0_{w}") for w in ("w", "mm", "q", "k", "v", "vbd", "kbd"))
        x_qmm, x_kmm, x_qsq, x_qcp, x_ksq, x_ksum, x_kln, x_krs, x_krdy, x_qsum = (
            sem(f"x_{w}") for w in ("qmm", "kmm", "qsq", "qcp", "ksq", "ksum", "kln", "krs", "krdy", "qsum"))
        r_ln, r_row, r_T, r_rq = (sem(f"r_{w}") for w in ("ln", "row", "T", "rq"))
        (l_qcmm, l_qc, l_kmm, l_vmm, l_ckmm, l_ksq, l_ksum, l_kln, l_krs, l_keys, l_v, l_ckss, l_ckln, l_ckrs, l_ckv,
         l_ckT, l_qmm, l_qsq, l_qrest, l_qhalf, l_qrdy, l_qsum) = (
            sem(f"l_{w}") for w in ("qcmm", "qc", "kmm", "vmm", "ckmm", "ksq", "ksum", "kln", "krs", "keys", "v",
                                    "ckss", "ckln", "ckrs", "ckv", "ckT", "qmm", "qsq", "qrest", "qhalf", "qrdy",
                                    "qsum"))
        f_mm = [sem("f0_mm"), sem("f1_mm")]
        f_silu = [sem("f0_silu"), sem("f1_silu")]
        f_hid = [sem("f0_hid"), sem("f1_hid")]
        f_down = [sem("f0_down"), sem("f1_down")]

        def bank(i, n=CN):
            return ps[:, i, 0:n]

        def two(i):
            return ps[:, i:i + 2, :]

        Yp = ps[:, 6:8, :].rearrange("p a (b n) -> p (a b) n", n=D)

        block = ctx.enter_context(nc.Block())

        @block.sync
        def _(sp):
            def load(dst, src, s):
                sp.dma_start(dst, src).then_inc(s, 16)

            load(X[:, 0:CT, :], a["x"][0:CT].rearrange("t p d -> p t d"), d_x)
            load(ident[:], a["c_ident"], d_const)
            load(a0q_w, a["a0_q"].rearrange("(f p) n -> p f n", p=P), d_a0)
            load(a0k_w, a["a0_k"].rearrange("(f p) n -> p f n", p=P), d_a0)
            load(rot0[:, 0, :], a["c_cos0"].partition_broadcast(P), d_a0)
            load(rot0[:, 1, :], a["c_sin0"].partition_broadcast(P), d_a0)
            load(a0v_w, a["a0_v"].rearrange("(f p) n -> p f n", p=P), d_a0)
            load(a0o_w, a["a0_o"].rearrange("(f p) n -> p f n", p=P), d_a0)
            for dst, name in ((causal[:], "c_causal"), (keep[:], "c_keep"), (blockmask[:], "c_blockmask"),
                              (cos1[:], "c_cos1"), (sin1[:], "c_sin1"),
                              (headmask[:], "c_headmask")):
                load(dst, a[name], d_const)
            load(X[:, CT:NT, :], a["x"][CT:NT].rearrange("t p d -> p t d"), d_x)
            for i, name in enumerate(("gq", "gk", None, "qw", "kw")):
                if name:
                    load(cols[:, i:i + 1], a[name], d_const)
            load(sg0, a["f0_sg"], d_const)
            load(su0, a["f0_su"], d_const)
            for dst, name in ((sg1, "f1_sg"), (su1, "f1_su")):
                load(dst[:, 0:5], a[name], d_const)
                load(dst[0:64, 5:6], a[name + "_tail"], d_const)
            load(rowsB[:, 0, :], a["f0_sd"].partition_broadcast(P), d_const)
            load(rowsB[:, 1, :], a["f1_sd"].partition_broadcast(P), d_const)
            load(onehot[:].rearrange("p h g -> p (h g)"), a["c_onehot"].partition_broadcast(P), d_const)
            load(kwB[:], a["kw_row"].partition_broadcast(32), d_const)
            load(sinkB[:], a["sink"].partition_broadcast(P), d_const)
            mk = a["mask"].rearrange("(t two) k -> two t k", two=2)
            for j in range(2):
                load(vmask8[64 * j:64 * j + 64, :, :], mk[j].partition_broadcast(64), d_const)
            load(raw0[:, 0:512].rearrange("p (k n) -> p k n", n=256), a["f0_g"].rearrange("(k p) n -> p k n", p=P), d_f0)
            load(raw0[:, 512:1024].rearrange("p (k n) -> p k n", n=256), a["f0_u"].rearrange("(k p) n -> p k n", p=P), d_f0)
            load(raw0[:, 1024:1536].rearrange("p (j n) -> p j n", n=64), a["f0_d"].rearrange("(j p) n -> p j n", p=P), d_f0)
            load(x0_vT, a["x0_vT"].rearrange("(h p) c -> p h c", p=P), d_x0o)
            load(x0_o, a["x0_o"].rearrange("(h p) n -> p h n", p=P), d_x0o)
            load(xq_w, a["x0_q"].rearrange("(k p) n -> p k n", p=P), d_x0)
            load(xk_w, a["x0_k"], d_x0)

            def load_ctx(c):
                sp.dma_start(ctxT[:], a["ctxT"][:, bass.ts(c, CN)]).then_inc(d_ctx, 16)
                sp.dma_start(ctxN[:], a["ctx"][bass.ds(c, 1)].rearrange("a p (g n) -> p (a g) n", n=P)).then_inc(d_ctx, 16)

            load_ctx(0)
            with sp.Fori(1, NC) as c:
                sp.wait_ge(y_done, c + NC)
                load_ctx(c)
            sp.wait_ge(y_done, 2 * NC)
            load(cq_w, a["l1_qc"].rearrange("(k p) n -> p k n", p=P), d_l1)
            load(up_w[0:64], a["l1_up"].rearrange("p (h n) -> p h n", n=HD), d_l1)
            load(k1_w, a["l1_k"].rearrange("(k p) n -> p k n", p=P), d_l1)
            load(v1_w, a["l1_v"].rearrange("(k p) n -> p k n", p=P), d_l1)
            load(comp_w, a["l1_comp"].rearrange("(m p) n -> p m n", p=P), d_l1)
            load(g_wgT, a["l1_gT"].rearrange("(m p) n -> p m n", p=P), d_l1o)
            load(g_wo, a["l1_o"].rearrange("(m p) n -> p m n", p=P), d_l1o)
            with sp.Fori(0, NC) as c:
                sp.wait_ge(l_ckv, c + 1)
                for b in range(CB):
                    sp.dma_start(vals[T:W1, b, :], ckv[NB * b:NB * b + NB, :]).then_inc(d_ck, 16)
            sp.wait_ge(y_done, 4 * NC)
            load(x1_qT, a["x1_qT"].rearrange("(h p) n -> p h n", p=P), d_x1o)
            load(x1_kT, a["x1_kT"].rearrange("(h p) n -> p h n", p=P), d_x1o)
            load(x1_vT, a["x1_vT"].rearrange("(h p) n -> p h n", p=P), d_x1o)
            load(x1_o, a["x1_o"].rearrange("(h p) n -> p h n", p=P), d_x1o)
            load(raw1[:, 0:1408].rearrange("p (k n) -> p k n", n=FF1N), a["f1_g"].rearrange("(k p) n -> p k n", p=P), d_f1)
            load(raw1[:, 1408:2816].rearrange("p (k n) -> p k n", n=FF1N), a["f1_u"].rearrange("(k p) n -> p k n", p=P), d_f1)
            load(raw1[:, 2816:4096].rearrange("p (j n) -> p j n", n=D),
                 a["f1_d"][0:640].rearrange("(j p) n -> p j n", p=P), d_f1)
            load(raw1[0:64, 4096:4352], a["f1_d"][640:704], d_f1)
            load_ctx(0)
            with sp.Fori(1, NC) as c:
                sp.wait_ge(y_done, c + 4 * NC)
                load_ctx(c)
            with sp.Fori(0, NC) as c:
                sp.wait_ge(ln_done, c + 5 * NC + 1)
                sp.dma_start(out[bass.ts(c, CT)].rearrange("t p d -> p t d"), X[:, bass.ts(c, CT), :]).then_inc(d_out, 16)
            sp.wait_ge(d_out, 16 * NC)

        N_CONST = 16 * (1 + 1 + 6 + 4 + 2 + 4 + 2 + 1 + 1 + 2)

        @block.gpsimd
        def _(g):
            order = Order(g, g_own)

            def fetch(L, c):
                if L == 0:
                    g.wait_ge(d_x, 32)
                else:
                    g.wait_ge(ln_done, c + (L - 1) * NC + 1)
                g.wait_ge(xt_psum, c + L * NC + 1)
                g.tensor_copy(Xc[:], X[:, bass.ts(c, CT), :]).then_inc(xc_ready, 1)

            g.memset(ones[:], 1.0).then_inc(const_g, 1)
            g.memset(v0bd, 0.0).then_inc(const_g, 1)
            g.wait_ge(const_g, 2)
            g.sem_inc(xt_psum, 1)
            with g.Fori(0, NC) as c:
                fetch(0, c)
                g.wait_ge(a0_k, c + 1)
                g.wait_ge(d_const, N_CONST)
                for b in range(CB):
                    g.tensor_tensor(kbd[:, b, :].rearrange("p (h k) -> p h k", k=T),
                                    k0T[:, b * T:(b + 1) * T].unsqueeze(1).broadcast_to([P, 8, T]),
                                    headmask[:].unsqueeze(2).broadcast_to([P, 8, T]), ALU.mult).then_inc(a0_kbd, 1)
            g.wait_ge(d_f0, 48)
            g.tensor_copy(R2[:, 2080:8224], raw0.bitcast(I8)).then_inc(f0_cvt, 1)
            with g.Fori(0, NC) as c:
                fetch(1, c)
            with g.Fori(0, NC) as c:
                fetch(2, c)
            with g.Fori(0, NC) as c:
                fetch(3, c)
                for h in range(H):
                    g.wait_ge(l_qhalf, c * H + h + 1)
                    g.tensor_tensor(qT[0:64, h, :], qT[0:64, h, :], SQr[h % 2][0:64, :], ALU.add).then_inc(l_qrdy, 1)
            g.wait_ge(y_done, 4 * NC)
            g.wait_ge(d_f1, 64)
            g.tensor_scalar(R1[:, 0:4096], raw1[:, 0:4096], -128.0, None, ALU.add).then_inc(f1_cvt, 1)
            g.tensor_scalar(R1[0:64, 4096:4352], raw1[0:64, 4096:4352], -128.0, None, ALU.add).then_inc(f1_cvt, 1)
            with g.Fori(0, NC) as c:
                fetch(4, c)
            with g.Fori(0, NC) as c:
                fetch(5, c)

        @block.tensor
        def _(pe):
            mm = pe.matmul

            def transposes(L, c):
                pe.wait_ge(xc_ready, c + L * NC + 1)
                for k in range(KD):
                    for t in range(CT):
                        last = pe.transpose(ps[:, k, t * P:(t + 1) * P], Xc[:, t, k * P:(k + 1) * P], ident[:])
                last.then_inc(xt_psum, 1)
                pe.wait_ge(xt_ready, c + L * NC + 1)

            def score(U, u, n, lhs, rhs, w, mask=None):
                if u >= 1:
                    pe.wait_ge(U.s_free, n)
                for h in range(2):
                    if mask is not None:
                        mm(ps[:, 2 + h, 0:CT * T], identb[:], mask, start=True, stop=False, skip_group_check=True)
                    for b in range(CB):
                        r, t = 64 * (b % 2), b // 2
                        last = mm(ps[r:r + 64, 2 + h, t * w:(t + 1) * w], lhs(h, b), rhs(h, b),
                                  start=mask is None, stop=True, skip_group_check=True)
                last.then_inc(U.s_done, 1)

            def turn(U, u, n, w):
                pe.wait_ge(U.p_ready, n + 1)
                if u >= 1:
                    pe.wait_ge(U.ot_ready, n)
                    pe.wait_ge(U.ot_ready2, n)
                mm(ps[:, 4, 0:1], identb[:], identb[:, 0:1], start=True, stop=True)
                for h in range(2):
                    if w == T:
                        for g in range(2):
                            last = pe.transpose(ps[:, 4 + h, g * P:(g + 1) * P], E64[:, u % 2, h, 2 * g:2 * g + 2, :].rearrange("p t k -> p (t k)"), ident[:])
                    else:
                        for t in range(CT):
                            last = pe.transpose(ps[0:w, 4 + h, t * P:(t + 1) * P], E[:, u % 2, h, t, 0:w], ident[:])
                last.then_inc(U.t_done, 1)

            def weigh(U, u, n, w, values=None):
                pe.wait_ge(U.pt_ready, n + 1)
                for b in range(CB):
                    t, j = b // 2, b % 2
                    o = ps[:, 4 + t % 2, :].rearrange("p (h m) -> p h m", h=2)[:, :, (t // 2 * 2 + j) * T:(t // 2 * 2 + j + 1) * T]
                    if w == T:
                        r = T * (t % 2)
                        pr = PT[r:r + T, 0:CN].rearrange("p (h m) -> p h m", h=2)[:, :, t // 2 * P + j * T:t // 2 * P + (j + 1) * T]
                        val = ctxN[r:r + T, t // 2 * 2 + j, :]
                    else:
                        pr = PT[0:w, :].rearrange("p (h m) -> p h m", h=2)[:, :, b * T:(b + 1) * T]
                        val = values(b)
                    last = mm(o, val, pr, start=True, stop=True, skip_group_check=True)
                last.then_inc(U.v_done, 1)

            def q_rms(n, k):
                pe.wait_ge(r_row, n + k * NC + 1)
                mm(ps[:, 4, 0:1], identb[:], identb[:, 0:1], start=True, stop=True)
                for t in range(CT):
                    last = pe.transpose(ps[:, 4, t * H:(t + 1) * H], rrow[:, t * P:(t + 1) * P], ident[0:H, 0:H])
                last.then_inc(r_T, 1)
                pe.wait_ge(r_rq, n + k * NC + 1)

            def project(U, L, c, u, n, wo):
                pe.wait_ge(U.ot_ready, n + 1)
                pe.wait_ge(U.ot_ready2, n + 1)
                if u == 0:
                    pe.wait_ge(y_read, c + L * NC + 1)
                for h in range(2):
                    for t in range(CT):
                        last = mm(Yp[:, t, :], OT[:, u % 2, h * CN + t * P:h * CN + (t + 1) * P], wo(2 * u + h),
                                  start=(u == 0 and h == 0 and t % 2 == 0), stop=(u == NU - 1 and h == 1),
                                  skip_group_check=True)
                last.then_inc(y_done if u == NU - 1 else U.o_done, 1)

            pe.wait_ge(const_v, 1)
            pe.wait_ge(const_g, 2)
            pe.wait_ge(d_const, N_CONST)
            pe.wait_ge(d_a0, 96)
            pe.wait_ge(a0_w, 1)
            with pe.Fori(0, NC) as c:
                transposes(0, c)
                for i in range(3):
                    for k in range(KD):
                        w = a0q_w[:, k, i * P:(i + 1) * P] if i < 2 else a0k_w[:, k, :]
                        last = mm(bank((2, 0, 1)[i]), w, XT[:, k, :], start=k == 0, stop=k == 1)
                    last.then_inc(a0_mm, 1)
                for b in range(CB):
                    for j in range(2):
                        for k in range(KD):
                            last = mm(ps[64 * j:64 * j + 64, 4, b * 32 + 16 * j:b * 32 + 16 * j + 16],
                                      XT[:, k, b * T:(b + 1) * T], a0v_w[:, k, :], start=k == 0, stop=k == 1,
                                      skip_group_check=True)
                last.then_inc(a0_v, 1)

                def score0(u, n):
                    t, hf = u // 2, u % 2
                    if u == 0:
                        pe.wait_ge(a0_q, c * 2 + 2)
                        pe.wait_ge(a0_kbd, c * CB + CB)
                    if u >= 1:
                        pe.wait_ge(U0.sub, n)
                    mm(bank(2), identb[:], causalb[:].rearrange("p h k -> p (h k)"), start=True, stop=False,
                       skip_group_check=True)
                    for j in range(2):
                        last = mm(ps[64 * j:64 * j + 64, 2, :], q0T[:, hf, t * P + 64 * j:t * P + 64 * j + 64],
                                  kbd[:, 2 * t + j, :], start=False, stop=True, skip_group_check=True)
                    last.then_inc(U0.s_done, 1)

                def turn0(u, n):
                    pe.wait_ge(U0.p_ready, n + 1)
                    if u >= 1:
                        pe.wait_ge(U0.ot_ready, n)
                    for m in range(4):
                        last = pe.transpose(ps[:, 4, m * P:(m + 1) * P], e0[:, u % 2, m * P:(m + 1) * P], ident[:])
                    last.then_inc(U0.t_done, 1)

                def weigh0(u, n):
                    pe.wait_ge(U0.pt_ready, n + 1)
                    if u == 0:
                        pe.wait_ge(a0_vbd, c + 1)
                    for m in range(4):
                        for j in range(2):
                            last = mm(ps[32 * m:32 * m + 32, 5, j * T:(j + 1) * T], v0bd[:, 2 * (u // 2) + j, :],
                                      PT[:, m * P + j * T:m * P + (j + 1) * T], start=True, stop=True,
                                      skip_group_check=True)
                    last.then_inc(U0.v_done, 1)

                def project0(u, n):
                    t, hf = u // 2, u % 2
                    pe.wait_ge(U0.ot_ready, n + 1)
                    if u == 0:
                        pe.wait_ge(y_read, c + 1)
                    last = mm(Yp[:, t, :], OT[:, u % 2, 0:P], a0o_w[:, hf, :], start=(hf == 0 and t % 2 == 0),
                              stop=hf == 1, skip_group_check=True)
                    last.then_inc(y_done if u == NU - 1 else U0.o_done, 1)

                for u in range(NU + 2):
                    n = c * NU + u
                    if u < NU:
                        score0(u, n)
                    if u == 0:
                        pe.wait_ge(a0_vbd, c + 1)
                    if 1 <= u <= NU:
                        turn0(u - 1, n - 1)
                        weigh0(u - 1, n - 1)
                    if u >= 2:
                        project0(u - 2, n - 2)

            pe.wait_ge(d_x0o, 32)
            for h in range(H):
                if h >= 2:
                    pe.wait_ge(fuse_cp, h - 1)
                mm(bank(h % 2, D), x0_vT[:, h, :], x0_o[:, h, :], start=True, stop=True).then_inc(fuse_mm, 1)
            pe.wait_ge(fuse_cp, H)
            pe.wait_ge(d_x0, 32)
            with pe.Fori(0, NC) as c:
                transposes(1, c)
                pe.wait_ge(d_ctx, c * 32 + 32)

                def sums(h):
                    pe.wait_ge(x_qsq, c * H + h + 1)
                    mm(ps[0:H, 4, :], onehot[:, h, :], SQ[:, h % 2, :], start=h == 0, stop=h == H - 1,
                       skip_group_check=True).then_inc(x_qsum, 1)
                    pe.wait_ge(x_ksq, c * H + h + 1)
                    if h >= 1:
                        pe.wait_ge(x_kln, c * H + h)
                    mm(bank(5), ones[:], KSQ[:, h % 2, :], start=True, stop=True).then_inc(x_ksum, 1)

                for h in range(H + 1):
                    if h < H:
                        if h >= 2:
                            pe.wait_ge(x_qcp, c * H + h - 1)
                            pe.wait_ge(x_qsq, c * H + h - 1)
                        for k in range(KD):
                            last = mm(bank(h % 2), xq_w[:, k, h * HD:(h + 1) * HD], XT[:, k, :], start=k == 0, stop=k == 1)
                        last.then_inc(x_qmm, 1)
                        if h >= 2:
                            pe.wait_ge(x_krdy, c * H + h - 1)
                        mm(bank(2 + h % 2), xk_w[:, h * HD:(h + 1) * HD], ctxT[:], start=True, stop=True).then_inc(x_kmm, 1)
                    if h >= 1:
                        sums(h - 1)
                pe.wait_ge(x_krdy, c * H + H)
                pe.wait_ge(x_qcp, c * H + H)
                q_rms(c, 0)
                for u in range(NU + 2):
                    n = c * NU + u
                    if u < NU:
                        score(U1, u, n, lambda h, b: qT[:, 2 * u + h, b * T:(b + 1) * T],
                              lambda h, b: kT[:, 2 * u + h, b * T:(b + 1) * T], T)
                    if 1 <= u <= NU:
                        turn(U1, u - 1, n - 1, T)
                    if u >= 2:
                        project(U1, 1, c, u - 2, n - 2, lambda h: xvo_w[:, h, :])
                    if 1 <= u <= NU:
                        weigh(U1, u - 1, n - 1, T)

            def ffn(i, L, sizes, wg, wu, wd):
                with pe.Fori(0, NC) as c:
                    transposes(L, c)
                    nj = len(sizes)
                    for j in range(nj + 1):
                        if j < nj:
                            m = sizes[j]
                            if j >= 2:
                                pe.wait_ge(f_hid[i], c * nj + j - 1)
                            for s, w in ((0, wg), (2, wu)):
                                for k in range(KD):
                                    last = mm(ps[0:m, s + j % 2, :], w[:, k, j * P:j * P + m], XT[:, k, :],
                                              start=k == 0, stop=k == 1)
                            last.then_inc(f_mm[i], 1)
                        if j >= 1:
                            m = sizes[j - 1]
                            pe.wait_ge(f_hid[i], c * nj + j)
                            if j == 1:
                                pe.wait_ge(y_read, c + L * NC + 1)
                            for t in range(CT):
                                last = mm(Yp[:, t, :], hidT[0:m, (j - 1) % 2, t * P:(t + 1) * P], wd[0:m, j - 1, :],
                                          start=(j == 1 and t % 2 == 0), stop=j == nj, skip_group_check=True)
                            last.then_inc(y_done if j == nj else f_down[i], 1)

            pe.wait_ge(f0_cvt, 1)
            ffn(0, 2, [P] * FF0, f0g_w, f0u_w, f0d_w)

            pe.wait_ge(d_l1o, 32)
            for h in range(H):
                if h >= 2:
                    pe.wait_ge(fuse_cp, H + h - 1)
                for k in range(KD):
                    last = mm(bank(h % 2, D), g_wgT[:, 2 * (h // 4) + k, (h % 4) * P:(h % 4 + 1) * P],
                              g_wo[:, 2 * (h // 4) + k, :], start=k == 0, stop=k == 1)
                last.then_inc(fuse_mm, 1)
            pe.wait_ge(fuse_cp, 2 * H)
            pe.wait_ge(d_l1, 16 * 5)
            with pe.Fori(0, NC) as c:
                transposes(3, c)
                for k in range(KD):
                    last = mm(ps[0:64, 2, :], cq_w[:, k, :], XT[:, k, :], start=k == 0, stop=k == 1)
                last.then_inc(l_qcmm, 1)
                for k in range(KD):
                    last = mm(bank(0), k1_w[:, k, :], XT[:, k, :], start=k == 0, stop=k == 1)
                    if k == 1:
                        last.then_inc(l_kmm, 1)
                for m in range(16):
                    for k in range(KD):
                        last = mm(ps[0:32, 3, 0:HD], XT[:, k, m:CN:16], comp_w[:, KD * m + k, :],
                                  start=(m == 0 and k == 0), stop=(m == 15 and k == 1))
                last.then_inc(l_ckmm, 1)
                for b in range(CB):
                    for k in range(KD):
                        last = mm(ps[0:64, 4 + b // 4, (b % 4) * P:(b % 4 + 1) * P], XT[:, k, b * T:(b + 1) * T],
                                  v1_w[:, k, :], start=k == 0, stop=k == 1, skip_group_check=True)
                last.then_inc(l_vmm, 1)
                pe.wait_ge(l_ksq, c + 1)
                pe.wait_ge(l_qc, c + 1)
                mm(bank(2), ones[:], l1k[:, :], start=True, stop=True).then_inc(l_ksum, 1)
                pe.wait_ge(l_ckv, c + 1)
                mm(ps[:, 3, 0:1], ident[:], ones[:, 0:1], start=True, stop=True)
                pe.transpose(ps[:, 3, 0:32], ckv[:], ident[0:32, 0:32]).then_inc(l_ckT, 1)
                pe.wait_ge(l_keys, 2 * c + 2)
                pe.wait_ge(l_v, c + 1)
                pe.wait_ge(d_ck, 16 * CB * c + 16 * CB)

                def qsums(h):
                    pe.wait_ge(l_qsq, c * H + h + 1)
                    mm(ps[0:H, 4, :], onehot[:, h, :], SQ[:, h % 2, :], start=h == 0, stop=h == H - 1,
                       skip_group_check=True).then_inc(l_qsum, 1)

                for h in range(H + 1):
                    if h < H:
                        if h >= 4:
                            pe.wait_ge(l_qhalf, c * H + h - 3)
                            pe.wait_ge(l_qrest, c * H + h - 3)
                        mm(bank(h % 4), up_w[0:64, h, :], qcT[0:64, :], start=True, stop=True).then_inc(l_qmm, 1)
                    if h >= 1:
                        qsums(h - 1)
                pe.wait_ge(l_qrdy, c * H + H)
                pe.wait_ge(l_qrest, c * H + H)
                q_rms(c, 1)
                for u in range(NU + 2):
                    n = c * NU + u
                    if u < NU:
                        score(U3, u, n, lambda h, b: qT[:, 2 * u + h, b * T:(b + 1) * T], lambda h, b: keysT[:, b, :], W1)
                    if 1 <= u <= NU:
                        turn(U3, u - 1, n - 1, W1)
                    if u >= 2:
                        project(U3, 3, c, u - 2, n - 2, lambda h: go_w[:, h, :])
                    if 1 <= u <= NU:
                        weigh(U3, u - 1, n - 1, W1, lambda b: vals[0:W1, b, :])

            pe.wait_ge(d_x1o, 64)
            for h in range(H):
                pe.wait_ge(fuse_cp, 2 * H + h)
                for k in range(KD):
                    mm(ps[:, 0, k * P:(k + 1) * P], x1_qT[:, h, k * P:(k + 1) * P], x1_kT[:, h // 2, :],
                       start=True, stop=True, skip_group_check=True)
                mm(ps[:, 1, 0:D], x1_vT[:, h // 2, :], x1_o[:, h, :], start=True, stop=True).then_inc(fuse_mm, 1)
            pe.wait_ge(fuse_cp, 3 * H)
            with pe.Fori(0, NC) as c:
                transposes(4, c)
                pe.wait_ge(d_ctx, c * 32 + 32 * NC + 32)

                def query(u, n):
                    if u >= 1:
                        pe.wait_ge(U4.q_ready, n)
                    for h in range(2):
                        for k in range(KD):
                            last = mm(bank(h), x1a_w[:, KD * (2 * u + h) + k, :], XT[:, k, :], start=k == 0, stop=k == 1)
                    last.then_inc(U4.q_mm, 1)

                query(0, c * NU)
                for u in range(NU + 2):
                    n = c * NU + u
                    if u < NU:
                        pe.wait_ge(U4.q_ready, n + 1)
                        score(U4, u, n, lambda h, b: q1T[:, u % 2, h * CN + b * T:h * CN + (b + 1) * T],
                              lambda h, b: ctxT[:, b * T:(b + 1) * T], T, mask=vmaskb[:, bass.ts(c, CT), :])
                    if 1 <= u <= NU:
                        turn(U4, u - 1, n - 1, T)
                    if u < NU - 1:
                        query(u + 1, n + 1)
                    if 1 <= u <= NU:
                        weigh(U4, u - 1, n - 1, T)
                    if u >= 2:
                        project(U4, 4, c, u - 2, n - 2, lambda h: x1vo_w[:, h, :])

            pe.wait_ge(f1_cvt, 2)
            ffn(1, 5, FF1_SIZES, f1g_w, f1u_w, f1d_w)

        @block.scalar
        def _(act):
            act_ = act.activation

            def xt_copy(L, c):
                act.wait_ge(xt_psum, c + L * NC + 2)
                act_(XT[:], two(0), ACT.Copy).then_inc(xt_ready, 1)

            def ln_sqrt(L, c):
                act.wait_ge(ln_var, c + L * NC + 1)
                act_(std[:], mv[:, :, 1], ACT.Ln).then_inc(ln_log, 1)
                act.wait_ge(ln_log, c + L * NC + 1)
                act_(rstd[:], std[:], ACT.Exp, scale=-0.5).then_inc(ln_std, 1)

            def unit_copy(U, u, n, w):
                act.wait_ge(U.t_done, n + 1)
                if u >= 1:
                    act.wait_ge(U.v_done, n)
                if w == T:
                    act_(PT[:, 0:CN].rearrange("p (h m) -> p h m", h=2), ps[:, 4:6, 0:2 * P], ACT.Copy).then_inc(U.pt_ready, 1)
                else:
                    act_(PT[0:w, :].rearrange("p (h m) -> p h m", h=2), ps[0:w, 4:6, :], ACT.Copy).then_inc(U.pt_ready, 1)

            def out_copy(U, u, n, per):
                act.wait_ge(U.v_done, n + 1)
                if u >= 2:
                    act.wait_ge(U.o_done, per)
                dst = OT[:, u % 2, :].rearrange("p (h g q m) -> p q h g m", h=2, g=2, q=2)[:, 1]
                act_(dst, ps[:, 5, :].rearrange("p (h g m) -> p h g m", h=2, g=2), ACT.Copy).then_inc(U.ot_ready2, 1)

            def q_rms(n, k, scale, bias):
                act_(rrow[:], ps[0:H, 4, :], ACT.Ln, scale=scale, bias=bias).then_inc(r_ln, 1)
                act.wait_ge(r_ln, n + k * NC + 1)
                act_(rrow[:], rrow[:], ACT.Exp, scale=-0.5).then_inc(r_row, 1)

            act.wait_ge(const_v, 1)
            with act.Fori(0, NC) as c:
                xt_copy(0, c)
                for i in range(2):
                    act.wait_ge(a0_mm, c * 3 + i + 1)
                    act_(q0T[:, i, :], bank((2, 0)[i]), ACT.Copy).then_inc(a0_q, 1)
                for u in range(NU + 1):
                    n = c * NU + u
                    if u < NU:
                        act.wait_ge(U0.sub, n + 1)
                        act_(e0[:, u % 2, :], e0[:, u % 2, :], ACT.Exp, scale=0.25).then_inc(U0.exp, 1)
                    if u >= 1:
                        act.wait_ge(U0.t_done, n)
                        if u >= 2:
                            act.wait_ge(U0.v_done, n - 1)
                        act_(PT[:, 0:CN], bank(4), ACT.Copy).then_inc(U0.pt_ready, 1)
                ln_sqrt(0, c)
            act.preload_act_table_set("natural_log_exp_and_others")
            for h in range(H):
                act.wait_ge(fuse_mm, h + 1)
                act_(xvo_w[:, h, :], bank(h % 2, D), ACT.Copy).then_inc(fuse_cp, 1)
            with act.Fori(0, NC) as c:
                xt_copy(1, c)
                for h in range(H + 1):
                    if h < H:
                        act.wait_ge(x_qmm, c * H + h + 1)
                        if h >= 2:
                            act.wait_ge(x_qsum, c * H + h - 1)
                        act_(SQ[:, h % 2, :], bank(h % 2), ACT.Square).then_inc(x_qsq, 1)
                        act.wait_ge(x_kmm, c * H + h + 1)
                        if h >= 2:
                            act.wait_ge(x_ksum, c * H + h - 1)
                        act_(KSQ[:, h % 2, :], bank(2 + h % 2), ACT.Square).then_inc(x_ksq, 1)
                    if h >= 1:
                        act.wait_ge(x_ksum, c * H + h)
                        if h >= 2:
                            act.wait_ge(x_krs, c * H + h - 1)
                        act_(krms, bank(5), ACT.Ln, scale=1.0 / HD, bias=eps5[:, 0:1]).then_inc(x_kln, 1)
                        act.wait_ge(x_kln, c * H + h)
                        if h >= 2:
                            act.wait_ge(x_krdy, c * H + h - 1)
                        act_(krs, krms, ACT.Exp, scale=-0.5).then_inc(x_krs, 1)
                act.wait_ge(x_qsum, c * H + H)
                q_rms(c, 0, 1.0 / HD, eps5[0:H, 0:1])
                for u in range(NU + 1):
                    n = c * NU + u
                    if u < NU:
                        act.wait_ge(U1.sub, n + 1)
                        act_(E64[:, u % 2], E64[:, u % 2], ACT.Exp, scale=HD ** -0.5).then_inc(U1.exp, 1)
                    if u >= 1:
                        unit_copy(U1, u - 1, n - 1, T)
                        out_copy(U1, u - 1, n - 1, c * (NU - 1) + u - 2)
                ln_sqrt(1, c)

            def ffn(i, L, sizes, sg):
                nj = len(sizes)
                with act.Fori(0, NC) as c:
                    xt_copy(L, c)
                    for j, m in enumerate(sizes):
                        act.wait_ge(f_mm[i], c * nj + j + 1)
                        if j >= 2:
                            act.wait_ge(f_hid[i], c * nj + j - 1)
                        act_(silu_b[0:m, j % 2, :], ps[0:m, j % 2, :], ACT.Silu, scale=sg[0:m, j:j + 1]).then_inc(f_silu[i], 1)
                    ln_sqrt(L, c)

            ffn(0, 2, [P] * FF0, sg0)
            for h in range(H):
                act.wait_ge(fuse_mm, H + h + 1)
                act_(go_w[:, h, :], bank(h % 2, D), ACT.Copy).then_inc(fuse_cp, 1)
            act_(sinkexp[:], sinkexp[:], ACT.Exp).then_inc(const_a, 1)
            with act.Fori(0, NC) as c:
                xt_copy(3, c)
                act.wait_ge(l_qcmm, c + 1)
                act_(qcT[0:64, :], ps[0:64, 2, :], ACT.Copy).then_inc(l_qc, 1)
                act.wait_ge(l_kmm, c + 1)
                act_(l1k, bank(0), ACT.Square).then_inc(l_ksq, 1)
                act.wait_ge(l_ckmm, c + 1)
                act_(ckt[:], ps[0:32, 3, 0:HD], ACT.Square, accum_out=cks[:, 0:1]).then_inc(l_ckss, 1)
                act.wait_ge(l_ckss, c + 1)
                act_(cks[:, 1:2], cks[:, 0:1], ACT.Ln, scale=1.0 / HD, bias=eps6[0:32, 0:1]).then_inc(l_ckln, 1)
                act.wait_ge(l_ckln, c + 1)
                act_(cks[:, 2:3], cks[:, 1:2], ACT.Exp, scale=-0.5).then_inc(l_ckrs, 1)
                act.wait_ge(l_ksum, c + 1)
                act_(l1k, bank(2), ACT.Ln, scale=1.0 / HD, bias=eps6[:, 0:1]).then_inc(l_kln, 1)
                act.wait_ge(l_kln, c + 1)
                act_(l1k, l1k, ACT.Exp, scale=-0.5).then_inc(l_krs, 1)
                for h in range(H):
                    act.wait_ge(l_qmm, c * H + h + 1)
                    if h >= 2:
                        act.wait_ge(l_qsum, c * H + h - 1)
                    act_(SQ[:, h % 2, :], bank(h % 4), ACT.Square).then_inc(l_qsq, 1)
                    act_(qT[64:P, h, :], ps[64:P, h % 4, :], ACT.Copy).then_inc(l_qrest, 1)
                act.wait_ge(l_qsum, c * H + H)
                q_rms(c, 1, 1.0, eps6b[0:H, 0:1])
                for u in range(NU + 1):
                    n = c * NU + u
                    if u < NU:
                        act.wait_ge(U3.s_free, n + 1)
                        act_(E[:, u % 2, :, :, 0:T], E[:, u % 2, :, :, 0:T], ACT.Tanh, scale=1.0 / 50.0).then_inc(U3.tanh, 1)
                        act.wait_ge(U3.tanh, n + 1)
                        for h in range(2):
                            act_(E[:, u % 2, h, :, 0:T], E[:, u % 2, h, :, 0:T], ACT.Exp, scale=50.0,
                                 bias=sinkneg[:, 2 * u + h:2 * u + h + 1]).then_inc(U3.exp, 1)
                        act.wait_ge(U3.sub, n + 1)
                        act_(cb[:], cb[:], ACT.Exp).then_inc(U3.cexp, 1)
                    if u >= 1:
                        unit_copy(U3, u - 1, n - 1, W1)
                        out_copy(U3, u - 1, n - 1, c * (NU - 1) + u - 2)
                ln_sqrt(3, c)
            for h in range(H):
                act.wait_ge(fuse_mm, 2 * H + h + 1)
                act_(x1a_w[:, KD * h:KD * h + KD, :], ps[:, 0, 0:D].rearrange("p (k m) -> p k m", k=KD), ACT.Copy).then_inc(a_own, 1)
                act_(x1vo_w[:, h, :], ps[:, 1, 0:D], ACT.Copy).then_inc(fuse_cp, 1)
            with act.Fori(0, NC) as c:
                xt_copy(4, c)

                def q_copy(u, n):
                    act.wait_ge(U4.q_mm, n + 1)
                    if u >= 2:
                        act.wait_ge(U4.s_done, n - 1)
                    act_(q1T[:, u % 2, :].rearrange("p (h m) -> p h m", h=2), two(0), ACT.Copy).then_inc(U4.q_ready, 1)

                q_copy(0, c * NU)
                for u in range(NU + 1):
                    n = c * NU + u
                    if u < NU:
                        act.wait_ge(U4.s_free, n + 1)
                        act_(E64[:, u % 2], E64[:, u % 2], ACT.Exp, scale=HD ** -0.5).then_inc(U4.exp, 1)
                    if u >= 1:
                        unit_copy(U4, u - 1, n - 1, T)
                    if u < NU - 1:
                        q_copy(u + 1, n + 1)
                    if u >= 1:
                        out_copy(U4, u - 1, n - 1, c * (NU - 1) + u - 2)
                ln_sqrt(4, c)
            ffn(1, 5, FF1_SIZES, sg1)

        @block.vector
        def _(v):
            order = Order(v, v_own)
            tt, ts_, red = v.tensor_tensor, v.tensor_scalar, v.tensor_reduce

            def layer_norm(L, c, scale_row=None):
                v.wait_ge(y_done, c + L * NC + 1)
                if scale_row is None:
                    tt(Y[:], Yp, X[:, bass.ts(c, CT), :], ALU.add).then_inc(y_read, 1)
                else:
                    tt(Y[:], Yp, scale_row.unsqueeze(1).broadcast_to([P, CT, D]), ALU.mult).then_inc(y_read, 1)
                v.wait_ge(y_read, c + L * NC + 2)
                if scale_row is not None:
                    order.then(tt(Y[:], Y[:], X[:, bass.ts(c, CT), :], ALU.add))
                for t in range(CT):
                    order.then(v.bn_stats(bst[:, t, :], Y[:, t, :]))
                for t in range(CT):
                    v.tensor_copy(sm[:, 0:1], eps5[:])
                    order.then(v.bn_aggr(mv[:, t, :], bst[:, t, :]))
                ts_(mv[:, :, 1], mv[:, :, 1], LN_EPS, None, ALU.add).then_inc(ln_var, 1)
                v.wait_ge(ln_std, c + L * NC + 1)
                for t in range(CT):
                    ins = ts_(X[:, bass.ds(c * CT + t, 1), :].rearrange("p a d -> p (a d)"), Y[:, t, :], mv[:, t, 0:1], rstd[:, t:t + 1], ALU.subtract, ALU.mult)
                    if t < CT - 1:
                        order.then(ins)
                ins.then_inc(ln_done, 1)
                v.wait_ge(ln_done, c + L * NC + 1)

            LN_N = 4 + 4 + 3

            def bc(small, k=T, a_=2, b_=CT):
                return small.rearrange("p (a b) -> p a b", a=a_).unsqueeze(3).broadcast_to([P, a_, b_, k])

            def out_copy(U, u, n, per):
                v.wait_ge(U.v_done, n + 1)
                if u >= 2:
                    v.wait_ge(U.o_done, per)
                dst = OT[:, u % 2, :].rearrange("p (h g q m) -> p q h g m", h=2, g=2, q=2)[:, 0]
                v.tensor_copy(dst, ps[:, 4, :].rearrange("p (h g m) -> p h g m", h=2, g=2)).then_inc(U.ot_ready, 1)

            v.wait_ge(d_const, N_CONST)
            v.memset(eps5[:], 1e-5).then_inc(y_read, 1)
            order.then(v.memset(eps6[:], 1e-6))
            order.then(v.memset(eps6b[:], 1e-6 * HD))
            order.then(v.tensor_copy(identb[:], ident[:]))
            order.then(tt(gqk_c, gq_c, gk_c, ALU.mult))
            order.then(tt(qkw_c, qw_c, kw_c, ALU.mult))
            order.then(ts_(vmaskb[:], vmask8, -1.0, 1e30, ALU.add, ALU.mult))
            order.then(red(anykey[:], vmask8, AX.X, ALU.max))
            order.then(ts_(sinkneg[:], sinkB[:], 0.0, -1.0, ALU.max, ALU.mult))
            order.then(tt(sinkexp[:], sinkB[:], sinkneg[:], ALU.add))
            v.tensor_copy(causalb[:], causal[:].unsqueeze(1).broadcast_to([P, 8, T])).then_inc(const_v, 1)
            v.wait_ge(const_g, 2)

            v.wait_ge(d_a0, 96)
            for f in range(2):
                w = a0q_w[:, KD * f:KD * f + KD, :]
                order.then(tt(w, w, rot0[:, f, :].unsqueeze(1).broadcast_to([P, KD, D]), ALU.mult))
            tt(a0q_w[:, 0:KD, :], a0q_w[:, 0:KD, :], a0q_w[:, KD:2 * KD, :], ALU.add).then_inc(a0_w, 1)

            with v.Fori(0, NC) as c:
                order.enter(c, 1 + NU * 3 + LN_N)
                v.wait_ge(a0_mm, c * 3 + 3)
                v.tensor_copy(k0T, bank(1)).then_inc(a0_k, 1)
                v.wait_ge(a0_v, c + 1)
                for j in range(2):
                    cp = v.tensor_copy(v0bd[64 * j:64 * j + 64, :, 16 * j:16 * j + 16],
                                       ps[64 * j:64 * j + 64, 4, 0:CB * 32].rearrange("p (b n) -> p b n", n=32)[:, :, 16 * j:16 * j + 16])
                    if j == 0:
                        order.then(cp)
                cp.then_inc(a0_vbd, 1)
                for u in range(NU):
                    n = c * NU + u
                    e = e0[:, u % 2, :].rearrange("p (h k) -> p h k", k=T)
                    s = bank(2).rearrange("p (h k) -> p h k", k=T)
                    b8 = lambda x: x.unsqueeze(2).broadcast_to([P, 8, T])
                    v.wait_ge(U0.s_done, n + 1)
                    order.then(red(mx[:], s, AX.X, ALU.max))
                    if u >= 2:
                        v.wait_ge(U0.t_done, n - 1)
                    tt(e, s, b8(mx[:]), ALU.subtract).then_inc(U0.sub, 1)
                    v.wait_ge(U0.exp, n + 1)
                    order.then(red(sm[:], e, AX.X, ALU.add))
                    order.then(v.reciprocal(rs[:], sm[:]))
                    tt(e, e, b8(rs[:]), ALU.mult).then_inc(U0.p_ready, 1)
                    if u >= 1:
                        v.wait_ge(U0.v_done, n)
                        if u >= 3:
                            v.wait_ge(U0.o_done, c * (NU - 1) + u - 2)
                        v.tensor_copy(OT[:, (u - 1) % 2, 0:P], ps[:, 5, 0:P]).then_inc(U0.ot_ready, 1)
                v.wait_ge(U0.v_done, c * NU + NU)
                v.wait_ge(U0.o_done, c * (NU - 1) + NU - 2)
                v.tensor_copy(OT[:, (NU - 1) % 2, 0:P], ps[:, 5, 0:P]).then_inc(U0.ot_ready, 1)
                layer_norm(0, c)
            order.leave(NC)

            def softmax_front(U, u, n, scale=None):
                s = ps[:, 2:4, 0:CT * T].rearrange("p h (t k) -> p h t k", k=T)
                e = E64[:, u % 2]
                v.wait_ge(U.s_done, n + 1)
                order.then(red(mx[:].rearrange("p (h t) -> p h t", h=2), s, AX.X, ALU.max))
                if u >= 2:
                    v.wait_ge(U.t_done, n - 1)
                tt(e, s, bc(mx[:]), ALU.subtract).then_inc(U.s_free, 1)
                if scale is not None:
                    v.wait_ge(U.s_free, n + 1)
                    tt(e, e, scale, ALU.mult).then_inc(U.sub, 1)

            def softmax_back(U, u, n, any_=None):
                e = E64[:, u % 2]
                v.wait_ge(U.exp, n + 1)
                order.then(red(sm[:].rearrange("p (h t) -> p h t", h=2), e, AX.X, ALU.add))
                order.then(v.reciprocal(rs[:], sm[:]))
                if any_ is not None:
                    order.then(tt(rs[:].rearrange("p (h t) -> p h t", h=2), rs[:].rearrange("p (h t) -> p h t", h=2),
                                  any_, ALU.mult))
                tt(e, e, bc(rs[:]), ALU.mult).then_inc(U.p_ready, 1)

            def rq_copy(n, k):
                v.wait_ge(r_T, n + k * NC + 1)
                v.tensor_copy(rq[:].rearrange("p t h -> p (t h)"), ps[:, 4, 0:CT * H]).then_inc(r_rq, 1)
                v.wait_ge(r_rq, n + k * NC + 1)

            def rq_of(u, w):
                return rq[:, :, 2 * u:2 * u + 2].rearrange("p t h -> p h t").unsqueeze(3).broadcast_to([P, 2, CT, w])

            with v.Fori(0, NC) as c:
                order.enter(c, NU * 3 + LN_N)
                for h in range(H + 1):
                    if h < H:
                        v.wait_ge(x_qsq, c * H + h + 1)
                        v.tensor_copy(qT[:, h, :], bank(h % 2)).then_inc(x_qcp, 1)
                    if h >= 1:
                        v.wait_ge(x_krs, c * H + h)
                        v.scalar_tensor_tensor(out=kT[:, h - 1, :], in0=bank(2 + (h - 1) % 2), scalar=gqk_c, in1=krs,
                                               op0=ALU.mult, op1=ALU.mult).then_inc(x_krdy, 1)
                rq_copy(c, 0)
                for u in range(NU + 1):
                    n = c * NU + u
                    if u < NU:
                        softmax_front(U1, u, n, rq_of(u, T))
                        softmax_back(U1, u, n)
                    if u >= 1:
                        out_copy(U1, u - 1, n - 1, c * (NU - 1) + u - 2)
                layer_norm(1, c)
            order.leave(NC)

            def ffn(i, L, sizes, su, row):
                nj = len(sizes)
                with v.Fori(0, NC) as c:
                    order.enter(c, 1 + LN_N)
                    for j, m in enumerate(sizes):
                        v.wait_ge(f_silu[i], c * nj + j + 1)
                        if j >= 2:
                            v.wait_ge(f_down[i], c * (nj - 1) + j - 1)
                        v.scalar_tensor_tensor(out=hidT[0:m, j % 2, :], in0=ps[0:m, 2 + j % 2, :], scalar=su[0:m, j:j + 1],
                                               in1=silu_b[0:m, j % 2, :], op0=ALU.mult, op1=ALU.mult).then_inc(f_hid[i], 1)
                    layer_norm(L, c, rowsB[:, i, :])
                order.leave(NC)

            ffn(0, 2, [P] * FF0, su0, 0)

            v.wait_ge(const_a, 1)
            with v.Fori(0, NC) as c:
                order.enter(c, 4 + NU * 12 + LN_N)
                cosb = cos1[:].unsqueeze(1).broadcast_to([64, CB, T])
                sinb = sin1[:].unsqueeze(1).broadcast_to([64, CB, T])
                r3 = lambda x: x.rearrange("p (b t) -> p b t", t=T)
                v.wait_ge(l_ksq, c + 1)
                order.then(tt(r3(l1t1[0:64, :]), r3(ps[0:64, 0, :]), cosb, ALU.mult))
                order.then(tt(r3(l1t2[0:32, :]), r3(ps[32:64, 0, :]), sinb[32:64], ALU.mult))
                order.then(tt(r3(l1t2[32:64, :]), r3(ps[0:32, 0, :]), sinb[0:32], ALU.mult))
                v.tensor_copy(l1t1[64:P, :], ps[64:P, 0, :])
                order.then(tt(l1t1[0:64, :], l1t1[0:64, :], l1t2[0:64, :], ALU.add))
                v.wait_ge(l_ckrs, c + 1)
                v.scalar_tensor_tensor(out=ckv[:], in0=ps[0:32, 3, 0:HD], scalar=cks[:, 2:3], in1=kwB[:],
                                       op0=ALU.mult, op1=ALU.mult).then_inc(l_ckv, 1)
                v.wait_ge(l_vmm, c + 1)
                v.tensor_copy(vals[0:T, :, :], ps[0:T, 4:6, :].rearrange("p q (b n) -> p (q b) n", n=HD)).then_inc(l_v, 1)
                v.wait_ge(l_krs, c + 1)
                v.scalar_tensor_tensor(out=keysT[:, :, 0:T], in0=r3(l1t1), scalar=qkw_c, in1=r3(l1k),
                                       op0=ALU.mult, op1=ALU.mult).then_inc(l_keys, 1)
                v.wait_ge(l_ckT, c + 1)
                ts_(keysT[:, :, T:W1], ps[:, 3, 0:32].rearrange("p (b n) -> p b n", n=NB), qw_c, None, ALU.mult).then_inc(l_keys, 1)
                for h in range(H):
                    if h >= 2:
                        v.wait_ge(l_qrdy, c * H + h - 1)
                    v.wait_ge(l_qsq, c * H + h + 1)
                    i = h % 4
                    tt(r3(qT[0:64, h, :]), r3(ps[0:64, i, :]), cosb, ALU.mult)
                    tt(r3(SQr[h % 2][0:32, :]), r3(ps[32:64, i, :]), sinb[32:64], ALU.mult)
                    tt(r3(SQr[h % 2][32:64, :]), r3(ps[0:32, i, :]), sinb[0:32], ALU.mult).then_inc(l_qhalf, 1)
                rq_copy(c, 1)
                for u in range(NU + 1):
                    n = c * NU + u
                    if u < NU:
                        s = ps[:, 2:4, 0:CT * W1].rearrange("p h (t k) -> p h t k", k=W1)
                        e, sw = E[:, u % 2], E[:, u % 2, :, :, 0:T]
                        v.wait_ge(U3.s_done, n + 1)
                        if u >= 2:
                            v.wait_ge(U3.t_done, n - 1)
                        tt(e, s, rq_of(u, W1), ALU.mult).then_inc(U3.s_free, 1)
                        v.wait_ge(U3.s_free, n + 1)
                        for h in range(2):
                            order.then(tt(cb[:, h, :, 0:NB], e[:, h, :, T:W1],
                                          blockmask[:].unsqueeze(1).broadcast_to([P, CT, NB]), ALU.add))
                        order.then(v.tensor_copy(cb[:, :, :, NB:NB + 1].rearrange("p h t k -> p h (t k)"),
                                                 sinkB[:, 2 * u:2 * u + 2].unsqueeze(2).broadcast_to([P, 2, CT])))
                        order.then(red(mx[:].rearrange("p (h t) -> p h t", h=2), cb[:], AX.X, ALU.max))
                        tt(cb[:], cb[:], bc(mx[:], NB + 1), ALU.subtract).then_inc(U3.sub, 1)
                        v.wait_ge(U3.exp, 2 * n + 2)
                        for h in range(2):
                            order.then(tt(sw[:, h], sw[:, h], keep[:].unsqueeze(1).broadcast_to([P, CT, T]), ALU.mult))
                        order.then(red(sm[:].rearrange("p (h t) -> p h t", h=2), sw, AX.X, ALU.add))
                        order.then(tt(sm[:].rearrange("p (h t) -> p h t", h=2), sm[:].rearrange("p (h t) -> p h t", h=2),
                                      sinkexp[:, 2 * u:2 * u + 2].unsqueeze(2).broadcast_to([P, 2, CT]), ALU.add))
                        order.then(v.reciprocal(rs[:], sm[:]))
                        order.then(tt(sw, sw, bc(rs[:]), ALU.mult))
                        v.wait_ge(U3.cexp, n + 1)
                        order.then(red(mx[:].rearrange("p (h t) -> p h t", h=2), cb[:], AX.X, ALU.add))
                        order.then(v.reciprocal(sm[:], mx[:]))
                        tt(e[:, :, :, T:W1], cb[:, :, :, 0:NB], bc(sm[:], NB), ALU.mult).then_inc(U3.p_ready, 1)
                    if u >= 1:
                        out_copy(U3, u - 1, n - 1, c * (NU - 1) + u - 2)
                layer_norm(3, c)
            order.leave(NC)

            with v.Fori(0, NC) as c:
                order.enter(c, NU * 4 + LN_N)
                for u in range(NU + 1):
                    n = c * NU + u
                    if u < NU:
                        softmax_front(U4, u, n)
                        softmax_back(U4, u, n, anykey[:, bass.ts(c, CT)].unsqueeze(1).broadcast_to([P, 2, CT]))
                    if u >= 1:
                        out_copy(U4, u - 1, n - 1, c * (NU - 1) + u - 2)
                layer_norm(4, c)
            order.leave(NC)
            ffn(1, 5, FF1_SIZES, su1, 1)


def tables():
    import numpy as np
    f = np.float32
    pos = np.arange(T, dtype=f)
    tok = np.arange(P) % T
    key = np.arange(T)
    seen = key[None, :] <= tok[:, None]
    th0 = (f(1.0) / f(10000.0) ** (np.arange(0, 8, 2, dtype=f) / f(8))).astype(f)
    fr0 = (np.arange(H, dtype=f)[:, None] * th0[None, :]).astype(f)
    part = np.arange(D) % 16
    sign0 = np.where(part % 8 < 4, f(-1), f(1))
    th1 = (f(1.0) / f(10000.0) ** (np.arange(0, 64, 2, dtype=f) / f(64))).astype(f)
    fr1 = (th1[:, None] * pos[None, :]).astype(f)
    sign1 = np.where(np.arange(64) < 32, f(1), f(-1))
    return {
        "c_ident": np.eye(P, dtype=f),
        "c_causal": np.where(seen, f(0), f(NEG)).astype(f),
        "c_keep": seen.astype(f),
        "c_blockmask": np.where(np.arange(NB)[None, :] * 16 + 15 < tok[:, None], f(0), f(NEG)).astype(f),
        "c_cos0": np.cos(fr0)[np.arange(D) // 16, part % 4].astype(f),
        "c_sin0": (np.sin(fr0)[np.arange(D) // 16, part % 4] * sign0).astype(f),
        "c_cos1": np.cos(fr1)[np.arange(64) % 32].astype(f),
        "c_sin1": (np.sin(fr1)[np.arange(64) % 32] * sign1[:, None]).astype(f),
        "c_onehot": np.eye(H, dtype=f).reshape(-1),
        "c_headmask": (np.arange(P)[:, None] // 16 == np.arange(8)[None, :]).astype(f),
    }


def layouts(i):
    import numpy as np
    g = {k: np.asarray(v) for k, v in i.items()}
    straight = np.array([0, 2, 4, 6, 1, 3, 5, 7, 8, 10, 12, 14, 9, 11, 13, 15])
    partner = np.array([1, 3, 5, 7, 0, 2, 4, 6, 9, 11, 13, 15, 8, 10, 12, 14])
    heads = 16 * np.arange(H)[:, None]
    qT, kT = g["L0_attn_Wq"].T, g["L0_attn_Wk"].T
    up = g["L1_attn_Wq_up"]
    col = lambda x: x.reshape(-1, 1)
    row = lambda x: x.reshape(-1)
    words = lambda x: np.ascontiguousarray(x).view(np.int32)
    arrays = {
        "x": g["x"].reshape(NT, P, D),
        "ctx": g["ctx_1024"].reshape(NC, 2, 2, 2, T, P).transpose(0, 2, 4, 1, 3, 5).reshape(NC, P, 4 * P),
        "ctxT": g["ctx_1024"].reshape(B * T, P).T,
        "mask": g["mask_BxS2_bf1"].view(np.uint8),
        "a0_q": np.concatenate([qT[:, (heads + straight).ravel()], qT[:, (heads + partner).ravel()]], 0),
        "a0_k": np.tile(kT[:, straight], (1, 8)),
        "a0_v": g["L0_attn_Wv"].T,
        "a0_o": g["L0_attn_Wo"].T,
        "x0_q": g["L0_xattn_Wq"], "x0_k": g["L0_xattn_Wk"],
        "x0_vT": g["L0_xattn_Wv"].T, "x0_o": g["L0_xattn_Wo"],
        "gq": col(g["L0_xattn_gq"]), "gk": col(g["L0_xattn_gk"]),
        "f0_g": words(g["L0_ffn_w_gate"]), "f0_u": words(g["L0_ffn_w_up"]), "f0_d": words(g["L0_ffn_w_down"]),
        "f0_sg": g["L0_ffn_s_gate"].reshape(FF0, P).T, "f0_su": g["L0_ffn_s_up"].reshape(FF0, P).T, "f0_sd": row(g["L0_ffn_s_down"]),
        "l1_qc": g["L1_attn_Wq_c"], "l1_up": up,
        "l1_k": g["L1_attn_Wk"], "l1_v": g["L1_attn_Wv"],
        "l1_comp": g["L1_attn_W_comp"],
        "qw": col(g["L1_attn_q_norm_w"]), "kw": col(g["L1_attn_k_norm_w"]), "kw_row": row(g["L1_attn_k_norm_w"]),
        "sink": row(g["L1_attn_sink"]),
        "l1_gT": g["L1_attn_Wg"].transpose(0, 2, 1).reshape(4 * D, 4 * HD), "l1_o": g["L1_attn_Wo"],
        "x1_qT": g["L1_xattn_Wq"].T, "x1_kT": g["L1_xattn_Wk"].T, "x1_vT": g["L1_xattn_Wv"].T, "x1_o": g["L1_xattn_Wo"],
        "f1_g": g["L1_ffn_wq_gate"].T, "f1_u": g["L1_ffn_wq_up"].T, "f1_d": g["L1_ffn_wq_down"].T,
        "f1_sg": g["L1_ffn_s_gate"][:640].reshape(5, P).T, "f1_sg_tail": col(g["L1_ffn_s_gate"][640:]),
        "f1_su": g["L1_ffn_s_up"][:640].reshape(5, P).T, "f1_su_tail": col(g["L1_ffn_s_up"][640:]), "f1_sd": row(g["L1_ffn_s_down"]),
        **tables(),
    }
    return {"in_" + k: np.ascontiguousarray(v) for k, v in arrays.items()}


def kernel(**inputs):
    import concourse.bacc as bacc
    from concourse.bass_utils import run_bass_kernel_spmd

    nc = bacc.Bacc("TRN2", target_bir_lowering=False, num_devices=1)
    arrays = layouts(inputs)
    aps = {k[3:]: nc.dram_tensor(k, v.shape, mybir.dt.from_np(v.dtype), kind="ExternalInput").ap() for k, v in arrays.items()}
    out = nc.dram_tensor("out", (NT, P, D), F32, kind="ExternalOutput").ap()
    build(nc, aps, out)
    r = run_bass_kernel_spmd(nc, [arrays], core_ids=[0])
    return r.results[0]["out"].reshape(B, T, D)
```

```python
from contextlib import ExitStack

import concourse.bass as bass
from concourse import mybir

F32 = mybir.dt.float32
BF16 = mybir.dt.bfloat16
I32 = mybir.dt.int32
I8 = mybir.dt.int8
U8 = mybir.dt.uint8
ALU = mybir.AluOpType
ACT = mybir.ActivationFunctionType
AX = mybir.AxisListType

P = 128
B, T, D = 32, 64, 256
NT = B * T // P
NC = 4
CT = NT // NC
CN = CT * P
CB = CN // T
KD = D // P
H = 16
HD = 128
NU = H // 2
NB = 4
W1 = T + NB
NEG = -1e30
LN_EPS = 1e-5
FF0 = 1024 // P
FF1_SIZES = [128] * 5 + [64]
FF1N = 704


class Order:

    def __init__(self, eng, sem):
        self.eng, self.sem, self.base, self.n, self.it, self.per = eng, sem, 0, 0, None, 0

    def enter(self, it, per):
        self.it, self.per, self.n = it, per, 0

    def leave(self, trips):
        assert self.n == self.per, (self.n, self.per)
        self.base += trips * self.per
        self.it, self.n = None, 0

    def then(self, ins):
        ins.then_inc(self.sem, 1)
        if self.it is None:
            self.base += 1
            self.eng.wait_ge(self.sem, self.base)
        else:
            self.n += 1
            self.eng.wait_ge(self.sem, self.it * self.per + (self.base + self.n))


def build(nc, a, out):
    ctx = ExitStack()
    with ctx:
        def sb(name, shape, dt=F32):
            return ctx.enter_context(nc.sbuf_tensor(name, shape, dt))

        def sem(name):
            return ctx.enter_context(nc.semaphore(name))

        X = sb("X", [P, NT, D])
        Xc = sb("Xc", [P, CT, D])
        XT = sb("XT", [P, KD, CN])
        ctxT = sb("ctxT", [P, CN])
        ctxN = sb("ctxN", [P, 4, P])
        R1 = sb("R1", [P, 12032])
        R2 = sb("R2", [P, 8224])
        WL = sb("WL", [P, 8192])
        WU = sb("WU", [P, 8192])
        Eflat = sb("E", [P, 2 * 2 * CT * W1])
        PT = sb("PT", [P, 2 * CN])
        OT = sb("OT", [P, 2, 2 * CN])
        Y = sb("Y", [P, CT, D])
        ident = sb("ident", [P, P])
        identb = sb("identb", [P, P], BF16)
        causal = sb("causal", [P, T])
        causalb = sb("causalb", [P, 8, T], BF16)
        keep = sb("keep", [P, T])
        blockmask = sb("blockmask", [P, NB])
        rot0 = sb("rot0", [P, 2, D])
        cos1 = sb("cos1", [64, T])
        sin1 = sb("sin1", [64, T])
        headmask = sb("headmask", [P, 8])
        ones = sb("ones", [P, P])
        onehot = sb("onehot", [P, H, H])
        vmaskb = sb("vmaskb", [P, NT, T], BF16)
        anykey = sb("anykey", [P, NT])
        cols = sb("cols", [P, 40])
        rowsB = sb("rowsB", [P, 2, D])
        kwB = sb("kwB", [32, HD])
        sinkB = sb("sinkB", [P, H])
        sinkneg = sb("sinkneg", [P, H])
        sinkexp = sb("sinkexp", [P, H])
        rrow = sb("rrow", [H, CN])
        rq = sb("rq", [P, CT, H])
        mx = sb("mx", [P, 8])
        sm = sb("sm", [P, 8])
        rs = sb("rs", [P, 8])
        cb = sb("cb", [P, 2, CT, NB + 1])
        bst = sb("bst", [P, CT, 6])
        mv = sb("mv", [P, CT, 2])
        std = sb("std", [P, CT])
        rstd = sb("rstd", [P, CT])
        ckv = sb("ckv", [32, HD])
        ckt = sb("ckt", [32, HD])
        cks = sb("cks", [32, 4])
        eps5, eps6, eps6b = sb("eps5", [P, 1]), sb("eps6", [P, 1]), sb("eps6b", [P, 1])
        ps = ctx.enter_context(nc.psum_tensor("ps", [P, 8, CN], F32))

        gq_c, gk_c, gqk_c = cols[:, 0:1], cols[:, 1:2], cols[:, 2:3]
        qw_c, kw_c, qkw_c = cols[:, 3:4], cols[:, 4:5], cols[:, 5:6]
        sg0, su0 = cols[:, 6:14], cols[:, 14:22]
        sg1, su1 = cols[:, 22:28], cols[:, 28:34]

        def view(region, at, *shape):
            n = 1
            for s in shape:
                n *= s
            v = region[:, at:at + n]
            if len(shape) == 2:
                v = v.rearrange("p (a b) -> p a b", b=shape[1])
            if len(shape) == 3:
                v = v.rearrange("p (a b c) -> p a b c", b=shape[1], c=shape[2])
            return v

        xq_w = view(R1, 0, KD, H * HD)
        xk_w = view(R1, 4096, H * HD)
        xvo_w = view(R1, 6144, H, D)
        cq_w = view(R1, 0, KD, 64)
        up_w = view(R1, 128, H, HD)
        k1_w = view(R1, 3200, KD, HD)
        v1_w = view(R1, 3584, KD, HD)
        comp_w = view(R1, 3840, 16 * KD, HD)
        go_w = view(R1, 7936, H, D)
        f1g_w = view(R1, 0, KD, FF1N)
        f1u_w = view(R1, 1408, KD, FF1N)
        f1d_w = view(R1, 2816, 6, D)
        a0q_w = view(R2, 0, 2 * KD, D)
        a0k_w = view(R2, 1024, KD, P)
        a0v_w = view(R2, 1536, KD, 16)
        a0o_w = view(R2, 1568, KD, D)
        f0g_w = view(R2, 2080, KD, 1024)
        f0u_w = view(R2, 4128, KD, 1024)
        f0d_w = view(R2, 6176, FF0, D)
        x1a_w = view(R2, 0, H * KD, HD)
        x1vo_w = view(R2, 4096, H, D)
        x0_vT, x0_o = view(WU, 0, H, P), view(WU, 2048, H, D)
        g_wgT, g_wo = view(WU, 0, 8, CN), view(WU, 4096, 8, D)
        x1_qT, x1_kT, x1_vT = view(WL, 2048, H, D), view(WL, 6144, 8, P), view(WL, 7168, 8, P)

        def x1_o(h):
            if h < 8:
                return OT[:, h // 4, (h % 4) * D:(h % 4 + 1) * D]
            if h < 12:
                return PT[:, (h - 8) * D:(h - 7) * D]
            return Eflat[:, (h - 12) * D:(h - 11) * D]
        raw0 = view(WU, 6144, 1536).bitcast(I32)
        vmask8 = view(WU, 7680, 256).bitcast(U8).rearrange("p (t k) -> p t k", k=T)
        raw1 = view(WL, 0, 4352).bitcast(I32)
        q0T = view(WL, 0, 2, CN)
        k0T = view(WL, 1024, CN)
        v0bd = view(WL, 2560, CB, 32)
        kbd = view(WL, 3840, CB, 8 * T)
        qT = view(WL, 0, H, CN)
        kT = view(WU, 0, H, CN)
        krms, krs = PT[:, 0:CN], PT[:, CN:2 * CN]
        SQ, KSQ = (OT[:, j, :].rearrange("p (s m) -> p s m", s=2) for j in range(2))
        qcT = view(WU, 0, CN)
        keysT = view(WU, 512, CB, W1)
        E = Eflat[:].rearrange("p (r h t k) -> p r h t k", r=2, h=2, t=CT)
        E64 = Eflat[:, 0:4 * CT * T].rearrange("p (r h t k) -> p r h t k", r=2, h=2, t=CT)
        vals = view(WU, 1056, CB, HD)
        l1t1, l1t2, l1k = (view(WU, 2080 + CN * j, CN) for j in range(3))
        q1T = view(WU, 0, 2, 2 * CN)
        e0 = view(WL, 2816, 2, CN)
        SQr = [l1t1, l1t2]
        silu_b = view(WL, 0, 2, CN)
        hidT = view(WL, 1024, 2, CN)

        d_x, d_const, d_a0, d_x0, d_x0o, d_f0 = (sem(n) for n in ("d_x", "d_const", "d_a0", "d_x0", "d_x0o", "d_f0"))
        d_l1, d_l1o, d_x1o, d_f1, d_ctxT, d_ctxN, d_ck, d_out = (
            sem(n) for n in ("d_l1", "d_l1o", "d_x1o", "d_f1", "d_ctxT", "d_ctxN", "d_ck", "d_out"))
        v_own, a_own, g_own = sem("v_own"), sem("a_own"), sem("g_own")
        const_v, const_g, const_a = sem("const_v"), sem("const_g"), sem("const_a")
        xc_ready, xt_psum, xt_ready = (sem(n) for n in ("xc_ready", "xt_psum", "xt_ready"))
        y_done, y_read, ln_var, ln_log, ln_std, ln_done = (sem(n) for n in ("y_done", "y_read", "ln_var", "ln_log", "ln_std", "ln_done"))
        fuse_mm, fuse_cp = sem("fuse_mm"), sem("fuse_cp")
        f0_cvt, f1_cvt = sem("f0_cvt"), sem("f1_cvt")

        class Unit:

            def __init__(s, n):
                s.q_mm, s.q_ready, s.s_done, s.s_free, s.sub, s.tanh, s.exp, s.cexp = (
                    sem(f"{n}_{w}") for w in ("q_mm", "q_ready", "s_done", "s_free", "sub", "tanh", "exp", "cexp"))
                s.p_ready, s.t_done, s.pt_ready, s.v_done, s.ot_ready, s.o_done = (
                    sem(f"{n}_{w}") for w in ("p_ready", "t_done", "pt_ready", "v_done", "ot_ready", "o_done"))
                s.ot_ready2 = sem(f"{n}_ot_ready2")

        U0, U1, U3, U4 = Unit("sa0"), Unit("xa0"), Unit("sa1"), Unit("xa1")
        a0_w, a0_mm, a0_q, a0_k, a0_v, a0_vbd, a0_kbd = (
            sem(f"a0_{w}") for w in ("w", "mm", "q", "k", "v", "vbd", "kbd"))
        x_qmm, x_kmm, x_qsq, x_qcp, x_ksq, x_ksum, x_kln, x_krs, x_krdy, x_qsum = (
            sem(f"x_{w}") for w in ("qmm", "kmm", "qsq", "qcp", "ksq", "ksum", "kln", "krs", "krdy", "qsum"))
        r_ln, r_row, r_T, r_rq = (sem(f"r_{w}") for w in ("ln", "row", "T", "rq"))
        (l_qcmm, l_qc, l_kmm, l_vmm, l_ckmm, l_ksq, l_ksum, l_kln, l_krs, l_keys, l_v, l_ckss, l_ckln, l_ckrs, l_ckv,
         l_ckT, l_qmm, l_qsq, l_qrest, l_qhalf, l_qrdy, l_qsum) = (
            sem(f"l_{w}") for w in ("qcmm", "qc", "kmm", "vmm", "ckmm", "ksq", "ksum", "kln", "krs", "keys", "v",
                                    "ckss", "ckln", "ckrs", "ckv", "ckT", "qmm", "qsq", "qrest", "qhalf", "qrdy",
                                    "qsum"))
        f_mm = [sem("f0_mm"), sem("f1_mm")]
        f_silu = [sem("f0_silu"), sem("f1_silu")]
        f_hid = [sem("f0_hid"), sem("f1_hid")]
        f_down = [sem("f0_down"), sem("f1_down")]

        def bank(i, n=CN):
            return ps[:, i, 0:n]

        def two(i):
            return ps[:, i:i + 2, :]

        Yp = ps[:, 6:8, :].rearrange("p a (b n) -> p (a b) n", n=D)

        block = ctx.enter_context(nc.Block())

        @block.sync
        def _(sp):
            def load(dst, src, s):
                sp.dma_start(dst, src).then_inc(s, 16)

            load(X[:, 0:CT, :], a["x"][0:CT].rearrange("t p d -> p t d"), d_x)
            load(ident[:], a["c_ident"], d_const)
            load(a0q_w, a["a0_q"].rearrange("(f p) n -> p f n", p=P), d_a0)
            load(a0k_w, a["a0_k"].rearrange("(f p) n -> p f n", p=P), d_a0)
            load(rot0[:, 0, :], a["c_cos0"].partition_broadcast(P), d_a0)
            load(rot0[:, 1, :], a["c_sin0"].partition_broadcast(P), d_a0)
            load(a0v_w, a["a0_v"].rearrange("(f p) n -> p f n", p=P), d_a0)
            load(a0o_w, a["a0_o"].rearrange("(f p) n -> p f n", p=P), d_a0)
            for dst, name in ((causal[:], "c_causal"), (keep[:], "c_keep"), (blockmask[:], "c_blockmask"),
                              (cos1[:], "c_cos1"), (sin1[:], "c_sin1"),
                              (headmask[:], "c_headmask")):
                load(dst, a[name], d_const)
            load(X[:, CT:NT, :], a["x"][CT:NT].rearrange("t p d -> p t d"), d_x)
            for i, name in enumerate(("gq", "gk", None, "qw", "kw")):
                if name:
                    load(cols[:, i:i + 1], a[name], d_const)
            load(sg0, a["f0_sg"], d_const)
            load(su0, a["f0_su"], d_const)
            for dst, name in ((sg1, "f1_sg"), (su1, "f1_su")):
                load(dst[:, 0:5], a[name], d_const)
                load(dst[0:64, 5:6], a[name + "_tail"], d_const)
            load(rowsB[:, 0, :], a["f0_sd"].partition_broadcast(P), d_const)
            load(rowsB[:, 1, :], a["f1_sd"].partition_broadcast(P), d_const)
            load(onehot[:].rearrange("p h g -> p (h g)"), a["c_onehot"].partition_broadcast(P), d_const)
            load(kwB[:], a["kw_row"].partition_broadcast(32), d_const)
            load(sinkB[:], a["sink"].partition_broadcast(P), d_const)
            mk = a["mask"].rearrange("(t two) k -> two t k", two=2)
            for j in range(2):
                load(vmask8[64 * j:64 * j + 64, :, :], mk[j].partition_broadcast(64), d_const)
            load(raw0[:, 0:512].rearrange("p (k n) -> p k n", n=256), a["f0_g"].rearrange("(k p) n -> p k n", p=P), d_f0)
            load(raw0[:, 512:1024].rearrange("p (k n) -> p k n", n=256), a["f0_u"].rearrange("(k p) n -> p k n", p=P), d_f0)
            load(raw0[:, 1024:1536].rearrange("p (j n) -> p j n", n=64), a["f0_d"].rearrange("(j p) n -> p j n", p=P), d_f0)
            load(x0_vT, a["x0_vT"].rearrange("(h p) c -> p h c", p=P), d_x0o)
            load(x0_o, a["x0_o"].rearrange("(h p) n -> p h n", p=P), d_x0o)
            load(xq_w, a["x0_q"].rearrange("(k p) n -> p k n", p=P), d_x0)
            load(xk_w, a["x0_k"], d_x0)

            def load_ctxT(c):
                sp.dma_start(ctxT[:], a["ctxT"][:, bass.ts(c, CN)]).then_inc(d_ctxT, 16)

            def load_ctxN(c):
                sp.dma_start(ctxN[:], a["ctx"][bass.ds(c, 1)].rearrange("a p (g n) -> p (a g) n", n=P)).then_inc(d_ctxN, 16)

            load_ctxT(0)
            load_ctxN(0)
            with sp.Fori(1, NC) as c:
                sp.wait_ge(x_kmm, c * H)
                load_ctxT(c)
                sp.wait_ge(y_done, c + NC)
                load_ctxN(c)
            sp.wait_ge(y_done, 2 * NC)
            load(cq_w, a["l1_qc"].rearrange("(k p) n -> p k n", p=P), d_l1)
            load(up_w[0:64], a["l1_up"].rearrange("p (h n) -> p h n", n=HD), d_l1)
            load(k1_w, a["l1_k"].rearrange("(k p) n -> p k n", p=P), d_l1)
            load(v1_w, a["l1_v"].rearrange("(k p) n -> p k n", p=P), d_l1)
            load(comp_w, a["l1_comp"].rearrange("(m p) n -> p m n", p=P), d_l1)
            load(g_wgT, a["l1_gT"].rearrange("(m p) n -> p m n", p=P), d_l1o)
            load(g_wo, a["l1_o"].rearrange("(m p) n -> p m n", p=P), d_l1o)
            load(x1_qT, a["x1_qT"].rearrange("(h p) n -> p h n", p=P), d_x1o)
            load(x1_kT, a["x1_kT"].rearrange("(h p) n -> p h n", p=P), d_x1o)
            load(x1_vT, a["x1_vT"].rearrange("(h p) n -> p h n", p=P), d_x1o)
            x1_o_raw = a["x1_o"].rearrange("(h p) n -> p h n", p=P)
            load(OT[:].rearrange("p s (h n) -> p (s h) n", n=D), x1_o_raw[:, 0:8, :], d_x1o)
            load(PT[:].rearrange("p (h n) -> p h n", n=D), x1_o_raw[:, 8:12, :], d_x1o)
            load(Eflat[:, 0:4 * D].rearrange("p (h n) -> p h n", n=D), x1_o_raw[:, 12:16, :], d_x1o)
            load_ctxT(0)
            load_ctxN(0)
            with sp.Fori(0, NC) as c:
                sp.wait_ge(l_ckv, c + 1)
                for b in range(CB):
                    sp.dma_start(vals[T:W1, b, :], ckv[NB * b:NB * b + NB, :]).then_inc(d_ck, 16)
            sp.wait_ge(y_done, 4 * NC)
            load(raw1[:, 0:1408].rearrange("p (k n) -> p k n", n=FF1N), a["f1_g"].rearrange("(k p) n -> p k n", p=P), d_f1)
            load(raw1[:, 1408:2816].rearrange("p (k n) -> p k n", n=FF1N), a["f1_u"].rearrange("(k p) n -> p k n", p=P), d_f1)
            load(raw1[:, 2816:4096].rearrange("p (j n) -> p j n", n=D),
                 a["f1_d"][0:640].rearrange("(j p) n -> p j n", p=P), d_f1)
            load(raw1[0:64, 4096:4352], a["f1_d"][640:704], d_f1)
            with sp.Fori(1, NC) as c:
                sp.wait_ge(U4.s_done, c * NU)
                load_ctxT(c)
                sp.wait_ge(y_done, c + 4 * NC)
                load_ctxN(c)
            with sp.Fori(0, NC) as c:
                sp.wait_ge(ln_done, c + 5 * NC + 1)
                sp.dma_start(out[bass.ts(c, CT)].rearrange("t p d -> p t d"), X[:, bass.ts(c, CT), :]).then_inc(d_out, 16)
            sp.wait_ge(d_out, 16 * NC)

        N_CONST = 16 * (1 + 1 + 6 + 4 + 2 + 4 + 2 + 1 + 1 + 2)

        @block.gpsimd
        def _(g):
            order = Order(g, g_own)

            def fetch(L, c):
                if L == 0:
                    g.wait_ge(d_x, 32)
                else:
                    g.wait_ge(ln_done, c + (L - 1) * NC + 1)
                g.wait_ge(xt_psum, c + L * NC + 1)
                g.tensor_copy(Xc[:], X[:, bass.ts(c, CT), :]).then_inc(xc_ready, 1)

            g.memset(ones[:], 1.0).then_inc(const_g, 1)
            g.memset(v0bd, 0.0).then_inc(const_g, 1)
            g.wait_ge(const_g, 2)
            g.sem_inc(xt_psum, 1)
            with g.Fori(0, NC) as c:
                fetch(0, c)
                g.wait_ge(a0_k, c + 1)
                g.wait_ge(d_const, N_CONST)
                for b in range(CB):
                    g.tensor_tensor(kbd[:, b, :].rearrange("p (h k) -> p h k", k=T),
                                    k0T[:, b * T:(b + 1) * T].unsqueeze(1).broadcast_to([P, 8, T]),
                                    headmask[:].unsqueeze(2).broadcast_to([P, 8, T]), ALU.mult).then_inc(a0_kbd, 1)
            fetch(1, 0)
            g.wait_ge(d_f0, 48)
            g.tensor_copy(R2[:, 2080:8224], raw0.bitcast(I8)).then_inc(f0_cvt, 1)
            with g.Fori(1, NC) as c:
                fetch(1, c)
            with g.Fori(0, NC) as c:
                fetch(2, c)
            fetch(3, 0)

            def rotary_sums(c):
                for h in range(H):
                    g.wait_ge(l_qhalf, c * H + h + 1)
                    g.tensor_tensor(qT[0:64, h, :], qT[0:64, h, :], SQr[h % 2][0:64, :], ALU.add).then_inc(l_qrdy, 1)

            with g.Fori(0, NC - 1) as c:
                fetch(3, c + 1)
                rotary_sums(c)
            fetch(4, 0)
            rotary_sums(NC - 1)
            g.wait_ge(y_done, 4 * NC)
            g.wait_ge(d_f1, 64)
            g.tensor_scalar(R1[:, 0:4096], raw1[:, 0:4096], -128.0, None, ALU.add).then_inc(f1_cvt, 1)
            g.tensor_scalar(R1[0:64, 4096:4352], raw1[0:64, 4096:4352], -128.0, None, ALU.add).then_inc(f1_cvt, 1)
            with g.Fori(1, NC) as c:
                fetch(4, c)
            with g.Fori(0, NC) as c:
                fetch(5, c)

        @block.tensor
        def _(pe):
            mm = pe.matmul

            def transposes(L, c, b=0):
                pe.wait_ge(xc_ready, c + L * NC + 1)
                for k in range(KD):
                    for t in range(CT):
                        last = pe.transpose(ps[:, b + k, t * P:(t + 1) * P], Xc[:, t, k * P:(k + 1) * P], ident[:])
                last.then_inc(xt_psum, 1)

            def score(U, u, n, lhs, rhs, w, mask=None, deep=False):
                s = 2 - 2 * (u % 2) if deep else 2
                if deep and u >= 2:
                    pe.wait_ge(U.s_free, n - 1)
                if not deep and u >= 1:
                    pe.wait_ge(U.s_free, n)
                for h in range(2):
                    if mask is not None:
                        mm(ps[:, s + h, 0:CT * T], identb[:], mask, start=True, stop=False, skip_group_check=True)
                    for b in range(CB):
                        r, t = 64 * (b % 2), b // 2
                        last = mm(ps[r:r + 64, s + h, t * w:(t + 1) * w], lhs(h, b), rhs(h, b),
                                  start=mask is None, stop=True, skip_group_check=True)
                last.then_inc(U.s_done, 1)

            def turn(U, u, n, w):
                pe.wait_ge(U.p_ready, n + 1)
                if u >= 1:
                    pe.wait_ge(U.ot_ready, n)
                    pe.wait_ge(U.ot_ready2, n)
                mm(ps[:, 4, 0:1], identb[:], identb[:, 0:1], start=True, stop=True)
                for h in range(2):
                    if w == T:
                        for g in range(2):
                            last = pe.transpose(ps[:, 4 + h, g * P:(g + 1) * P], E64[:, u % 2, h, 2 * g:2 * g + 2, :].rearrange("p t k -> p (t k)"), ident[:])
                    else:
                        for t in range(CT):
                            last = pe.transpose(ps[0:w, 4 + h, t * P:(t + 1) * P], E[:, u % 2, h, t, 0:w], ident[:])
                last.then_inc(U.t_done, 1)

            def weigh(U, u, n, w, values=None):
                pe.wait_ge(U.pt_ready, n + 1)
                for b in range(CB):
                    t, j = b // 2, b % 2
                    o = ps[:, 4 + t % 2, :].rearrange("p (h m) -> p h m", h=2)[:, :, (t // 2 * 2 + j) * T:(t // 2 * 2 + j + 1) * T]
                    if w == T:
                        r = T * (t % 2)
                        pr = PT[r:r + T, 0:CN].rearrange("p (h m) -> p h m", h=2)[:, :, t // 2 * P + j * T:t // 2 * P + (j + 1) * T]
                        val = ctxN[r:r + T, t // 2 * 2 + j, :]
                    else:
                        pr = PT[0:w, :].rearrange("p (h m) -> p h m", h=2)[:, :, b * T:(b + 1) * T]
                        val = values(b)
                    last = mm(o, val, pr, start=True, stop=True, skip_group_check=True)
                last.then_inc(U.v_done, 1)

            def q_rms(n, k):
                pe.wait_ge(r_row, n + k * NC + 1)
                mm(ps[:, 4, 0:1], identb[:], identb[:, 0:1], start=True, stop=True)
                for t in range(CT):
                    last = pe.transpose(ps[:, 4, t * H:(t + 1) * H], rrow[:, t * P:(t + 1) * P], ident[0:H, 0:H])
                last.then_inc(r_T, 1)
                pe.wait_ge(r_rq, n + k * NC + 1)

            def project(U, L, c, u, n, wo):
                pe.wait_ge(U.ot_ready, n + 1)
                pe.wait_ge(U.ot_ready2, n + 1)
                if u == 0:
                    pe.wait_ge(y_read, c + L * NC + 1)
                for h in range(2):
                    for t in range(CT):
                        last = mm(Yp[:, t, :], OT[:, u % 2, h * CN + t * P:h * CN + (t + 1) * P], wo(2 * u + h),
                                  start=(u == 0 and h == 0 and t % 2 == 0), stop=(u == NU - 1 and h == 1),
                                  skip_group_check=True)
                last.then_inc(y_done if u == NU - 1 else U.o_done, 1)

            pe.wait_ge(const_v, 1)
            pe.wait_ge(const_g, 2)
            pe.wait_ge(d_const, N_CONST)
            pe.wait_ge(d_a0, 96)
            pe.wait_ge(a0_w, 1)
            transposes(0, 0)
            with pe.Fori(0, NC) as c:
                pe.wait_ge(xt_ready, c + 1)
                for i in range(3):
                    for k in range(KD):
                        w = a0q_w[:, k, i * P:(i + 1) * P] if i < 2 else a0k_w[:, k, :]
                        last = mm(bank((2, 0, 1)[i]), w, XT[:, k, :], start=k == 0, stop=k == 1)
                    last.then_inc(a0_mm, 1)
                for b in range(CB):
                    for j in range(2):
                        for k in range(KD):
                            last = mm(ps[64 * j:64 * j + 64, 4, b * 32 + 16 * j:b * 32 + 16 * j + 16],
                                      XT[:, k, b * T:(b + 1) * T], a0v_w[:, k, :], start=k == 0, stop=k == 1,
                                      skip_group_check=True)
                last.then_inc(a0_v, 1)

                def score0(u, n):
                    t, hf = u // 2, u % 2
                    if u == 0:
                        pe.wait_ge(a0_q, c * 2 + 2)
                        pe.wait_ge(a0_kbd, c * CB + CB)
                    if u >= 2:
                        pe.wait_ge(U0.sub, n - 1)
                    mm(bank(2 + u % 2), identb[:], causalb[:].rearrange("p h k -> p (h k)"), start=True, stop=False,
                       skip_group_check=True)
                    for j in range(2):
                        last = mm(ps[64 * j:64 * j + 64, 2 + u % 2, :], q0T[:, hf, t * P + 64 * j:t * P + 64 * j + 64],
                                  kbd[:, 2 * t + j, :], start=False, stop=True, skip_group_check=True)
                    last.then_inc(U0.s_done, 1)

                def turn0(u, n):
                    pe.wait_ge(U0.p_ready, n + 1)
                    for m in range(4):
                        last = pe.transpose(ps[:, 4, m * P:(m + 1) * P], e0[:, u % 2, m * P:(m + 1) * P], ident[:])
                    last.then_inc(U0.t_done, 1)

                def weigh0(u, n):
                    pe.wait_ge(U0.pt_ready, n + 1)
                    if u == 0:
                        pe.wait_ge(a0_vbd, c + 1)
                    for m in range(4):
                        for j in range(2):
                            last = mm(ps[32 * m:32 * m + 32, 5, j * T:(j + 1) * T], v0bd[:, 2 * (u // 2) + j, :],
                                      PT[:, m * P + j * T:m * P + (j + 1) * T], start=True, stop=True,
                                      skip_group_check=True)
                    last.then_inc(U0.v_done, 1)

                def project0(u, n):
                    t, hf = u // 2, u % 2
                    pe.wait_ge(U0.ot_ready, n + 1)
                    if u == 0:
                        pe.wait_ge(y_read, c + 1)
                    last = mm(Yp[:, t, :], OT[:, u % 2, 0:P], a0o_w[:, hf, :], start=(hf == 0 and t % 2 == 0),
                              stop=hf == 1, skip_group_check=True)
                    last.then_inc(y_done if u == NU - 1 else U0.o_done, 1)

                score0(0, c * NU)
                score0(1, c * NU + 1)
                pe.wait_ge(a0_vbd, c + 1)
                for u in range(NU):
                    n = c * NU + u
                    if u < NU - 2:
                        score0(u + 2, n + 2)
                    turn0(u, n)
                    if u == NU - 1:
                        transposes(0, c + 1)
                    if u >= 1:
                        project0(u - 1, n - 1)
                    weigh0(u, n)
                project0(NU - 1, c * NU + NU - 1)

            pe.wait_ge(d_x0o, 32)
            pe.wait_ge(xt_ready, NC + 1)
            for h in range(H):
                if h >= 2:
                    pe.wait_ge(fuse_cp, h - 1)
                mm(bank(h % 2, D), x0_vT[:, h, :], x0_o[:, h, :], start=True, stop=True).then_inc(fuse_mm, 1)
            pe.wait_ge(fuse_cp, H)
            pe.wait_ge(d_x0, 32)
            with pe.Fori(0, NC) as c:
                pe.wait_ge(xt_ready, c + NC + 1)
                pe.wait_ge(d_ctxT, c * 16 + 16)

                def q_sums(h):
                    pe.wait_ge(x_qsq, c * H + h + 1)
                    mm(ps[0:H, 4, :], onehot[:, h, :], SQ[:, h % 2, :], start=h == 0, stop=h == H - 1,
                       skip_group_check=True).then_inc(x_qsum, 1)

                def k_sums(h):
                    pe.wait_ge(x_ksq, c * H + h + 1)
                    if h >= 1:
                        pe.wait_ge(x_kln, c * H + h)
                    mm(bank(5), ones[:], KSQ[:, h % 2, :], start=True, stop=True).then_inc(x_ksum, 1)

                for h in range(H + 1):
                    if h < H:
                        if h >= 2:
                            pe.wait_ge(x_qcp, c * H + h - 1)
                            pe.wait_ge(x_qsq, c * H + h - 1)
                        for k in range(KD):
                            last = mm(bank(h % 2), xq_w[:, k, h * HD:(h + 1) * HD], XT[:, k, :], start=k == 0, stop=k == 1)
                        last.then_inc(x_qmm, 1)
                    if h >= 1:
                        k_sums(h - 1)
                    if h < H:
                        if h >= 2:
                            pe.wait_ge(x_krdy, c * H + h - 1)
                        mm(bank(2 + h % 2), xk_w[:, h * HD:(h + 1) * HD], ctxT[:], start=True, stop=True).then_inc(x_kmm, 1)
                    if h >= 1:
                        q_sums(h - 1)
                pe.wait_ge(x_qcp, c * H + H)
                transposes(1, c + 1)
                pe.wait_ge(x_krdy, c * H + H)

                def score1(u, n):
                    score(U1, u, n, lambda h, b: qT[:, 2 * u + h, b * T:(b + 1) * T],
                          lambda h, b: kT[:, 2 * u + h, b * T:(b + 1) * T], T, deep=True)

                score1(0, c * NU)
                q_rms(c, 0)
                pe.wait_ge(xt_ready, c + NC + 2)
                score1(1, c * NU + 1)
                for u in range(NU):
                    n = c * NU + u
                    if u < NU - 2:
                        score1(u + 2, n + 2)
                    turn(U1, u, n, T)
                    if u >= 1:
                        project(U1, 1, c, u - 1, n - 1, lambda h: xvo_w[:, h, :])
                    if u == 0:
                        pe.wait_ge(d_ctxN, c * 16 + 16)
                    weigh(U1, u, n, T)
                project(U1, 1, c, NU - 1, c * NU + NU - 1, lambda h: xvo_w[:, h, :])

            def ffn(i, L, sizes, wg, wu, wd):
                nj = len(sizes)

                def chunk(c, more):
                    pe.wait_ge(xt_ready, c + L * NC + 1)
                    for j in range(nj + 1):
                        if j == nj and more:
                            transposes(L, c + 1, 4)
                        if j < nj:
                            m = sizes[j]
                            if j >= 2:
                                pe.wait_ge(f_hid[i], c * nj + j - 1)
                            for s, w in ((0, wg), (2, wu)):
                                for k in range(KD):
                                    last = mm(ps[0:m, s + j % 2, :], w[:, k, j * P:j * P + m], XT[:, k, :],
                                              start=k == 0, stop=k == 1)
                            last.then_inc(f_mm[i], 1)
                        if j >= 1:
                            m = sizes[j - 1]
                            pe.wait_ge(f_hid[i], c * nj + j)
                            if j == 1:
                                pe.wait_ge(y_read, c + L * NC + 1)
                            for t in range(CT):
                                last = mm(Yp[:, t, :], hidT[0:m, (j - 1) % 2, t * P:(t + 1) * P], wd[0:m, j - 1, :],
                                          start=(j == 1 and t % 2 == 0), stop=j == nj, skip_group_check=True)
                            last.then_inc(y_done if j == nj else f_down[i], 1)

                whole = NC if L == 2 else NC - 1
                with pe.Fori(0, whole) as c:
                    chunk(c, True)
                if whole < NC:
                    chunk(NC - 1, False)

            pe.wait_ge(f0_cvt, 1)
            ffn(0, 2, [P] * FF0, f0g_w, f0u_w, f0d_w)

            pe.wait_ge(d_l1o, 32)
            for h in range(H):
                if h >= 2:
                    pe.wait_ge(fuse_cp, H + h - 1)
                for k in range(KD):
                    last = mm(bank(h % 2, D), g_wgT[:, 2 * (h // 4) + k, (h % 4) * P:(h % 4 + 1) * P],
                              g_wo[:, 2 * (h // 4) + k, :], start=k == 0, stop=k == 1)
                last.then_inc(fuse_mm, 1)
            pe.wait_ge(d_x1o, 16 * 6)
            for h in range(H):
                b = 2 * (h % 2)
                pe.wait_ge(fuse_cp, 2 * H if h < 2 else 2 * H + h - 1)
                for k in range(KD):
                    mm(ps[:, b, k * P:(k + 1) * P], x1_qT[:, h, k * P:(k + 1) * P], x1_kT[:, h // 2, :],
                       start=True, stop=True, skip_group_check=True)
                mm(ps[:, b + 1, 0:D], x1_vT[:, h // 2, :], x1_o(h), start=True, stop=True).then_inc(fuse_mm, 1)
            pe.wait_ge(fuse_cp, 3 * H)
            pe.wait_ge(d_l1, 16 * 5)
            with pe.Fori(0, NC) as c:
                pe.wait_ge(xt_ready, c + 3 * NC + 1)
                for k in range(KD):
                    last = mm(ps[0:64, 2, :], cq_w[:, k, :], XT[:, k, :], start=k == 0, stop=k == 1)
                last.then_inc(l_qcmm, 1)
                for k in range(KD):
                    last = mm(bank(0), k1_w[:, k, :], XT[:, k, :], start=k == 0, stop=k == 1)
                    if k == 1:
                        last.then_inc(l_kmm, 1)
                for b in range(CB):
                    for k in range(KD):
                        last = mm(ps[0:64, 4 + b // 4, (b % 4) * P:(b % 4 + 1) * P], XT[:, k, b * T:(b + 1) * T],
                                  v1_w[:, k, :], start=k == 0, stop=k == 1, skip_group_check=True)
                last.then_inc(l_vmm, 1)
                pe.wait_ge(l_ksq, c + 1)
                pe.wait_ge(l_qc, c + 1)
                mm(bank(2), ones[:], l1k[:, :], start=True, stop=True).then_inc(l_ksum, 1)
                for m in range(16):
                    for k in range(KD):
                        last = mm(ps[0:32, 3, 0:HD], XT[:, k, m:CN:16], comp_w[:, KD * m + k, :],
                                  start=(m == 0 and k == 0), stop=(m == 15 and k == 1))
                last.then_inc(l_ckmm, 1)
                pe.wait_ge(l_v, c + 1)
                pe.wait_ge(l_keys, 2 * c + 1)

                def qsums(h):
                    pe.wait_ge(l_qsq, c * H + h + 1)
                    mm(ps[0:H, 4, :], onehot[:, h, :], SQ[:, h % 2, :], start=h == 0, stop=h == H - 1,
                       skip_group_check=True).then_inc(l_qsum, 1)

                for h in range(H + 1):
                    if h < H:
                        if h == 2:
                            pe.wait_ge(l_ckv, c + 1)
                            mm(ps[:, 3, 0:1], ident[:], ones[:, 0:1], start=True, stop=True)
                            pe.transpose(ps[:, 3, 0:32], ckv[:], ident[0:32, 0:32]).then_inc(l_ckT, 1)
                        if h == 3:
                            pe.wait_ge(l_keys, 2 * c + 2)
                        if h >= 4:
                            pe.wait_ge(l_qhalf, c * H + h - 3)
                            pe.wait_ge(l_qrest, c * H + h - 3)
                        mm(bank(h % 4), up_w[0:64, h, :], qcT[0:64, :], start=True, stop=True).then_inc(l_qmm, 1)
                    if h >= 1:
                        qsums(h - 1)
                pe.wait_ge(l_qhalf, c * H + H - 2)
                pe.wait_ge(l_qrest, c * H + H - 2)
                transposes(3, c + 1)
                pe.wait_ge(l_qrdy, c * H + H)
                pe.wait_ge(l_qrest, c * H + H)

                def score3(u, n):
                    score(U3, u, n, lambda h, b: qT[:, 2 * u + h, b * T:(b + 1) * T], lambda h, b: keysT[:, b, :], W1, deep=True)

                score3(0, c * NU)
                q_rms(c, 1)
                pe.wait_ge(xt_ready, c + 3 * NC + 2)
                score3(1, c * NU + 1)
                for u in range(NU):
                    n = c * NU + u
                    if u < NU - 2:
                        score3(u + 2, n + 2)
                    turn(U3, u, n, W1)
                    if u >= 1:
                        project(U3, 3, c, u - 1, n - 1, lambda h: go_w[:, h, :])
                    if u == 0:
                        pe.wait_ge(d_ck, 16 * CB * c + 16 * CB)
                    weigh(U3, u, n, W1, lambda b: vals[0:W1, b, :])
                project(U3, 3, c, NU - 1, c * NU + NU - 1, lambda h: go_w[:, h, :])

            with pe.Fori(0, NC) as c:
                pe.wait_ge(xt_ready, c + 4 * NC + 1)
                pe.wait_ge(d_ctxT, c * 16 + 16 * NC + 16)
                pe.wait_ge(d_ctxN, c * 16 + 16 * NC + 16)

                def query(u, n):
                    if u >= 1:
                        pe.wait_ge(U4.q_ready, n)
                    for h in range(2):
                        for k in range(KD):
                            last = mm(bank(h), x1a_w[:, KD * (2 * u + h) + k, :], XT[:, k, :], start=k == 0, stop=k == 1)
                    last.then_inc(U4.q_mm, 1)

                query(0, c * NU)
                for u in range(NU + 2):
                    n = c * NU + u
                    if u < NU:
                        pe.wait_ge(U4.q_ready, n + 1)
                        score(U4, u, n, lambda h, b: q1T[:, u % 2, h * CN + b * T:h * CN + (b + 1) * T],
                              lambda h, b: ctxT[:, b * T:(b + 1) * T], T, mask=vmaskb[:, bass.ts(c, CT), :])
                    if 1 <= u <= NU:
                        turn(U4, u - 1, n - 1, T)
                    if u == NU:
                        transposes(4, c + 1)
                    if u < NU - 1:
                        query(u + 1, n + 1)
                    if 1 <= u <= NU:
                        weigh(U4, u - 1, n - 1, T)
                    if u >= 2:
                        project(U4, 4, c, u - 2, n - 2, lambda h: x1vo_w[:, h, :])

            pe.wait_ge(f1_cvt, 2)
            ffn(1, 5, FF1_SIZES, f1g_w, f1u_w, f1d_w)

        @block.scalar
        def _(act):
            act_ = act.activation

            def xt_copy(L, c, b=0):
                act.wait_ge(xt_psum, c + L * NC + 2)
                act_(XT[:], two(b), ACT.Copy).then_inc(xt_ready, 1)

            def ln_sqrt(L, c):
                act.wait_ge(ln_var, c + L * NC + 1)
                act_(std[:], mv[:, :, 1], ACT.Ln).then_inc(ln_log, 1)
                act.wait_ge(ln_log, c + L * NC + 1)
                act_(rstd[:], std[:], ACT.Exp, scale=-0.5).then_inc(ln_std, 1)

            def unit_copy(U, u, n, w):
                act.wait_ge(U.t_done, n + 1)
                if u >= 1:
                    act.wait_ge(U.v_done, n)
                if w == T:
                    act_(PT[:, 0:CN].rearrange("p (h m) -> p h m", h=2), ps[:, 4:6, 0:2 * P], ACT.Copy).then_inc(U.pt_ready, 1)
                else:
                    act_(PT[0:w, :].rearrange("p (h m) -> p h m", h=2), ps[0:w, 4:6, :], ACT.Copy).then_inc(U.pt_ready, 1)

            def out_copy(U, u, n, per):
                act.wait_ge(U.v_done, n + 1)
                if u >= 2:
                    act.wait_ge(U.o_done, per)
                dst = OT[:, u % 2, :].rearrange("p (h g q m) -> p q h g m", h=2, g=2, q=2)[:, 1]
                act_(dst, ps[:, 5, :].rearrange("p (h g m) -> p h g m", h=2, g=2), ACT.Copy).then_inc(U.ot_ready2, 1)

            def q_rms(n, k, scale, bias):
                act_(rrow[:], ps[0:H, 4, :], ACT.Ln, scale=scale, bias=bias).then_inc(r_ln, 1)
                act.wait_ge(r_ln, n + k * NC + 1)
                act_(rrow[:], rrow[:], ACT.Exp, scale=-0.5).then_inc(r_row, 1)

            act.wait_ge(const_v, 1)
            act.preload_act_table_set("natural_log_exp_and_others")
            xt_copy(0, 0)
            with act.Fori(0, NC) as c:
                for i in range(2):
                    act.wait_ge(a0_mm, c * 3 + i + 1)
                    act_(q0T[:, i, :], bank((2, 0)[i]), ACT.Copy).then_inc(a0_q, 1)
                for u in range(NU + 1):
                    n = c * NU + u
                    if u < NU:
                        act.wait_ge(U0.sub, n + 1)
                        act_(e0[:, u % 2, :], e0[:, u % 2, :], ACT.Exp, scale=0.25).then_inc(U0.exp, 1)
                    if u >= 1:
                        act.wait_ge(U0.t_done, n)
                        if u >= 2:
                            act.wait_ge(U0.v_done, n - 1)
                        act_(PT[:, 0:CN], bank(4), ACT.Copy).then_inc(U0.pt_ready, 1)
                xt_copy(0, c + 1)
                ln_sqrt(0, c)
            for h in range(H):
                act.wait_ge(fuse_mm, h + 1)
                act_(xvo_w[:, h, :], bank(h % 2, D), ACT.Copy).then_inc(fuse_cp, 1)
            with act.Fori(0, NC) as c:
                for h in range(H + 1):
                    if h < H:
                        act.wait_ge(x_qmm, c * H + h + 1)
                        if h >= 2:
                            act.wait_ge(x_qsum, c * H + h - 1)
                        act_(SQ[:, h % 2, :], bank(h % 2), ACT.Square).then_inc(x_qsq, 1)
                    if h >= 1:
                        act.wait_ge(x_ksum, c * H + h)
                        if h >= 2:
                            act.wait_ge(x_krs, c * H + h - 1)
                        act_(krms, bank(5), ACT.Ln, scale=1.0 / HD, bias=eps5[:, 0:1]).then_inc(x_kln, 1)
                        act.wait_ge(x_kln, c * H + h)
                        if h >= 2:
                            act.wait_ge(x_krdy, c * H + h - 1)
                        act_(krs, krms, ACT.Exp, scale=-0.5).then_inc(x_krs, 1)
                    if h < H:
                        act.wait_ge(x_kmm, c * H + h + 1)
                        if h >= 2:
                            act.wait_ge(x_ksum, c * H + h - 1)
                        act_(KSQ[:, h % 2, :], bank(2 + h % 2), ACT.Square).then_inc(x_ksq, 1)
                act.wait_ge(x_qsum, c * H + H)
                q_rms(c, 0, 1.0 / HD, eps5[0:H, 0:1])
                xt_copy(1, c + 1)
                for u in range(NU + 1):
                    n = c * NU + u
                    if u < NU:
                        act.wait_ge(U1.sub, n + 1)
                        act_(E64[:, u % 2], E64[:, u % 2], ACT.Exp, scale=HD ** -0.5).then_inc(U1.exp, 1)
                    if u >= 1:
                        unit_copy(U1, u - 1, n - 1, T)
                        out_copy(U1, u - 1, n - 1, c * (NU - 1) + u - 2)
                ln_sqrt(1, c)

            def ffn(i, L, sizes, sg):
                nj = len(sizes)

                def chunk(c, more):
                    for j, m in enumerate(sizes):
                        act.wait_ge(f_mm[i], c * nj + j + 1)
                        if j >= 2:
                            act.wait_ge(f_hid[i], c * nj + j - 1)
                        act_(silu_b[0:m, j % 2, :], ps[0:m, j % 2, :], ACT.Silu, scale=sg[0:m, j:j + 1]).then_inc(f_silu[i], 1)
                    if more:
                        xt_copy(L, c + 1, 4)
                    act.preload_act_table_set("natural_log_exp_and_others")
                    ln_sqrt(L, c)

                whole = NC if L == 2 else NC - 1
                with act.Fori(0, whole) as c:
                    chunk(c, True)
                if whole < NC:
                    chunk(NC - 1, False)

            ffn(0, 2, [P] * FF0, sg0)
            for h in range(H):
                act.wait_ge(fuse_mm, H + h + 1)
                act_(go_w[:, h, :], bank(h % 2, D), ACT.Copy).then_inc(fuse_cp, 1)
            for h in range(H):
                b = 2 * (h % 2)
                act.wait_ge(fuse_mm, 2 * H + h + 1)
                act_(x1a_w[:, KD * h:KD * h + KD, :], ps[:, b, 0:D].rearrange("p (k m) -> p k m", k=KD), ACT.Copy).then_inc(a_own, 1)
                act_(x1vo_w[:, h, :], ps[:, b + 1, 0:D], ACT.Copy).then_inc(fuse_cp, 1)
            act_(sinkexp[:], sinkexp[:], ACT.Exp).then_inc(const_a, 1)
            with act.Fori(0, NC) as c:
                act.wait_ge(l_qcmm, c + 1)
                act_(qcT[0:64, :], ps[0:64, 2, :], ACT.Copy).then_inc(l_qc, 1)
                act.wait_ge(l_kmm, c + 1)
                act_(l1k, bank(0), ACT.Square).then_inc(l_ksq, 1)
                act.wait_ge(l_ksum, c + 1)
                act_(l1k, bank(2), ACT.Ln, scale=1.0 / HD, bias=eps6[:, 0:1]).then_inc(l_kln, 1)
                act.wait_ge(l_kln, c + 1)
                act_(l1k, l1k, ACT.Exp, scale=-0.5).then_inc(l_krs, 1)
                act.wait_ge(l_ckmm, c + 1)
                act_(ckt[:], ps[0:32, 3, 0:HD], ACT.Square, accum_out=cks[:, 0:1]).then_inc(l_ckss, 1)
                act.wait_ge(l_ckss, c + 1)
                act_(cks[:, 1:2], cks[:, 0:1], ACT.Ln, scale=1.0 / HD, bias=eps6[0:32, 0:1]).then_inc(l_ckln, 1)
                act.wait_ge(l_ckln, c + 1)
                act_(cks[:, 2:3], cks[:, 1:2], ACT.Exp, scale=-0.5).then_inc(l_ckrs, 1)
                for h in range(H):
                    act.wait_ge(l_qmm, c * H + h + 1)
                    if h >= 2:
                        act.wait_ge(l_qsum, c * H + h - 1)
                    act_(SQ[:, h % 2, :], bank(h % 4), ACT.Square).then_inc(l_qsq, 1)
                    act_(qT[64:P, h, :], ps[64:P, h % 4, :], ACT.Copy).then_inc(l_qrest, 1)
                act.wait_ge(l_qsum, c * H + H)
                q_rms(c, 1, 1.0, eps6b[0:H, 0:1])
                xt_copy(3, c + 1)
                for u in range(NU + 1):
                    n = c * NU + u
                    if u < NU:
                        act.wait_ge(U3.s_free, n + 1)
                        act_(E[:, u % 2, :, :, 0:T], E[:, u % 2, :, :, 0:T], ACT.Tanh, scale=1.0 / 50.0).then_inc(U3.tanh, 1)
                        act.wait_ge(U3.tanh, n + 1)
                        for h in range(2):
                            act_(E[:, u % 2, h, :, 0:T], E[:, u % 2, h, :, 0:T], ACT.Exp, scale=50.0,
                                 bias=sinkneg[:, 2 * u + h:2 * u + h + 1]).then_inc(U3.exp, 1)
                        act.wait_ge(U3.sub, n + 1)
                        act_(cb[:], cb[:], ACT.Exp).then_inc(U3.cexp, 1)
                    if u == NU:
                        act.preload_act_table_set("natural_log_exp_and_others")
                    if u >= 1:
                        unit_copy(U3, u - 1, n - 1, W1)
                        out_copy(U3, u - 1, n - 1, c * (NU - 1) + u - 2)
                ln_sqrt(3, c)
            with act.Fori(0, NC) as c:
                def q_copy(u, n):
                    act.wait_ge(U4.q_mm, n + 1)
                    if u >= 2:
                        act.wait_ge(U4.s_done, n - 1)
                    act_(q1T[:, u % 2, :].rearrange("p (h m) -> p h m", h=2), two(0), ACT.Copy).then_inc(U4.q_ready, 1)

                q_copy(0, c * NU)
                for u in range(NU + 1):
                    n = c * NU + u
                    if u < NU:
                        act.wait_ge(U4.s_free, n + 1)
                        act_(E64[:, u % 2], E64[:, u % 2], ACT.Exp, scale=HD ** -0.5).then_inc(U4.exp, 1)
                    if u >= 1:
                        unit_copy(U4, u - 1, n - 1, T)
                    if u == NU:
                        xt_copy(4, c + 1)
                    if u < NU - 1:
                        q_copy(u + 1, n + 1)
                    if u >= 1:
                        out_copy(U4, u - 1, n - 1, c * (NU - 1) + u - 2)
                ln_sqrt(4, c)
            ffn(1, 5, FF1_SIZES, sg1)

        @block.vector
        def _(v):
            order = Order(v, v_own)
            tt, ts_, red = v.tensor_tensor, v.tensor_scalar, v.tensor_reduce

            def layer_norm(L, c, scale_row=None):
                v.wait_ge(y_done, c + L * NC + 1)
                if scale_row is None:
                    tt(Y[:], Yp, X[:, bass.ts(c, CT), :], ALU.add).then_inc(y_read, 1)
                else:
                    tt(Y[:], Yp, scale_row.unsqueeze(1).broadcast_to([P, CT, D]), ALU.mult).then_inc(y_read, 1)
                v.wait_ge(y_read, c + L * NC + 2)
                if scale_row is not None:
                    order.then(tt(Y[:], Y[:], X[:, bass.ts(c, CT), :], ALU.add))
                for t in range(CT):
                    order.then(v.bn_stats(bst[:, t, :], Y[:, t, :]))
                for t in range(CT):
                    v.tensor_copy(sm[:, 0:1], eps5[:])
                    order.then(v.bn_aggr(mv[:, t, :], bst[:, t, :]))
                ts_(mv[:, :, 1], mv[:, :, 1], LN_EPS, None, ALU.add).then_inc(ln_var, 1)
                v.wait_ge(ln_std, c + L * NC + 1)
                for t in range(CT):
                    ins = ts_(X[:, bass.ds(c * CT + t, 1), :].rearrange("p a d -> p (a d)"), Y[:, t, :], mv[:, t, 0:1], rstd[:, t:t + 1], ALU.subtract, ALU.mult)
                    if t < CT - 1:
                        order.then(ins)
                ins.then_inc(ln_done, 1)
                v.wait_ge(ln_done, c + L * NC + 1)

            LN_N = 4 + 4 + 3

            def bc(small, k=T, a_=2, b_=CT):
                return small.rearrange("p (a b) -> p a b", a=a_).unsqueeze(3).broadcast_to([P, a_, b_, k])

            def out_copy(U, u, n, per):
                v.wait_ge(U.v_done, n + 1)
                if u >= 2:
                    v.wait_ge(U.o_done, per)
                dst = OT[:, u % 2, :].rearrange("p (h g q m) -> p q h g m", h=2, g=2, q=2)[:, 0]
                v.tensor_copy(dst, ps[:, 4, :].rearrange("p (h g m) -> p h g m", h=2, g=2)).then_inc(U.ot_ready, 1)

            v.wait_ge(d_const, N_CONST)
            v.memset(eps5[:], 1e-5).then_inc(y_read, 1)
            order.then(v.memset(eps6[:], 1e-6))
            order.then(v.memset(eps6b[:], 1e-6 * HD))
            order.then(v.tensor_copy(identb[:], ident[:]))
            order.then(tt(gqk_c, gq_c, gk_c, ALU.mult))
            order.then(tt(qkw_c, qw_c, kw_c, ALU.mult))
            order.then(ts_(vmaskb[:], vmask8, -1.0, 1e30, ALU.add, ALU.mult))
            order.then(red(anykey[:], vmask8, AX.X, ALU.max))
            order.then(ts_(sinkneg[:], sinkB[:], 0.0, -1.0, ALU.max, ALU.mult))
            order.then(tt(sinkexp[:], sinkB[:], sinkneg[:], ALU.add))
            v.tensor_copy(causalb[:], causal[:].unsqueeze(1).broadcast_to([P, 8, T])).then_inc(const_v, 1)
            v.wait_ge(const_g, 2)

            v.wait_ge(d_a0, 96)
            for f in range(2):
                w = a0q_w[:, KD * f:KD * f + KD, :]
                order.then(tt(w, w, rot0[:, f, :].unsqueeze(1).broadcast_to([P, KD, D]), ALU.mult))
            tt(a0q_w[:, 0:KD, :], a0q_w[:, 0:KD, :], a0q_w[:, KD:2 * KD, :], ALU.add).then_inc(a0_w, 1)

            with v.Fori(0, NC) as c:
                order.enter(c, 1 + NU * 3 + LN_N)
                v.wait_ge(a0_mm, c * 3 + 3)
                v.tensor_copy(k0T, bank(1)).then_inc(a0_k, 1)
                v.wait_ge(a0_v, c + 1)
                for j in range(2):
                    cp = v.tensor_copy(v0bd[64 * j:64 * j + 64, :, 16 * j:16 * j + 16],
                                       ps[64 * j:64 * j + 64, 4, 0:CB * 32].rearrange("p (b n) -> p b n", n=32)[:, :, 16 * j:16 * j + 16])
                    if j == 0:
                        order.then(cp)
                cp.then_inc(a0_vbd, 1)
                def front0(u, n):
                    e = e0[:, u % 2, :].rearrange("p (h k) -> p h k", k=T)
                    s = bank(2 + u % 2).rearrange("p (h k) -> p h k", k=T)
                    v.wait_ge(U0.s_done, n + 1)
                    if u >= 1:
                        v.wait_ge(U0.sub, n)
                    order.then(red(mx[:], s, AX.X, ALU.max))
                    if u >= 2:
                        v.wait_ge(U0.t_done, n - 1)
                    tt(e, s, b8(mx[:]), ALU.subtract).then_inc(U0.sub, 1)

                b8 = lambda x: x.unsqueeze(2).broadcast_to([P, 8, T])
                front0(0, c * NU)
                for u in range(NU):
                    n = c * NU + u
                    if u < NU - 1:
                        front0(u + 1, n + 1)
                    e = e0[:, u % 2, :].rearrange("p (h k) -> p h k", k=T)
                    v.wait_ge(U0.exp, n + 1)
                    order.then(red(sm[:], e, AX.X, ALU.add))
                    order.then(v.reciprocal(rs[:], sm[:]))
                    tt(e, e, b8(rs[:]), ALU.mult).then_inc(U0.p_ready, 1)
                    if u >= 1:
                        v.wait_ge(U0.v_done, n)
                        if u >= 3:
                            v.wait_ge(U0.o_done, c * (NU - 1) + u - 2)
                        v.tensor_copy(OT[:, (u - 1) % 2, 0:P], ps[:, 5, 0:P]).then_inc(U0.ot_ready, 1)
                v.wait_ge(U0.v_done, c * NU + NU)
                v.wait_ge(U0.o_done, c * (NU - 1) + NU - 2)
                v.tensor_copy(OT[:, (NU - 1) % 2, 0:P], ps[:, 5, 0:P]).then_inc(U0.ot_ready, 1)
                layer_norm(0, c)
            order.leave(NC)

            def softmax_front(U, u, n, scale=None, deep=False):
                b = 2 - 2 * (u % 2) if deep else 2
                s = ps[:, b:b + 2, 0:CT * T].rearrange("p h (t k) -> p h t k", k=T)
                e = E64[:, u % 2]
                v.wait_ge(U.s_done, n + 1)
                order.then(red(mx[:].rearrange("p (h t) -> p h t", h=2), s, AX.X, ALU.max))
                if u >= 2:
                    v.wait_ge(U.t_done, n - 1)
                tt(e, s, bc(mx[:]), ALU.subtract).then_inc(U.s_free, 1)
                if scale is not None:
                    v.wait_ge(U.s_free, n + 1)
                    tt(e, e, scale, ALU.mult).then_inc(U.sub, 1)

            def softmax_back(U, u, n, any_=None):
                e = E64[:, u % 2]
                v.wait_ge(U.exp, n + 1)
                order.then(red(sm[:].rearrange("p (h t) -> p h t", h=2), e, AX.X, ALU.add))
                order.then(v.reciprocal(rs[:], sm[:]))
                if any_ is not None:
                    order.then(tt(rs[:].rearrange("p (h t) -> p h t", h=2), rs[:].rearrange("p (h t) -> p h t", h=2),
                                  any_, ALU.mult))
                tt(e, e, bc(rs[:]), ALU.mult).then_inc(U.p_ready, 1)

            def rq_copy(n, k):
                v.wait_ge(r_T, n + k * NC + 1)
                v.tensor_copy(rq[:].rearrange("p t h -> p (t h)"), ps[:, 4, 0:CT * H]).then_inc(r_rq, 1)
                v.wait_ge(r_rq, n + k * NC + 1)

            def rq_of(u, w):
                return rq[:, :, 2 * u:2 * u + 2].rearrange("p t h -> p h t").unsqueeze(3).broadcast_to([P, 2, CT, w])

            v.wait_ge(f0_cvt, 1)
            with v.Fori(0, NC) as c:
                order.enter(c, NU * 3 + LN_N)
                for h in range(H + 1):
                    if h < H:
                        v.wait_ge(x_qsq, c * H + h + 1)
                        v.tensor_copy(qT[:, h, :], bank(h % 2)).then_inc(x_qcp, 1)
                    if h >= 1:
                        v.wait_ge(x_krs, c * H + h)
                        v.scalar_tensor_tensor(out=kT[:, h - 1, :], in0=bank(2 + (h - 1) % 2), scalar=gqk_c, in1=krs,
                                               op0=ALU.mult, op1=ALU.mult).then_inc(x_krdy, 1)
                rq_copy(c, 0)
                for u in range(NU + 1):
                    n = c * NU + u
                    if u < NU:
                        softmax_front(U1, u, n, rq_of(u, T), deep=True)
                        softmax_back(U1, u, n)
                    if u >= 1:
                        out_copy(U1, u - 1, n - 1, c * (NU - 1) + u - 2)
                layer_norm(1, c)
            order.leave(NC)

            def ffn(i, L, sizes, su, row):
                nj = len(sizes)
                with v.Fori(0, NC) as c:
                    order.enter(c, 1 + LN_N)
                    for j, m in enumerate(sizes):
                        v.wait_ge(f_silu[i], c * nj + j + 1)
                        if j >= 2:
                            v.wait_ge(f_down[i], c * (nj - 1) + j - 1)
                        v.scalar_tensor_tensor(out=hidT[0:m, j % 2, :], in0=ps[0:m, 2 + j % 2, :], scalar=su[0:m, j:j + 1],
                                               in1=silu_b[0:m, j % 2, :], op0=ALU.mult, op1=ALU.mult).then_inc(f_hid[i], 1)
                    layer_norm(L, c, rowsB[:, i, :])
                order.leave(NC)

            ffn(0, 2, [P] * FF0, su0, 0)

            v.wait_ge(const_a, 1)
            with v.Fori(0, NC) as c:
                order.enter(c, 4 + NU * 12 + LN_N)
                cosb = cos1[:].unsqueeze(1).broadcast_to([64, CB, T])
                sinb = sin1[:].unsqueeze(1).broadcast_to([64, CB, T])
                r3 = lambda x: x.rearrange("p (b t) -> p b t", t=T)
                v.wait_ge(l_ksq, c + 1)
                order.then(tt(r3(l1t1[0:64, :]), r3(ps[0:64, 0, :]), cosb, ALU.mult))
                order.then(tt(r3(l1t2[0:32, :]), r3(ps[32:64, 0, :]), sinb[32:64], ALU.mult))
                order.then(tt(r3(l1t2[32:64, :]), r3(ps[0:32, 0, :]), sinb[0:32], ALU.mult))
                v.tensor_copy(l1t1[64:P, :], ps[64:P, 0, :])
                order.then(tt(l1t1[0:64, :], l1t1[0:64, :], l1t2[0:64, :], ALU.add))
                v.wait_ge(l_vmm, c + 1)
                v.tensor_copy(vals[0:T, :, :], ps[0:T, 4:6, :].rearrange("p q (b n) -> p (q b) n", n=HD)).then_inc(l_v, 1)
                v.wait_ge(l_krs, c + 1)
                v.scalar_tensor_tensor(out=keysT[:, :, 0:T], in0=r3(l1t1), scalar=qkw_c, in1=r3(l1k),
                                       op0=ALU.mult, op1=ALU.mult).then_inc(l_keys, 1)
                v.wait_ge(l_ckrs, c + 1)
                v.scalar_tensor_tensor(out=ckv[:], in0=ps[0:32, 3, 0:HD], scalar=cks[:, 2:3], in1=kwB[:],
                                       op0=ALU.mult, op1=ALU.mult).then_inc(l_ckv, 1)
                v.wait_ge(l_ckT, c + 1)
                ts_(keysT[:, :, T:W1], ps[:, 3, 0:32].rearrange("p (b n) -> p b n", n=NB), qw_c, None, ALU.mult).then_inc(l_keys, 1)
                for h in range(H):
                    if h >= 2:
                        v.wait_ge(l_qrdy, c * H + h - 1)
                    v.wait_ge(l_qsq, c * H + h + 1)
                    i = h % 4
                    tt(r3(qT[0:64, h, :]), r3(ps[0:64, i, :]), cosb, ALU.mult)
                    tt(r3(SQr[h % 2][0:32, :]), r3(ps[32:64, i, :]), sinb[32:64], ALU.mult)
                    tt(r3(SQr[h % 2][32:64, :]), r3(ps[0:32, i, :]), sinb[0:32], ALU.mult).then_inc(l_qhalf, 1)
                rq_copy(c, 1)
                for u in range(NU + 1):
                    n = c * NU + u
                    if u < NU:
                        s = ps[:, 2 - 2 * (u % 2):4 - 2 * (u % 2), 0:CT * W1].rearrange("p h (t k) -> p h t k", k=W1)
                        e, sw = E[:, u % 2], E[:, u % 2, :, :, 0:T]
                        v.wait_ge(U3.s_done, n + 1)
                        if u >= 2:
                            v.wait_ge(U3.t_done, n - 1)
                        tt(e, s, rq_of(u, W1), ALU.mult).then_inc(U3.s_free, 1)
                        v.wait_ge(U3.s_free, n + 1)
                        for h in range(2):
                            order.then(tt(cb[:, h, :, 0:NB], e[:, h, :, T:W1],
                                          blockmask[:].unsqueeze(1).broadcast_to([P, CT, NB]), ALU.add))
                        order.then(v.tensor_copy(cb[:, :, :, NB:NB + 1].rearrange("p h t k -> p h (t k)"),
                                                 sinkB[:, 2 * u:2 * u + 2].unsqueeze(2).broadcast_to([P, 2, CT])))
                        order.then(red(mx[:].rearrange("p (h t) -> p h t", h=2), cb[:], AX.X, ALU.max))
                        tt(cb[:], cb[:], bc(mx[:], NB + 1), ALU.subtract).then_inc(U3.sub, 1)
                        v.wait_ge(U3.exp, 2 * n + 2)
                        for h in range(2):
                            order.then(tt(sw[:, h], sw[:, h], keep[:].unsqueeze(1).broadcast_to([P, CT, T]), ALU.mult))
                        order.then(red(sm[:].rearrange("p (h t) -> p h t", h=2), sw, AX.X, ALU.add))
                        order.then(tt(sm[:].rearrange("p (h t) -> p h t", h=2), sm[:].rearrange("p (h t) -> p h t", h=2),
                                      sinkexp[:, 2 * u:2 * u + 2].unsqueeze(2).broadcast_to([P, 2, CT]), ALU.add))
                        order.then(v.reciprocal(rs[:], sm[:]))
                        order.then(tt(sw, sw, bc(rs[:]), ALU.mult))
                        v.wait_ge(U3.cexp, n + 1)
                        order.then(red(mx[:].rearrange("p (h t) -> p h t", h=2), cb[:], AX.X, ALU.add))
                        order.then(v.reciprocal(sm[:], mx[:]))
                        tt(e[:, :, :, T:W1], cb[:, :, :, 0:NB], bc(sm[:], NB), ALU.mult).then_inc(U3.p_ready, 1)
                    if u >= 1:
                        out_copy(U3, u - 1, n - 1, c * (NU - 1) + u - 2)
                layer_norm(3, c)
            order.leave(NC)

            with v.Fori(0, NC) as c:
                order.enter(c, NU * 4 + LN_N)
                for u in range(NU + 1):
                    n = c * NU + u
                    if u < NU:
                        softmax_front(U4, u, n)
                        softmax_back(U4, u, n, anykey[:, bass.ts(c, CT)].unsqueeze(1).broadcast_to([P, 2, CT]))
                    if u >= 1:
                        out_copy(U4, u - 1, n - 1, c * (NU - 1) + u - 2)
                layer_norm(4, c)
            order.leave(NC)
            ffn(1, 5, FF1_SIZES, su1, 1)


def tables():
    import numpy as np
    f = np.float32
    pos = np.arange(T, dtype=f)
    tok = np.arange(P) % T
    key = np.arange(T)
    seen = key[None, :] <= tok[:, None]
    th0 = (f(1.0) / f(10000.0) ** (np.arange(0, 8, 2, dtype=f) / f(8))).astype(f)
    fr0 = (np.arange(H, dtype=f)[:, None] * th0[None, :]).astype(f)
    part = np.arange(D) % 16
    sign0 = np.where(part % 8 < 4, f(-1), f(1))
    th1 = (f(1.0) / f(10000.0) ** (np.arange(0, 64, 2, dtype=f) / f(64))).astype(f)
    fr1 = (th1[:, None] * pos[None, :]).astype(f)
    sign1 = np.where(np.arange(64) < 32, f(1), f(-1))
    return {
        "c_ident": np.eye(P, dtype=f),
        "c_causal": np.where(seen, f(0), f(NEG)).astype(f),
        "c_keep": seen.astype(f),
        "c_blockmask": np.where(np.arange(NB)[None, :] * 16 + 15 < tok[:, None], f(0), f(NEG)).astype(f),
        "c_cos0": np.cos(fr0)[np.arange(D) // 16, part % 4].astype(f),
        "c_sin0": (np.sin(fr0)[np.arange(D) // 16, part % 4] * sign0).astype(f),
        "c_cos1": np.cos(fr1)[np.arange(64) % 32].astype(f),
        "c_sin1": (np.sin(fr1)[np.arange(64) % 32] * sign1[:, None]).astype(f),
        "c_onehot": np.eye(H, dtype=f).reshape(-1),
        "c_headmask": (np.arange(P)[:, None] // 16 == np.arange(8)[None, :]).astype(f),
    }


def layouts(i):
    import numpy as np
    g = {k: np.asarray(v) for k, v in i.items()}
    straight = np.array([0, 2, 4, 6, 1, 3, 5, 7, 8, 10, 12, 14, 9, 11, 13, 15])
    partner = np.array([1, 3, 5, 7, 0, 2, 4, 6, 9, 11, 13, 15, 8, 10, 12, 14])
    heads = 16 * np.arange(H)[:, None]
    qT, kT = g["L0_attn_Wq"].T, g["L0_attn_Wk"].T
    up = g["L1_attn_Wq_up"]
    col = lambda x: x.reshape(-1, 1)
    row = lambda x: x.reshape(-1)
    words = lambda x: np.ascontiguousarray(x).view(np.int32)
    arrays = {
        "x": g["x"].reshape(NT, P, D),
        "ctx": g["ctx_1024"].reshape(NC, 2, 2, 2, T, P).transpose(0, 2, 4, 1, 3, 5).reshape(NC, P, 4 * P),
        "ctxT": g["ctx_1024"].reshape(B * T, P).T,
        "mask": g["mask_BxS2_bf1"].view(np.uint8),
        "a0_q": np.concatenate([qT[:, (heads + straight).ravel()], qT[:, (heads + partner).ravel()]], 0),
        "a0_k": np.tile(kT[:, straight], (1, 8)),
        "a0_v": g["L0_attn_Wv"].T,
        "a0_o": g["L0_attn_Wo"].T,
        "x0_q": g["L0_xattn_Wq"], "x0_k": g["L0_xattn_Wk"],
        "x0_vT": g["L0_xattn_Wv"].T, "x0_o": g["L0_xattn_Wo"],
        "gq": col(g["L0_xattn_gq"]), "gk": col(g["L0_xattn_gk"]),
        "f0_g": words(g["L0_ffn_w_gate"]), "f0_u": words(g["L0_ffn_w_up"]), "f0_d": words(g["L0_ffn_w_down"]),
        "f0_sg": g["L0_ffn_s_gate"].reshape(FF0, P).T, "f0_su": g["L0_ffn_s_up"].reshape(FF0, P).T, "f0_sd": row(g["L0_ffn_s_down"]),
        "l1_qc": g["L1_attn_Wq_c"], "l1_up": up,
        "l1_k": g["L1_attn_Wk"], "l1_v": g["L1_attn_Wv"],
        "l1_comp": g["L1_attn_W_comp"],
        "qw": col(g["L1_attn_q_norm_w"]), "kw": col(g["L1_attn_k_norm_w"]), "kw_row": row(g["L1_attn_k_norm_w"]),
        "sink": row(g["L1_attn_sink"]),
        "l1_gT": g["L1_attn_Wg"].transpose(0, 2, 1).reshape(4 * D, 4 * HD), "l1_o": g["L1_attn_Wo"],
        "x1_qT": g["L1_xattn_Wq"].T, "x1_kT": g["L1_xattn_Wk"].T, "x1_vT": g["L1_xattn_Wv"].T, "x1_o": g["L1_xattn_Wo"],
        "f1_g": g["L1_ffn_wq_gate"].T, "f1_u": g["L1_ffn_wq_up"].T, "f1_d": g["L1_ffn_wq_down"].T,
        "f1_sg": g["L1_ffn_s_gate"][:640].reshape(5, P).T, "f1_sg_tail": col(g["L1_ffn_s_gate"][640:]),
        "f1_su": g["L1_ffn_s_up"][:640].reshape(5, P).T, "f1_su_tail": col(g["L1_ffn_s_up"][640:]), "f1_sd": row(g["L1_ffn_s_down"]),
        **tables(),
    }
    return {"in_" + k: np.ascontiguousarray(v) for k, v in arrays.items()}


def kernel(**inputs):
    import concourse.bacc as bacc
    from concourse.bass_utils import run_bass_kernel_spmd

    nc = bacc.Bacc("TRN2", target_bir_lowering=False, num_devices=1)
    arrays = layouts(inputs)
    aps = {k[3:]: nc.dram_tensor(k, v.shape, mybir.dt.from_np(v.dtype), kind="ExternalInput").ap() for k, v in arrays.items()}
    out = nc.dram_tensor("out", (NT, P, D), F32, kind="ExternalOutput").ap()
    build(nc, aps, out)
    r = run_bass_kernel_spmd(nc, [arrays], core_ids=[0])
    return r.results[0]["out"].reshape(B, T, D)
```

```python
from contextlib import ExitStack

import concourse.bass as bass
from concourse import mybir

F32 = mybir.dt.float32
BF16 = mybir.dt.bfloat16
F32R = mybir.dt.float32r
I32 = mybir.dt.int32
I8 = mybir.dt.int8
U8 = mybir.dt.uint8
ALU = mybir.AluOpType
ACT = mybir.ActivationFunctionType
AX = mybir.AxisListType

P = 128
B, T, D = 32, 64, 256
NT = B * T // P
NC = 4
CT = NT // NC
CN = CT * P
CB = CN // T
KD = D // P
H = 16
HD = 128
NU = H // 2
NB = 4
W1 = T + NB
NEG = -1e30
LN_EPS = 1e-5
FF0 = 1024 // P
FF1_SIZES = [128] * 5 + [64]
FF1N = 704


class Order:

    def __init__(self, eng, sem):
        self.eng, self.sem, self.base, self.n, self.it, self.per = eng, sem, 0, 0, None, 0

    def enter(self, it, per):
        self.it, self.per, self.n = it, per, 0

    def leave(self, trips):
        assert self.n == self.per, (self.n, self.per)
        self.base += trips * self.per
        self.it, self.n = None, 0

    def then(self, ins):
        ins.then_inc(self.sem, 1)
        if self.it is None:
            self.base += 1
            self.eng.wait_ge(self.sem, self.base)
        else:
            self.n += 1
            self.eng.wait_ge(self.sem, self.it * self.per + (self.base + self.n))


def build(nc, a, out):
    ctx = ExitStack()
    with ctx:
        def sb(name, shape, dt=F32):
            return ctx.enter_context(nc.sbuf_tensor(name, shape, dt))

        def sem(name):
            return ctx.enter_context(nc.semaphore(name))

        def overlay(name, n, *layouts):
            with nc.sbuf_tensor(name, [P, n], F32) as region:
                pass
            tensors = [region]
            for parts in layouts:
                with ExitStack() as scope:
                    tensors += [scope.enter_context(nc.sbuf_tensor(part, [P, m], F32R)) for part, m in parts]
                    if parts is layouts[-1]:
                        ctx.enter_context(scope.pop_all())
            return tensors

        X = sb("X", [P, NT, D])
        Xc = sb("Xc", [P, CT, D])
        XT = sb("XT", [P, KD, CN])
        ctxT = sb("ctxT", [P, CN])
        ctxN = sb("ctxN", [P, 4, P])
        R1, W1_hi, W1_lo, XT1_parts, _ = overlay(
            "R1", 12032, (("W1_hi", 4608), ("W1_lo", 4608), ("XT1_parts", 2048), ("R1_end", 768)))
        R2, XT_parts, _, W0 = overlay("R2", 8224, (("XT_parts", 2048), ("R2_gap", 32), ("W0", 6144)))
        WL, X1A_hi, X1A_lo, _, hid_parts, _ = overlay(
            "WL", 8192, (("X1A_hi", 4096), ("X1A_lo", 4096)), (("WL_low", 1024), ("hid_parts", 2048), ("WL_high", 5120)))
        WU = sb("WU", [P, 8192])
        Eflat = sb("E", [P, 2 * 2 * CT * W1])
        PT = sb("PT", [P, 2 * CN])
        OT = sb("OT", [P, 2, 2 * CN])
        Y = sb("Y", [P, CT, D])
        ident = sb("ident", [P, P])
        identb = sb("identb", [P, P], BF16)
        causal = sb("causal", [P, T])
        causalb = sb("causalb", [P, 8, T], BF16)
        keep = sb("keep", [P, T])
        blockmask = sb("blockmask", [P, NB])
        rot0 = sb("rot0", [P, 2, D])
        cos1 = sb("cos1", [64, T])
        sin1 = sb("sin1", [64, T])
        headmask = sb("headmask", [P, 8])
        ones = sb("ones", [P, P])
        pick = sb("pick", [P, H + P], F32R)
        onesr = sb("onesr", [P, P], F32R)
        onehot = sb("onehot", [P, H, H])
        vmaskb = sb("vmaskb", [P, NT, T], BF16)
        anykey = sb("anykey", [P, NT])
        cols = sb("cols", [P, 40])
        rowsB = sb("rowsB", [P, 2, D])
        kwB = sb("kwB", [32, HD])
        sinkB = sb("sinkB", [P, H])
        sinkneg = sb("sinkneg", [P, H])
        sinkexp = sb("sinkexp", [P, H])
        rrow = sb("rrow", [H, CN])
        rq = sb("rq", [P, CT, H])
        mx = sb("mx", [P, 8])
        sm = sb("sm", [P, 8])
        rs = sb("rs", [P, 8])
        cb = sb("cb", [P, 2, CT, NB + 1])
        bst = sb("bst", [P, CT, 6])
        mv = sb("mv", [P, CT, 2])
        std = sb("std", [P, CT])
        rstd = sb("rstd", [P, CT])
        ckv = sb("ckv", [32, HD])
        ckt = sb("ckt", [32, HD])
        cks = sb("cks", [32, 4])
        eps5, eps6, eps6b = sb("eps5", [P, 1]), sb("eps6", [P, 1]), sb("eps6b", [P, 1])
        ps = ctx.enter_context(nc.psum_tensor("ps", [P, 8, CN], F32))

        gq_c, gk_c, gqk_c = cols[:, 0:1], cols[:, 1:2], cols[:, 2:3]
        qw_c, kw_c, qkw_c = cols[:, 3:4], cols[:, 4:5], cols[:, 5:6]
        sg0, su0 = cols[:, 6:14], cols[:, 14:22]
        sg1, su1 = cols[:, 22:28], cols[:, 28:34]

        def view(region, at, *shape):
            n = 1
            for s in shape:
                n *= s
            v = region[:, at:at + n]
            if len(shape) == 2:
                v = v.rearrange("p (a b) -> p a b", b=shape[1])
            if len(shape) == 3:
                v = v.rearrange("p (a b c) -> p a b c", b=shape[1], c=shape[2])
            return v

        xq_w = view(R1, 0, KD, H * HD)
        xk_w = view(R1, 4096, H * HD)
        xvo_w = view(R1, 6144, H, D)
        cq_w = view(R1, 0, KD, 64)
        up_w = view(R1, 128, H, HD)
        k1_w = view(R1, 3200, KD, HD)
        v1_w = view(R1, 3584, KD, HD)
        comp_w = view(R1, 3840, 16 * KD, HD)
        go_w = view(R1, 7936, H, D)
        f1_w = [(view(w, 0, KD, 6 * P), view(w, 6 * P * KD, KD, 6 * P), view(w, 12 * P * KD, 6, D)) for w in (W1_hi, W1_lo)]
        a0q_w = view(R2, 0, 2 * KD, D)
        a0k_w = view(R2, 1024, KD, P)
        a0v_w = view(R2, 1536, KD, 16)
        a0o_w = view(R2, 1568, KD, D)
        f0g_w = view(W0, 0, KD, 1024)
        f0u_w = view(W0, 2048, KD, 1024)
        f0d_w = view(W0, 4096, FF0, D)
        xt_parts = [(view(x, 0, KD, CN), view(x, KD * CN, KD, CN)) for x in (XT_parts, XT1_parts)]
        SQ_hi, SQ_lo, KSQ_hi, KSQ_lo = (view(XT_parts, CN * j, CN) for j in range(4))
        x1a_w = view(R2, 0, H * KD, HD)
        x1vo_w = view(R2, 4096, H, D)
        x0_vT, x0_o = view(WU, 0, H, P), view(WU, 2048, H, D)
        g_wgT, g_wo = view(WU, 0, 8, CN), view(WU, 4096, 8, D)
        x1_qT, x1_kT, x1_vT = view(WL, 3072, H, D), view(WL, 7168, 8, P), view(WU, 7168, 8, P)

        def x1_o(h):
            if h < 8:
                return OT[:, h // 4, (h % 4) * D:(h % 4 + 1) * D]
            if h < 12:
                return PT[:, (h - 8) * D:(h - 7) * D]
            return Eflat[:, (h - 12) * D:(h - 11) * D]
        raw0 = view(WU, 6144, 1536).bitcast(I32)
        vmask8 = view(WU, 7680, 256).bitcast(U8).rearrange("p (t k) -> p t k", k=T)
        raw1 = view(WU, 2048, 4352).bitcast(I32)
        f1_f32, f1_f32_tail = view(R2, 0, 4096), view(WU, 6400, D)[0:64, :]
        x1a_parts = [view(w, 0, H * KD, HD) for w in (X1A_hi, X1A_lo)]
        q0T = view(WL, 0, 2, CN)
        k0T = view(WL, 1024, CN)
        v0bd = view(WL, 2560, CB, 32)
        kbd = view(WL, 3840, CB, 8 * T)
        qT = view(WL, 0, H, CN)
        kT = view(WU, 0, H, CN)
        krms, krs = PT[:, 0:CN], PT[:, CN:2 * CN]
        SQ, KSQ = (OT[:, j, :].rearrange("p (s m) -> p s m", s=2) for j in range(2))
        qcT = view(WU, 0, CN)
        keysT = view(WU, 512, CB, W1)
        E = Eflat[:].rearrange("p (r h t k) -> p r h t k", r=2, h=2, t=CT)
        E64 = Eflat[:, 0:4 * CT * T].rearrange("p (r h t k) -> p r h t k", r=2, h=2, t=CT)
        vals = view(WU, 1056, CB, HD)
        l1t1, l1t2, l1k = (view(WU, 2080 + CN * j, CN) for j in range(3))
        q1T = view(WU, 0, 2, 2 * CN)
        e0 = view(WL, 2816, 2, CN)
        SQr = [l1t1, l1t2]
        silu_b = view(WL, 0, 2, CN)
        hid_hi, hid_lo = view(hid_parts, 0, 2, CN), view(hid_parts, 1024, 2, CN)

        d_x, d_early, d_const, d_a0, d_x0, d_x0o, d_f0 = (sem(n) for n in ("d_x", "d_early", "d_const", "d_a0", "d_x0", "d_x0o", "d_f0"))
        d_l1, d_l1o, d_x1o, d_f1, d_ctxT, d_ctxN, d_ck, d_out = (
            sem(n) for n in ("d_l1", "d_l1o", "d_x1o", "d_f1", "d_ctxT", "d_ctxN", "d_ck", "d_out"))
        v_own, a_own, g_own = sem("v_own"), sem("a_own"), sem("g_own")
        const_v, const_g, const_a = sem("const_v"), sem("const_g"), sem("const_a")
        xc_ready, xt_psum, xt_ready = (sem(n) for n in ("xc_ready", "xt_psum", "xt_ready"))
        y_done, y_read, ln_var, ln_log, ln_std, ln_done = (sem(n) for n in ("y_done", "y_read", "ln_var", "ln_log", "ln_std", "ln_done"))
        fuse_mm, fuse_cp = sem("fuse_mm"), sem("fuse_cp")
        f0_cvt, f1_cvt = sem("f0_cvt"), sem("f1_cvt")
        x1a_cut = sem("x1a_cut")

        class Unit:

            def __init__(s, n, q=False, out2=True, sub=True, capped=False):
                s.s_done, s.s_free, s.exp = (sem(f"{n}_{w}") for w in ("s_done", "s_free", "exp"))
                s.p_ready, s.t_done, s.pt_ready, s.v_done, s.ot_ready, s.o_done = (
                    sem(f"{n}_{w}") for w in ("p_ready", "t_done", "pt_ready", "v_done", "ot_ready", "o_done"))
                if q:
                    s.q_mm, s.q_ready = sem(f"{n}_q_mm"), sem(f"{n}_q_ready")
                if out2:
                    s.ot_ready2 = sem(f"{n}_ot_ready2")
                if sub:
                    s.sub = sem(f"{n}_sub")
                if capped:
                    s.tanh, s.cexp = sem(f"{n}_tanh"), sem(f"{n}_cexp")

        U0, U1 = Unit("sa0", out2=False), Unit("xa0")
        U3, U4 = Unit("sa1", capped=True), Unit("xa1", q=True, sub=False)
        a0_w, a0_mm, a0_q, a0_k, a0_v, a0_vbd, a0_kbd = (
            sem(f"a0_{w}") for w in ("w", "mm", "q", "k", "v", "vbd", "kbd"))
        x_qhi, x_qlo, x_khi, x_klo = (sem(f"x_{w}") for w in ("qhi", "qlo", "khi", "klo"))
        x_qmm, x_kmm, x_qcp, x_ksum, x_kln, x_krs, x_krdy, x_qsum = (
            sem(f"x_{w}") for w in ("qmm", "kmm", "qcp", "ksum", "kln", "krs", "krdy", "qsum"))
        r_ln, r_row, r_T, r_rq = (sem(f"r_{w}") for w in ("ln", "row", "T", "rq"))
        (l_qcmm, l_qc, l_kmm, l_vmm, l_ckmm, l_ksq, l_ksum, l_kln, l_krs, l_keys, l_v, l_ckss, l_ckln, l_ckrs, l_ckv,
         l_ckT, l_qmm, l_qsq, l_qrest, l_qhalf, l_qrdy, l_qsum) = (
            sem(f"l_{w}") for w in ("qcmm", "qc", "kmm", "vmm", "ckmm", "ksq", "ksum", "kln", "krs", "keys", "v",
                                    "ckss", "ckln", "ckrs", "ckv", "ckT", "qmm", "qsq", "qrest", "qhalf", "qrdy",
                                    "qsum"))
        f_mm = [sem("f0_mm"), sem("f1_mm")]
        f_silu = [sem("f0_silu"), sem("f1_silu")]
        f_hid = [sem("f0_hid"), sem("f1_hid")]
        f_down = [sem("f0_down"), sem("f1_down")]
        x_hi, x_lo, h_hi, h_lo = ([sem(f"{n}0"), sem(f"{n}1")] for n in ("x_hi", "x_lo", "h_hi", "h_lo"))

        def bank(i, n=CN):
            return ps[:, i, 0:n]

        def two(i):
            return ps[:, i:i + 2, :]

        Yp = ps[:, 6:8, :].rearrange("p a (b n) -> p (a b) n", n=D)

        block = ctx.enter_context(nc.Block())

        @block.sync
        def _(sp):
            def load(dst, src, s):
                sp.dma_start(dst, src).then_inc(s, 16)

            load(X[:, 0:CT, :], a["x"][0:CT].rearrange("t p d -> p t d"), d_x)
            load(ident[:], a["c_ident"], d_early)
            load(a0q_w, a["a0_q"].rearrange("(f p) n -> p f n", p=P), d_a0)
            load(a0k_w, a["a0_k"].rearrange("(f p) n -> p f n", p=P), d_a0)
            load(rot0[:, 0, :], a["c_cos0"].partition_broadcast(P), d_a0)
            load(rot0[:, 1, :], a["c_sin0"].partition_broadcast(P), d_a0)
            load(a0v_w, a["a0_v"].rearrange("(f p) n -> p f n", p=P), d_a0)
            load(a0o_w, a["a0_o"].rearrange("(f p) n -> p f n", p=P), d_a0)
            load(causal[:], a["c_causal"], d_early)
            load(headmask[:], a["c_headmask"], d_early)
            load(X[:, CT:NT, :], a["x"][CT:NT].rearrange("t p d -> p t d"), d_x)
            for dst, name in ((keep[:], "c_keep"), (blockmask[:], "c_blockmask"), (cos1[:], "c_cos1"), (sin1[:], "c_sin1")):
                load(dst, a[name], d_const)
            for i, name in enumerate(("gq", "gk", None, "qw", "kw")):
                if name:
                    load(cols[:, i:i + 1], a[name], d_const)
            load(sg0, a["f0_sg"], d_const)
            load(su0, a["f0_su"], d_const)
            for dst, name in ((sg1, "f1_sg"), (su1, "f1_su")):
                load(dst[:, 0:5], a[name], d_const)
                load(dst[0:64, 5:6], a[name + "_tail"], d_const)
            load(rowsB[:, 0, :], a["f0_sd"].partition_broadcast(P), d_const)
            load(rowsB[:, 1, :], a["f1_sd"].partition_broadcast(P), d_const)
            load(onehot[:].rearrange("p h g -> p (h g)"), a["c_onehot"].partition_broadcast(P), d_const)
            load(kwB[:], a["kw_row"].partition_broadcast(32), d_const)
            load(sinkB[:], a["sink"].partition_broadcast(P), d_const)
            mk = a["mask"].rearrange("(t two) k -> two t k", two=2)
            for j in range(2):
                load(vmask8[64 * j:64 * j + 64, :, :], mk[j].partition_broadcast(64), d_const)
            load(raw0[:, 0:512].rearrange("p (k n) -> p k n", n=256), a["f0_g"].rearrange("(k p) n -> p k n", p=P), d_f0)
            load(raw0[:, 512:1024].rearrange("p (k n) -> p k n", n=256), a["f0_u"].rearrange("(k p) n -> p k n", p=P), d_f0)
            load(raw0[:, 1024:1536].rearrange("p (j n) -> p j n", n=64), a["f0_d"].rearrange("(j p) n -> p j n", p=P), d_f0)
            load(x0_vT, a["x0_vT"].rearrange("(h p) c -> p h c", p=P), d_x0o)
            load(x0_o, a["x0_o"].rearrange("(h p) n -> p h n", p=P), d_x0o)
            load(xq_w, a["x0_q"].rearrange("(k p) n -> p k n", p=P), d_x0)
            load(xk_w, a["x0_k"], d_x0)

            def load_ctxT(c):
                sp.dma_start(ctxT[:], a["ctxT"][:, bass.ts(c, CN)]).then_inc(d_ctxT, 16)

            def load_ctxN(c):
                sp.dma_start(ctxN[:], a["ctx"][bass.ds(c, 1)].rearrange("a p (g n) -> p (a g) n", n=P)).then_inc(d_ctxN, 16)

            load_ctxT(0)
            load_ctxN(0)
            with sp.Fori(1, NC) as c:
                sp.wait_ge(x_kmm, c * H)
                load_ctxT(c)
                sp.wait_ge(y_done, c + NC)
                load_ctxN(c)
            sp.wait_ge(y_done, 2 * NC)
            load(cq_w, a["l1_qc"].rearrange("(k p) n -> p k n", p=P), d_l1)
            load(up_w[0:64], a["l1_up"].rearrange("p (h n) -> p h n", n=HD), d_l1)
            load(k1_w, a["l1_k"].rearrange("(k p) n -> p k n", p=P), d_l1)
            load(v1_w, a["l1_v"].rearrange("(k p) n -> p k n", p=P), d_l1)
            load(comp_w, a["l1_comp"].rearrange("(m p) n -> p m n", p=P), d_l1)
            load(g_wgT, a["l1_gT"].rearrange("(m p) n -> p m n", p=P), d_l1o)
            load(g_wo, a["l1_o"].rearrange("(m p) n -> p m n", p=P), d_l1o)
            load(x1_qT, a["x1_qT"].rearrange("(h p) n -> p h n", p=P), d_x1o)
            load(x1_kT, a["x1_kT"].rearrange("(h p) n -> p h n", p=P), d_x1o)
            load(x1_vT, a["x1_vT"].rearrange("(h p) n -> p h n", p=P), d_x1o)
            x1_o_raw = a["x1_o"].rearrange("(h p) n -> p h n", p=P)
            load(OT[:].rearrange("p s (h n) -> p (s h) n", n=D), x1_o_raw[:, 0:8, :], d_x1o)
            load(PT[:].rearrange("p (h n) -> p h n", n=D), x1_o_raw[:, 8:12, :], d_x1o)
            load(Eflat[:, 0:4 * D].rearrange("p (h n) -> p h n", n=D), x1_o_raw[:, 12:16, :], d_x1o)
            load_ctxT(0)
            load_ctxN(0)
            with sp.Fori(0, NC) as c:
                sp.wait_ge(l_ckv, c + 1)
                for b in range(CB):
                    sp.dma_start(vals[T:W1, b, :], ckv[NB * b:NB * b + NB, :]).then_inc(d_ck, 16)
            sp.wait_ge(y_done, 4 * NC)
            load(raw1[:, 0:1408].rearrange("p (k n) -> p k n", n=FF1N), a["f1_g"].rearrange("(k p) n -> p k n", p=P), d_f1)
            load(raw1[:, 1408:2816].rearrange("p (k n) -> p k n", n=FF1N), a["f1_u"].rearrange("(k p) n -> p k n", p=P), d_f1)
            load(raw1[:, 2816:4096].rearrange("p (j n) -> p j n", n=D),
                 a["f1_d"][0:640].rearrange("(j p) n -> p j n", p=P), d_f1)
            load(raw1[0:64, 4096:4352], a["f1_d"][640:704], d_f1)
            with sp.Fori(1, NC) as c:
                sp.wait_ge(U4.s_done, c * NU)
                load_ctxT(c)
                sp.wait_ge(y_done, c + 4 * NC)
                load_ctxN(c)
            with sp.Fori(0, NC) as c:
                sp.wait_ge(ln_done, c + 5 * NC + 1)
                sp.dma_start(out[bass.ts(c, CT)].rearrange("t p d -> p t d"), X[:, bass.ts(c, CT), :]).then_inc(d_out, 16)
            sp.wait_ge(d_out, 16 * NC)

        N_CONST = 16 * (1 + 4 + 4 + 2 + 4 + 2 + 1 + 1 + 2)

        @block.gpsimd
        def _(g):
            order = Order(g, g_own)

            def fetch(L, c):
                if L == 0:
                    g.wait_ge(d_x, 32)
                else:
                    g.wait_ge(ln_done, c + (L - 1) * NC + 1)
                g.wait_ge(xt_psum, c + L * NC + 1)
                g.tensor_copy(Xc[:], X[:, bass.ts(c, CT), :]).then_inc(xc_ready, 1)

            def first_x_low(i):
                hi, lo = xt_parts[i]
                g.wait_ge(x_hi[i], 1)
                g.tensor_tensor(lo, XT[:], hi.bitcast(F32), ALU.subtract).then_inc(x_lo[i], 1)

            g.memset(ones[:], 1.0).then_inc(const_g, 1)
            g.memset(v0bd, 0.0).then_inc(const_g, 1)
            g.wait_ge(const_g, 2)
            g.sem_inc(xt_psum, 1)
            g.sem_inc(xc_ready, 1)

            def spread_keys(c):
                g.wait_ge(a0_k, c + 1)
                for b in range(CB):
                    g.tensor_tensor(kbd[:, b, :].rearrange("p (h k) -> p h k", k=T),
                                    k0T[:, b * T:(b + 1) * T].unsqueeze(1).broadcast_to([P, 8, T]),
                                    headmask[:].unsqueeze(2).broadcast_to([P, 8, T]), ALU.mult).then_inc(a0_kbd, 1)

            g.wait_ge(d_early, 48)
            spread_keys(0)
            with g.Fori(1, NC) as c:
                fetch(0, c)
                spread_keys(c)
            fetch(1, 0)
            g.wait_ge(d_f0, 48)
            g.tensor_copy(W0[:], raw0.bitcast(I8)).then_inc(f0_cvt, 1)
            with g.Fori(1, NC) as c:
                fetch(1, c)
            fetch(2, 0)
            first_x_low(0)
            with g.Fori(1, NC) as c:
                fetch(2, c)
            fetch(3, 0)

            def rotary_sums(c):
                for h in range(H):
                    g.wait_ge(l_qhalf, c * H + h + 1)
                    g.tensor_tensor(qT[0:64, h, :], qT[0:64, h, :], SQr[h % 2][0:64, :], ALU.add).then_inc(l_qrdy, 1)

            with g.Fori(0, NC - 1) as c:
                fetch(3, c + 1)
                rotary_sums(c)
            fetch(4, 0)
            rotary_sums(NC - 1)
            g.wait_ge(U3.s_done, NC * NU)
            for u in range(NU):
                pair = slice(2 * KD * u, 2 * KD * (u + 1))
                g.tensor_copy(x1a_parts[0][:, pair, :], x1a_w[:, pair, :]).then_inc(x1a_cut, 1)
                g.wait_ge(x1a_cut, 2 * u + 1)
                g.tensor_tensor(x1a_parts[1][:, pair, :], x1a_w[:, pair, :], x1a_parts[0][:, pair, :].bitcast(F32),
                                ALU.subtract).then_inc(x1a_cut, 1)
                if u == NU - 3:
                    first_x_low(1)
            g.wait_ge(x1a_cut, 2 * NU)
            g.wait_ge(y_done, 4 * NC)
            g.wait_ge(d_f1, 64)
            g.tensor_scalar(f1_f32[:, 0:4096], raw1[:, 0:4096], -128.0, None, ALU.add).then_inc(f1_cvt, 1)
            g.tensor_scalar(f1_f32_tail, raw1[0:64, 4096:4352], -128.0, None, ALU.add).then_inc(f1_cvt, 1)
            g.wait_ge(f1_cvt, 2)
            gate, up = (f1_f32[:, 1408 * j:1408 * (j + 1)].rearrange("p (k n) -> p k n", n=FF1N) for j in range(2))
            down = f1_f32[:, 2816:4096].rearrange("p (j n) -> p j n", n=D)
            (gate_hi, up_hi, down_hi), (gate_lo, up_lo, down_lo) = f1_w
            g.tensor_copy(gate_hi[:, :, 0:FF1N], gate).then_inc(f1_cvt, 1)
            g.tensor_copy(up_hi[:, :, 0:FF1N], up).then_inc(f1_cvt, 1)
            g.tensor_copy(down_hi[:, 0:5, :], down).then_inc(f1_cvt, 1)
            g.tensor_copy(down_hi[0:64, 5, :], f1_f32_tail).then_inc(f1_cvt, 1)
            g.wait_ge(f1_cvt, 6)
            g.tensor_tensor(gate_lo[:, :, 0:FF1N], gate, gate_hi[:, :, 0:FF1N].bitcast(F32), ALU.subtract).then_inc(f1_cvt, 1)
            g.tensor_tensor(up_lo[:, :, 0:FF1N], up, up_hi[:, :, 0:FF1N].bitcast(F32), ALU.subtract).then_inc(f1_cvt, 1)
            g.tensor_tensor(down_lo[:, 0:5, :], down, down_hi[:, 0:5, :].bitcast(F32), ALU.subtract).then_inc(f1_cvt, 1)
            g.tensor_tensor(down_lo[0:64, 5, :], f1_f32_tail, down_hi[0:64, 5, :].bitcast(F32), ALU.subtract).then_inc(f1_cvt, 1)
            for w in f1_w:
                for i in range(2):
                    g.tensor_scalar(w[i][:, :, FF1N:6 * P], ones[:].rearrange("p (k n) -> p k n", k=KD), 0.0, None,
                                    ALU.mult).then_inc(f1_cvt, 1)
            with g.Fori(1, NC) as c:
                fetch(4, c)
            fetch(5, 0)
            with g.Fori(1, NC) as c:
                fetch(5, c)

        @block.tensor
        def _(pe):
            mm = pe.matmul

            def transposes(L, c, b=0):
                pe.wait_ge(xc_ready, c + L * NC + 1)
                for k in range(KD):
                    for t in range(CT):
                        last = pe.transpose(ps[:, b + k, t * P:(t + 1) * P], Xc[:, t, k * P:(k + 1) * P], ident[:])
                last.then_inc(xt_psum, 1)

            def score(U, u, n, lhs, rhs, w, mask=None, deep=False):
                s = 2 * (u % 2) if deep else 2
                if deep and u >= 2:
                    pe.wait_ge(U.s_free, n - 1)
                if not deep and u >= 1:
                    pe.wait_ge(U.s_free, n)
                for h in range(2):
                    if mask is not None:
                        mm(ps[:, s + h, 0:CT * T], identb[:], mask, start=True, stop=False, skip_group_check=True)
                    for b in range(CB):
                        r, t = 64 * (b % 2), b // 2
                        last = mm(ps[r:r + 64, s + h, t * w:(t + 1) * w], lhs(h, b), rhs(h, b),
                                  start=mask is None, stop=True, skip_group_check=True)
                last.then_inc(U.s_done, 1)

            def turn(U, u, n, w):
                pe.wait_ge(U.p_ready, n + 1)
                if u >= 1:
                    pe.wait_ge(U.ot_ready, n)
                    pe.wait_ge(U.ot_ready2, n)
                mm(ps[:, 4, 0:1], identb[:], identb[:, 0:1], start=True, stop=True)
                for h in range(2):
                    if w == T:
                        for g in range(2):
                            last = pe.transpose(ps[:, 4 + h, g * P:(g + 1) * P], E64[:, u % 2, h, 2 * g:2 * g + 2, :].rearrange("p t k -> p (t k)"), ident[:])
                    else:
                        for t in range(CT):
                            last = pe.transpose(ps[0:w, 4 + h, t * P:(t + 1) * P], E[:, u % 2, h, t, 0:w], ident[:])
                last.then_inc(U.t_done, 1)

            def weigh(U, u, n, w, values=None):
                pe.wait_ge(U.pt_ready, n + 1)
                for b in range(CB):
                    t, j = b // 2, b % 2
                    o = ps[:, 4 + t % 2, :].rearrange("p (h m) -> p h m", h=2)[:, :, (t // 2 * 2 + j) * T:(t // 2 * 2 + j + 1) * T]
                    if w == T:
                        r = T * (t % 2)
                        pr = PT[r:r + T, 0:CN].rearrange("p (h m) -> p h m", h=2)[:, :, t // 2 * P + j * T:t // 2 * P + (j + 1) * T]
                        val = ctxN[r:r + T, t // 2 * 2 + j, :]
                    else:
                        pr = PT[0:w, :].rearrange("p (h m) -> p h m", h=2)[:, :, b * T:(b + 1) * T]
                        val = values(b)
                    last = mm(o, val, pr, start=True, stop=True, skip_group_check=True)
                last.then_inc(U.v_done, 1)

            def q_rms(n, k):
                pe.wait_ge(r_row, n + k * NC + 1)
                mm(ps[:, 4, 0:1], identb[:], identb[:, 0:1], start=True, stop=True)
                for t in range(CT):
                    last = pe.transpose(ps[:, 4, t * H:(t + 1) * H], rrow[:, t * P:(t + 1) * P], ident[0:H, 0:H])
                last.then_inc(r_T, 1)
                pe.wait_ge(r_rq, n + k * NC + 1)

            def project(U, L, c, u, n, wo, heads=(0, 1)):
                pe.wait_ge(U.ot_ready, n + 1)
                pe.wait_ge(U.ot_ready2, n + 1)
                if u == 0 and heads[0] == 0:
                    pe.wait_ge(y_read, c + L * NC + 1)
                for h in heads:
                    for t in range(CT):
                        last = mm(Yp[:, t, :], OT[:, u % 2, h * CN + t * P:h * CN + (t + 1) * P], wo(2 * u + h),
                                  start=(u == 0 and h == 0 and t % 2 == 0), stop=(u == NU - 1 and h == 1),
                                  skip_group_check=True)
                if heads[-1] == 1:
                    last.then_inc(y_done if u == NU - 1 else U.o_done, 1)

            pe.wait_ge(d_x, 16)
            pe.wait_ge(d_early, 48)
            for k in range(KD):
                for t in range(CT):
                    last = pe.transpose(ps[:, k, t * P:(t + 1) * P], X[:, t, k * P:(k + 1) * P], ident[:])
            last.then_inc(xt_psum, 1)
            pe.wait_ge(const_v, 1)
            pe.wait_ge(const_g, 2)
            pe.wait_ge(d_a0, 96)
            pe.wait_ge(a0_w, 1)
            with pe.Fori(0, NC) as c:
                pe.wait_ge(xt_ready, c + 1)
                for i in (2, 0, 1):
                    for k in range(KD):
                        w = a0q_w[:, k, i * P:(i + 1) * P] if i < 2 else a0k_w[:, k, :]
                        last = mm(bank((2, 0, 1)[i]), w, XT[:, k, :], start=k == 0, stop=k == 1)
                    last.then_inc(a0_mm, 1)
                for b in range(CB):
                    for j in range(2):
                        for k in range(KD):
                            last = mm(ps[64 * j:64 * j + 64, 4, b * 32 + 16 * j:b * 32 + 16 * j + 16],
                                      XT[:, k, b * T:(b + 1) * T], a0v_w[:, k, :], start=k == 0, stop=k == 1,
                                      skip_group_check=True)
                last.then_inc(a0_v, 1)

                def score0(u, n):
                    t, hf = u // 2, u % 2
                    if u == 0:
                        pe.wait_ge(a0_q, c * 2 + 2)
                    if hf == 0:
                        pe.wait_ge(a0_kbd, c * CB + 2 * t + 2)
                    if u >= 2:
                        pe.wait_ge(U0.sub, n - 1)
                    mm(bank(2 + u % 2), identb[:], causalb[:].rearrange("p h k -> p (h k)"), start=True, stop=False,
                       skip_group_check=True)
                    for j in range(2):
                        last = mm(ps[64 * j:64 * j + 64, 2 + u % 2, :], q0T[:, hf, t * P + 64 * j:t * P + 64 * j + 64],
                                  kbd[:, 2 * t + j, :], start=False, stop=True, skip_group_check=True)
                    last.then_inc(U0.s_done, 1)

                def turn0(u, n):
                    pe.wait_ge(U0.p_ready, n + 1)
                    for m in range(4):
                        last = pe.transpose(ps[:, 4, m * P:(m + 1) * P], e0[:, u % 2, m * P:(m + 1) * P], ident[:])
                    last.then_inc(U0.t_done, 1)

                def weigh0(u, n):
                    pe.wait_ge(U0.pt_ready, n + 1)
                    if u == 0:
                        pe.wait_ge(a0_vbd, c + 1)
                    for m in range(4):
                        for j in range(2):
                            last = mm(ps[32 * m:32 * m + 32, 5, j * T:(j + 1) * T], v0bd[:, 2 * (u // 2) + j, :],
                                      PT[:, m * P + j * T:m * P + (j + 1) * T], start=True, stop=True,
                                      skip_group_check=True)
                    last.then_inc(U0.v_done, 1)

                def project0(u, n):
                    t, hf = u // 2, u % 2
                    pe.wait_ge(U0.ot_ready, n + 1)
                    if u == 0:
                        pe.wait_ge(y_read, c + 1)
                    last = mm(Yp[:, t, :], OT[:, u % 2, 0:P], a0o_w[:, hf, :], start=(hf == 0 and t % 2 == 0),
                              stop=hf == 1, skip_group_check=True)
                    last.then_inc(y_done if u == NU - 1 else U0.o_done, 1)

                score0(0, c * NU)
                score0(1, c * NU + 1)
                pe.wait_ge(a0_vbd, c + 1)
                for u in range(NU):
                    n = c * NU + u
                    if u < NU - 2:
                        score0(u + 2, n + 2)
                    turn0(u, n)
                    if u == NU - 1:
                        transposes(0, c + 1)
                    if u >= 1:
                        project0(u - 1, n - 1)
                    weigh0(u, n)
                project0(NU - 1, c * NU + NU - 1)

            pe.wait_ge(d_x0o, 32)
            pe.wait_ge(xt_ready, NC + 1)
            for h in range(H):
                if h >= 2:
                    pe.wait_ge(fuse_cp, h - 1)
                mm(bank(h % 2, D), x0_vT[:, h, :], x0_o[:, h, :], start=True, stop=True).then_inc(fuse_mm, 1)
            pe.wait_ge(fuse_cp, H)
            pe.wait_ge(d_x0, 32)
            with pe.Fori(0, NC) as c:
                pe.wait_ge(xt_ready, c + NC + 1)

                def q_sums(h):
                    pe.wait_ge(x_qhi, c * H + h + 1)
                    mm(bank(4), pick[:, H - 1 - h:H - 1 - h + P], SQ_hi, start=h == 0, stop=False, skip_group_check=True)
                    pe.wait_ge(x_qlo, c * H + h + 1)
                    mm(bank(4), pick[:, H - 1 - h:H - 1 - h + P], SQ_lo, start=False, stop=h == H - 1,
                       skip_group_check=True).then_inc(x_qsum, 1)

                def k_sums(h):
                    if h >= 1:
                        pe.wait_ge(x_kln, c * H + h)
                    pe.wait_ge(x_khi, c * H + h + 1)
                    mm(bank(5), onesr[:], KSQ_hi, start=True, stop=False)
                    pe.wait_ge(x_klo, c * H + h + 1)
                    mm(bank(5), onesr[:], KSQ_lo, start=False, stop=True).then_inc(x_ksum, 1)

                for h in range(H + 1):
                    if h < H:
                        if h >= 2:
                            pe.wait_ge(x_qcp, c * H + h - 1)
                            pe.wait_ge(x_qhi, c * H + h - 1)
                        for k in range(KD):
                            last = mm(bank(h % 2), xq_w[:, k, h * HD:(h + 1) * HD], XT[:, k, :], start=k == 0, stop=k == 1)
                        last.then_inc(x_qmm, 1)
                    if h == 1:
                        pe.wait_ge(const_v, 2)
                    if h >= 1:
                        q_sums(h - 1)
                        k_sums(h - 1)
                    if h < H:
                        if h >= 2:
                            pe.wait_ge(x_krdy, c * H + h - 1)
                        if h == 0:
                            pe.wait_ge(d_ctxT, c * 16 + 16)
                        mm(bank(2 + h % 2), xk_w[:, h * HD:(h + 1) * HD], ctxT[:], start=True, stop=True).then_inc(x_kmm, 1)
                pe.wait_ge(x_qcp, c * H + H)

                def score1(u, n):
                    score(U1, u, n, lambda h, b: qT[:, 2 * u + h, b * T:(b + 1) * T],
                          lambda h, b: kT[:, 2 * u + h, b * T:(b + 1) * T], T, deep=True)

                pe.wait_ge(x_krdy, c * H + 2)
                score1(0, c * NU)
                pe.wait_ge(x_krdy, c * H + H)
                transposes(1, c + 1, 2)
                q_rms(c, 0)
                pe.wait_ge(xt_ready, c + NC + 2)
                score1(1, c * NU + 1)
                for u in range(NU):
                    n = c * NU + u
                    if u < NU - 2:
                        score1(u + 2, n + 2)
                    turn(U1, u, n, T)
                    if u >= 1:
                        project(U1, 1, c, u - 1, n - 1, lambda h: xvo_w[:, h, :], (0,))
                    if u == 0:
                        pe.wait_ge(d_ctxN, c * 16 + 16)
                    weigh(U1, u, n, T)
                    if u >= 1:
                        project(U1, 1, c, u - 1, n - 1, lambda h: xvo_w[:, h, :], (1,))
                project(U1, 1, c, NU - 1, c * NU + NU - 1, lambda h: xvo_w[:, h, :])

            def ffn(i, L, sizes, weights):
                nj = len(sizes)
                hi, lo = xt_parts[i]
                splits = NC * i
                products = [(w, hi) for w in weights] + [(weights[0], lo)]

                def chunk(c, more):
                    for j in range(nj + 2):
                        if j < nj:
                            if j >= 2:
                                pe.wait_ge(f_hid[i], c * nj + j - 1)
                            if j == 0:
                                pe.wait_ge(x_hi[i], c + 1 + splits)
                            for n, (w, x) in enumerate(products):
                                if j == 0 and x is lo:
                                    pe.wait_ge(x_lo[i], c + 1 + splits)
                                for s in range(2):
                                    for k in range(KD):
                                        last = mm(ps[:, 2 * s + j % 2, :], w[s][:, k, j * P:(j + 1) * P], x[:, k, :],
                                                  start=n == 0 and k == 0, stop=n == len(products) - 1 and k == 1,
                                                  skip_group_check=True)
                            last.then_inc(f_mm[i], 1)
                        if j == 4 and more:
                            transposes(L, c + 1, 4)
                        if j >= 2:
                            q, m = j - 2, sizes[j - 2]
                            pe.wait_ge(h_hi[i], c * nj + q + 1)
                            if q == 0:
                                pe.wait_ge(y_read, c + L * NC + 1)
                            downs = [(hid_hi, w) for w in weights] + [(hid_lo, weights[0])]
                            for n, (h, w) in enumerate(downs):
                                if h is hid_lo:
                                    pe.wait_ge(h_lo[i], c * nj + q + 1)
                                for t in range(CT):
                                    last = mm(Yp[:, t, :], h[0:m, q % 2, t * P:(t + 1) * P], w[2][0:m, q, :],
                                              start=n == 0 and q == 0 and t % 2 == 0, stop=n == len(downs) - 1 and q == nj - 1,
                                              skip_group_check=True)
                            last.then_inc(y_done if q == nj - 1 else f_down[i], 1)

                with pe.Fori(0, NC if i == 0 else NC - 1) as c:
                    chunk(c, True)
                if i == 1:
                    chunk(NC - 1, False)

            pe.wait_ge(f0_cvt, 1)
            ffn(0, 2, [P] * FF0, [(f0g_w, f0u_w, f0d_w)])
            pe.wait_ge(xt_ready, 3 * NC + 1)

            pe.wait_ge(d_l1o, 32)
            for h in range(H):
                if h >= 2:
                    pe.wait_ge(fuse_cp, H + h - 1)
                for k in range(KD):
                    last = mm(bank(h % 2, D), g_wgT[:, 2 * (h // 4) + k, (h % 4) * P:(h % 4 + 1) * P],
                              g_wo[:, 2 * (h // 4) + k, :], start=k == 0, stop=k == 1)
                last.then_inc(fuse_mm, 1)
            pe.wait_ge(d_x1o, 16 * 6)
            for h in range(H):
                b = 2 * (h % 2)
                pe.wait_ge(fuse_cp, 2 * H if h < 2 else 2 * H + h - 1)
                for k in range(KD):
                    mm(ps[:, b, k * P:(k + 1) * P], x1_qT[:, h, k * P:(k + 1) * P], x1_kT[:, h // 2, :],
                       start=True, stop=True, skip_group_check=True)
                mm(ps[:, b + 1, 0:D], x1_vT[:, h // 2, :], x1_o(h), start=True, stop=True).then_inc(fuse_mm, 1)
            pe.wait_ge(fuse_cp, 3 * H)
            pe.wait_ge(d_l1, 16 * 5)
            with pe.Fori(0, NC) as c:
                pe.wait_ge(xt_ready, c + 3 * NC + 1)
                for k in range(KD):
                    last = mm(ps[0:64, 2, :], cq_w[:, k, :], XT[:, k, :], start=k == 0, stop=k == 1)
                last.then_inc(l_qcmm, 1)
                for k in range(KD):
                    last = mm(bank(0), k1_w[:, k, :], XT[:, k, :], start=k == 0, stop=k == 1)
                    if k == 1:
                        last.then_inc(l_kmm, 1)
                for b in range(CB):
                    for k in range(KD):
                        last = mm(ps[0:64, 4 + b // 4, (b % 4) * P:(b % 4 + 1) * P], XT[:, k, b * T:(b + 1) * T],
                                  v1_w[:, k, :], start=k == 0, stop=k == 1, skip_group_check=True)
                last.then_inc(l_vmm, 1)
                pe.wait_ge(l_ksq, c + 1)
                pe.wait_ge(l_qc, c + 1)
                mm(bank(2), ones[:], l1k[:, :], start=True, stop=True).then_inc(l_ksum, 1)
                for m in range(16):
                    for k in range(KD):
                        last = mm(ps[0:32, 3, 0:HD], XT[:, k, m:CN:16], comp_w[:, KD * m + k, :],
                                  start=(m == 0 and k == 0), stop=(m == 15 and k == 1))
                last.then_inc(l_ckmm, 1)
                pe.wait_ge(l_v, c + 1)
                pe.wait_ge(l_keys, 2 * c + 1)

                def qsums(h):
                    pe.wait_ge(l_qsq, c * H + h + 1)
                    mm(ps[0:H, 4, :], onehot[:, h, :], SQ[:, h % 2, :], start=h == 0, stop=h == H - 1,
                       skip_group_check=True).then_inc(l_qsum, 1)

                for h in range(H + 1):
                    if h < H:
                        if h == 2:
                            pe.wait_ge(l_ckv, c + 1)
                            mm(ps[:, 3, 0:1], ident[:], ones[:, 0:1], start=True, stop=True)
                            pe.transpose(ps[:, 3, 0:32], ckv[:], ident[0:32, 0:32]).then_inc(l_ckT, 1)
                        if h == 3:
                            pe.wait_ge(l_keys, 2 * c + 2)
                        if h >= 4:
                            pe.wait_ge(l_qhalf, c * H + h - 3)
                            pe.wait_ge(l_qrest, c * H + h - 3)
                        mm(bank(h % 4), up_w[0:64, h, :], qcT[0:64, :], start=True, stop=True).then_inc(l_qmm, 1)
                    if h >= 1:
                        qsums(h - 1)
                pe.wait_ge(l_qhalf, c * H + H - 2)
                pe.wait_ge(l_qrest, c * H + H - 2)

                def score3(u, n):
                    if u <= 1:
                        pe.wait_ge(l_qrdy, c * H + (2, H)[u])
                    score(U3, u, n, lambda h, b: qT[:, 2 * u + h, b * T:(b + 1) * T], lambda h, b: keysT[:, b, :], W1, deep=True)

                score3(0, c * NU)
                pe.wait_ge(l_qhalf, c * H + H)
                pe.wait_ge(l_qrest, c * H + H)
                transposes(3, c + 1, 2)
                q_rms(c, 1)
                pe.wait_ge(xt_ready, c + 3 * NC + 2)
                score3(1, c * NU + 1)
                for u in range(NU):
                    n = c * NU + u
                    if u < NU - 2:
                        score3(u + 2, n + 2)
                    turn(U3, u, n, W1)
                    if u >= 1:
                        project(U3, 3, c, u - 1, n - 1, lambda h: go_w[:, h, :], (0,))
                    if u == 0:
                        pe.wait_ge(d_ck, 16 * CB * c + 16 * CB)
                    weigh(U3, u, n, W1, lambda b: vals[0:W1, b, :])
                    if u >= 1:
                        project(U3, 3, c, u - 1, n - 1, lambda h: go_w[:, h, :], (1,))
                project(U3, 3, c, NU - 1, c * NU + NU - 1, lambda h: go_w[:, h, :])

            def query(c, u):
                if u >= 1:
                    pe.wait_ge(U4.q_ready, c * NU + u)
                pe.wait_ge(x1a_cut, 2 * u + 2)
                if u == 0:
                    pe.wait_ge(x_hi[1], c + 1)
                (w_hi, w_lo), (hi, lo) = x1a_parts, xt_parts[1]
                for p, (w, x) in enumerate(((w_hi, hi), (w_lo, hi), (w_hi, lo))):
                    if u == 0 and x is lo:
                        pe.wait_ge(x_lo[1], c + 1)
                    for h in range(2):
                        for k in range(KD):
                            last = mm(bank(h), w[:, KD * (2 * u + h) + k, :], x[:, k, :], start=p == 0 and k == 0,
                                      stop=p == 2 and k == 1, skip_group_check=True)
                last.then_inc(U4.q_mm, 1)

            def cross1(c, more):
                for u in range(NU + 2):
                    n = c * NU + u
                    if u < NU:
                        pe.wait_ge(U4.q_ready, n + 1)
                        if u == 0:
                            pe.wait_ge(d_ctxT, c * 16 + 16 * NC + 16)
                        score(U4, u, n, lambda h, b: q1T[:, u % 2, h * CN + b * T:h * CN + (b + 1) * T],
                              lambda h, b: ctxT[:, b * T:(b + 1) * T], T, mask=vmaskb[:, bass.ts(c, CT), :])
                    if 1 <= u <= NU:
                        turn(U4, u - 1, n - 1, T)
                    if u == NU:
                        transposes(4, c + 1)
                    if u < NU - 1:
                        query(c, u + 1)
                    if NU - 1 <= u <= NU:
                        project(U4, 4, c, u - 2, n - 2, lambda h: x1vo_w[:, h, :], (0,))
                    if u == 1:
                        pe.wait_ge(d_ctxN, c * 16 + 16 * NC + 16)
                    if 1 <= u <= NU:
                        weigh(U4, u - 1, n - 1, T)
                    if u == NU + 1 and more:
                        query(c + 1, 0)
                    if u >= 2:
                        project(U4, 4, c, u - 2, n - 2, lambda h: x1vo_w[:, h, :], (1,) if NU - 1 <= u <= NU else (0, 1))

            query(0, 0)
            with pe.Fori(0, NC - 1) as c:
                cross1(c, True)
            cross1(NC - 1, False)

            pe.wait_ge(f1_cvt, 14)
            ffn(1, 5, FF1_SIZES, f1_w)

        @block.scalar
        def _(act):
            act_ = act.activation

            def xt_copy(L, c, b=0):
                act.wait_ge(xt_psum, c + L * NC + 2)
                act_(XT[:], two(b), ACT.Copy).then_inc(xt_ready, 1)

            def ln_rstd(L, c):
                act.wait_ge(ln_var, c + L * NC + 1)
                act_(std[:], mv[:, :, 1], ACT.Ln).then_inc(ln_log, 1)
                act.wait_ge(ln_log, c + L * NC + 1)
                act_(rstd[:], std[:], ACT.Exp, scale=-0.5).then_inc(ln_std, 1)

            def unit_copy(U, u, n, w):
                act.wait_ge(U.t_done, n + 1)
                if u >= 1:
                    act.wait_ge(U.v_done, n)
                if w == T:
                    act_(PT[:, 0:CN].rearrange("p (h m) -> p h m", h=2), ps[:, 4:6, 0:2 * P], ACT.Copy).then_inc(U.pt_ready, 1)
                else:
                    act_(PT[0:w, :].rearrange("p (h m) -> p h m", h=2), ps[0:w, 4:6, :], ACT.Copy).then_inc(U.pt_ready, 1)

            def out_copy(U, u, n, per):
                act.wait_ge(U.v_done, n + 1)
                if u >= 2:
                    act.wait_ge(U.o_done, per)
                dst = OT[:, u % 2, :].rearrange("p (h g q m) -> p q h g m", h=2, g=2, q=2)[:, 1]
                act_(dst, ps[:, 5, :].rearrange("p (h g m) -> p h g m", h=2, g=2), ACT.Copy).then_inc(U.ot_ready2, 1)

            def q_rms(n, k, scale, bias):
                act_(rrow[:], ps[0:H, 4, :], ACT.Ln, scale=scale, bias=bias).then_inc(r_ln, 1)
                act.wait_ge(r_ln, n + k * NC + 1)
                act_(rrow[:], rrow[:], ACT.Exp, scale=-0.5).then_inc(r_row, 1)

            act.preload_act_table_set("natural_log_exp_and_others")
            xt_copy(0, 0)
            with act.Fori(0, NC) as c:
                for i in range(2):
                    act.wait_ge(a0_mm, c * 3 + i + 2)
                    act_(q0T[:, i, :], bank((2, 0)[i]), ACT.Copy).then_inc(a0_q, 1)
                for u in range(NU + 1):
                    n = c * NU + u
                    if u == 5:
                        ln_rstd(0, c)
                    if u < NU:
                        act.wait_ge(U0.sub, n + 1)
                        act_(e0[:, u % 2, :], e0[:, u % 2, :], ACT.Exp, scale=0.25).then_inc(U0.exp, 1)
                    if u >= 1:
                        act.wait_ge(U0.t_done, n)
                        if u >= 2:
                            act.wait_ge(U0.v_done, n - 1)
                        act_(PT[:, 0:CN], bank(4), ACT.Copy).then_inc(U0.pt_ready, 1)
                xt_copy(0, c + 1)
            for h in range(H):
                act.wait_ge(fuse_mm, h + 1)
                act_(xvo_w[:, h, :], bank(h % 2, D), ACT.Copy).then_inc(fuse_cp, 1)
            act.wait_ge(const_v, 2)
            with act.Fori(0, NC) as c:
                for h in range(H + 1):
                    if h < H:
                        act.wait_ge(x_qmm, c * H + h + 1)
                        if h >= 2:
                            act.wait_ge(x_qlo, c * H + h - 1)
                        act_(SQ[:, h % 2, :], bank(h % 2), ACT.Square)
                        if h >= 1:
                            act.wait_ge(x_qsum, c * H + h)
                        act_(SQ_hi, bank(h % 2), ACT.Square).then_inc(x_qhi, 1)
                        if h == 5:
                            ln_rstd(1, c)
                    if h >= 1:
                        act.wait_ge(x_ksum, c * H + h)
                        if h >= 2:
                            act.wait_ge(x_krs, c * H + h - 1)
                        act_(krms, bank(5), ACT.Ln, scale=1.0 / HD, bias=eps5[:, 0:1]).then_inc(x_kln, 1)
                    if h < H:
                        act.wait_ge(x_kmm, c * H + h + 1)
                        if h >= 2:
                            act.wait_ge(x_klo, c * H + h - 1)
                        act_(KSQ[:, h % 2, :], bank(2 + h % 2), ACT.Square)
                        act_(KSQ_hi, bank(2 + h % 2), ACT.Square).then_inc(x_khi, 1)
                    if h >= 1:
                        act.wait_ge(x_kln, c * H + h)
                        if h >= 2:
                            act.wait_ge(x_krdy, c * H + h - 1)
                        act_(krs, krms, ACT.Exp, scale=-0.5).then_inc(x_krs, 1)
                act.wait_ge(x_qsum, c * H + H)
                q_rms(c, 0, 1.0 / HD, eps5[0:H, 0:1])
                xt_copy(1, c + 1, 2)
                for u in range(NU + 1):
                    n = c * NU + u
                    if u == 1:
                        unit_copy(U1, 0, n - 1, T)
                    if u < NU:
                        act.wait_ge(U1.sub, n + 1)
                        act_(E64[:, u % 2], E64[:, u % 2], ACT.Exp, scale=HD ** -0.5).then_inc(U1.exp, 1)
                    if u >= 2:
                        unit_copy(U1, u - 1, n - 1, T)
                    if u >= 1:
                        out_copy(U1, u - 1, n - 1, c * (NU - 1) + u - 2)

            def x_high(i):
                act_(xt_parts[i][0], XT[:], ACT.Copy).then_inc(x_hi[i], 1)

            def ffn(i, L, sizes, sg):
                nj = len(sizes)

                splits = NC * i

                def chunk(c, more):
                    for j in range(nj + 1):
                        if j < nj:
                            m = sizes[j]
                            act.wait_ge(f_mm[i], c * nj + j + 1)
                            if j >= 2:
                                act.wait_ge(h_lo[i], c * nj + j - 1)
                            act_(silu_b[0:m, j % 2, :], ps[0:m, j % 2, :], ACT.Silu, scale=sg[0:m, j:j + 1]).then_inc(f_silu[i], 1)
                        if j >= 1:
                            m = sizes[j - 1]
                            act.wait_ge(f_hid[i], c * nj + j)
                            if j >= 3:
                                act.wait_ge(f_down[i], c * (nj - 1) + j - 2)
                            act_(hid_hi[0:m, (j - 1) % 2, :], silu_b[0:m, (j - 1) % 2, :], ACT.Copy).then_inc(h_hi[i], 1)
                        if j == 3:
                            act.preload_act_table_set("natural_log_exp_and_others")
                            ln_rstd(L, c)
                        if j == 5 and more:
                            act.wait_ge(x_lo[i], c + 1 + splits)
                            xt_copy(L, c + 1, 4)
                    if more:
                        act.wait_ge(xt_ready, c + L * NC + 2)
                        x_high(i)

                if i == 0:
                    act.wait_ge(xt_ready, L * NC + 1)
                    x_high(i)
                with act.Fori(0, NC if i == 0 else NC - 1) as c:
                    chunk(c, True)
                if i == 1:
                    chunk(NC - 1, False)
                act.preload_act_table_set("natural_log_exp_and_others")

            ffn(0, 2, [P] * FF0, sg0)
            for h in range(H):
                act.wait_ge(fuse_mm, H + h + 1)
                act_(go_w[:, h, :], bank(h % 2, D), ACT.Copy).then_inc(fuse_cp, 1)
            act.wait_ge(x_lo[0], NC + 1)
            for h in range(H):
                b = 2 * (h % 2)
                act.wait_ge(fuse_mm, 2 * H + h + 1)
                act_(x1a_w[:, KD * h:KD * h + KD, :], ps[:, b, 0:D].rearrange("p (k m) -> p k m", k=KD), ACT.Copy).then_inc(a_own, 1)
                act_(x1vo_w[:, h, :], ps[:, b + 1, 0:D], ACT.Copy).then_inc(fuse_cp, 1)
            act_(sinkexp[:], sinkexp[:], ACT.Exp).then_inc(const_a, 1)
            with act.Fori(0, NC) as c:
                act.wait_ge(l_qcmm, c + 1)
                act_(qcT[0:64, :], ps[0:64, 2, :], ACT.Copy).then_inc(l_qc, 1)
                act.wait_ge(l_kmm, c + 1)
                act_(l1k, bank(0), ACT.Square).then_inc(l_ksq, 1)
                ln_rstd(3, c)
                act.wait_ge(l_ksum, c + 1)
                act_(l1k, bank(2), ACT.Ln, scale=1.0 / HD, bias=eps6[:, 0:1]).then_inc(l_kln, 1)
                act.wait_ge(l_kln, c + 1)
                act_(l1k, l1k, ACT.Exp, scale=-0.5).then_inc(l_krs, 1)
                act.wait_ge(l_ckmm, c + 1)
                act_(ckt[:], ps[0:32, 3, 0:HD], ACT.Square, accum_out=cks[:, 0:1]).then_inc(l_ckss, 1)
                act.wait_ge(l_ckss, c + 1)
                act_(cks[:, 1:2], cks[:, 0:1], ACT.Ln, scale=1.0 / HD, bias=eps6[0:32, 0:1]).then_inc(l_ckln, 1)
                act.wait_ge(l_ckln, c + 1)
                act_(cks[:, 2:3], cks[:, 1:2], ACT.Exp, scale=-0.5).then_inc(l_ckrs, 1)
                for h in range(H):
                    act.wait_ge(l_qmm, c * H + h + 1)
                    if h >= 2:
                        act.wait_ge(l_qsum, c * H + h - 1)
                    act_(SQ[:, h % 2, :], bank(h % 4), ACT.Square).then_inc(l_qsq, 1)
                    act_(qT[64:P, h, :], ps[64:P, h % 4, :], ACT.Copy).then_inc(l_qrest, 1)
                act.wait_ge(l_qsum, c * H + H)
                q_rms(c, 1, 1.0, eps6b[0:H, 0:1])
                xt_copy(3, c + 1, 2)
                for u in range(NU + 1):
                    n = c * NU + u
                    if u == 1:
                        unit_copy(U3, 0, n - 1, W1)
                    if u < NU:
                        act.wait_ge(U3.s_free, n + 1)
                        act_(E[:, u % 2, :, :, 0:T], E[:, u % 2, :, :, 0:T], ACT.Tanh, scale=1.0 / 50.0).then_inc(U3.tanh, 1)
                        act.wait_ge(U3.tanh, n + 1)
                        for h in range(2):
                            act_(E[:, u % 2, h, :, 0:T], E[:, u % 2, h, :, 0:T], ACT.Exp, scale=50.0,
                                 bias=sinkneg[:, 2 * u + h:2 * u + h + 1]).then_inc(U3.exp, 1)
                        act.wait_ge(U3.sub, n + 1)
                        act_(cb[:], cb[:], ACT.Exp).then_inc(U3.cexp, 1)
                    if u == NU:
                        act.preload_act_table_set("natural_log_exp_and_others")
                    if u >= 2:
                        unit_copy(U3, u - 1, n - 1, W1)
                    if u >= 1:
                        out_copy(U3, u - 1, n - 1, c * (NU - 1) + u - 2)
            act.wait_ge(xt_ready, 4 * NC + 1)
            x_high(1)
            def cross1(c, first):
                def q_copy(u, n):
                    act.wait_ge(U4.q_mm, n + 1)
                    if u >= 2:
                        act.wait_ge(U4.s_done, n - 1)
                    act_(q1T[:, u % 2, :].rearrange("p (h m) -> p h m", h=2), two(0), ACT.Copy).then_inc(U4.q_ready, 1)

                q_copy(0, c * NU)
                if first:
                    ln_rstd(4, c)
                for u in range(NU + 1):
                    n = c * NU + u
                    if u == 0:
                        q_copy(1, n + 1)
                    if u in (1, NU - 1):
                        unit_copy(U4, u - 1, n - 1, T)
                    if u == 4 and not first:
                        ln_rstd(4, c)
                    if u < NU:
                        act.wait_ge(U4.s_free, n + 1)
                        act_(E64[:, u % 2], E64[:, u % 2], ACT.Exp, scale=HD ** -0.5).then_inc(U4.exp, 1)
                    if 2 <= u and u != NU - 1:
                        unit_copy(U4, u - 1, n - 1, T)
                    if u == NU:
                        act.wait_ge(x_lo[1], c + 1)
                        xt_copy(4, c + 1)
                        act.wait_ge(xt_ready, c + 4 * NC + 2)
                        x_high(1)
                    if 1 <= u < NU - 1:
                        q_copy(u + 1, n + 1)
                    if u >= 1:
                        out_copy(U4, u - 1, n - 1, c * (NU - 1) + u - 2)

            cross1(0, True)
            with act.Fori(1, NC) as c:
                cross1(c, False)
            ffn(1, 5, FF1_SIZES, sg1)
            ln_rstd(6, 0)

        @block.vector
        def _(v):
            order = Order(v, v_own)
            tt, ts_, red = v.tensor_tensor, v.tensor_scalar, v.tensor_reduce

            def ln_sum(L, c, scale_row=None):
                v.wait_ge(y_done, c + L * NC + 1)
                if scale_row is None:
                    tt(Y[:], Yp, X[:, bass.ts(c, CT), :], ALU.add).then_inc(y_read, 1)
                else:
                    tt(Y[:], Yp, scale_row.unsqueeze(1).broadcast_to([P, CT, D]), ALU.mult).then_inc(y_read, 1)
                v.wait_ge(y_read, c + L * NC + 2)
                if scale_row is not None:
                    order.then(tt(Y[:], Y[:], X[:, bass.ts(c, CT), :], ALU.add))

            def ln_stats(tiles):
                for t in tiles:
                    order.then(v.bn_stats(bst[:, t, :], Y[:, t, :]))

            def ln_variance():
                for t in range(CT):
                    v.tensor_copy(sm[:, 0:1], eps5[:])
                    order.then(v.bn_aggr(mv[:, t, :], bst[:, t, :]))
                ts_(mv[:, :, 1], mv[:, :, 1], LN_EPS, None, ALU.add).then_inc(ln_var, 1)

            def ln_apply(L, c, tiles):
                v.wait_ge(ln_std, c + L * NC + 2)
                for t in tiles:
                    ins = ts_(X[:, bass.ds(c * CT + t, 1), :].rearrange("p a d -> p (a d)"), Y[:, t, :], mv[:, t, 0:1], rstd[:, t:t + 1], ALU.subtract, ALU.mult)
                    if t < CT - 1:
                        order.then(ins)
                    else:
                        ins.then_inc(ln_done, 1)
                        v.wait_ge(ln_done, c + L * NC + 1)

            def ln_rest(L, c):
                ln_stats(range(CT))
                ln_variance()
                ln_apply(L, c, range(CT))

            def layer_norm(L, c):
                ln_sum(L, c)
                ln_rest(L, c)

            LN_N = 4 + 4 + 3

            def bc(small, k=T, a_=2, b_=CT):
                return small.rearrange("p (a b) -> p a b", a=a_).unsqueeze(3).broadcast_to([P, a_, b_, k])

            def out_copy(U, u, n, per):
                v.wait_ge(U.v_done, n + 1)
                if u >= 2:
                    v.wait_ge(U.o_done, per)
                dst = OT[:, u % 2, :].rearrange("p (h g q m) -> p q h g m", h=2, g=2, q=2)[:, 0]
                v.tensor_copy(dst, ps[:, 4, :].rearrange("p (h g m) -> p h g m", h=2, g=2)).then_inc(U.ot_ready, 1)

            v.memset(mv[:], 1.0).then_inc(ln_var, 1)
            v.memset(eps5[:], 1e-5).then_inc(y_read, 1)
            v.wait_ge(d_early, 48)
            order.then(v.tensor_copy(identb[:], ident[:]))
            v.tensor_copy(causalb[:], causal[:].unsqueeze(1).broadcast_to([P, 8, T])).then_inc(const_v, 1)
            v.wait_ge(const_g, 2)

            v.wait_ge(d_a0, 96)
            for f in range(2):
                w = a0q_w[:, KD * f:KD * f + KD, :]
                order.then(tt(w, w, rot0[:, f, :].unsqueeze(1).broadcast_to([P, KD, D]), ALU.mult))
            tt(a0q_w[:, 0:KD, :], a0q_w[:, 0:KD, :], a0q_w[:, KD:2 * KD, :], ALU.add).then_inc(a0_w, 1)

            def self0(c, first):
                v.wait_ge(a0_mm, c * 3 + 1)
                v.tensor_copy(k0T, bank(1)).then_inc(a0_k, 1)
                v.wait_ge(a0_v, c + 1)
                for j in range(2):
                    cp = v.tensor_copy(v0bd[64 * j:64 * j + 64, :, 16 * j:16 * j + 16],
                                       ps[64 * j:64 * j + 64, 4, 0:CB * 32].rearrange("p (b n) -> p b n", n=32)[:, :, 16 * j:16 * j + 16])
                    if j == 0:
                        order.then(cp)
                cp.then_inc(a0_vbd, 1)
                def front0(u, n):
                    e = e0[:, u % 2, :].rearrange("p (h k) -> p h k", k=T)
                    s = bank(2 + u % 2).rearrange("p (h k) -> p h k", k=T)
                    v.wait_ge(U0.s_done, n + 1)
                    if u >= 1:
                        v.wait_ge(U0.sub, n)
                    order.then(red(mx[:], s, AX.X, ALU.max))
                    if u >= 2:
                        v.wait_ge(U0.t_done, n - 1)
                    tt(e, s, b8(mx[:]), ALU.subtract).then_inc(U0.sub, 1)

                b8 = lambda x: x.unsqueeze(2).broadcast_to([P, 8, T])
                front0(0, c * NU)
                for u in range(NU):
                    n = c * NU + u
                    if u < NU - 1:
                        front0(u + 1, n + 1)
                    e = e0[:, u % 2, :].rearrange("p (h k) -> p h k", k=T)
                    v.wait_ge(U0.exp, n + 1)
                    order.then(red(sm[:], e, AX.X, ALU.add))
                    order.then(v.reciprocal(rs[:], sm[:]))
                    tt(e, e, b8(rs[:]), ALU.mult).then_inc(U0.p_ready, 1)
                    if u >= 1:
                        v.wait_ge(U0.v_done, n)
                        if u >= 3:
                            v.wait_ge(U0.o_done, c * (NU - 1) + u - 2)
                        v.tensor_copy(OT[:, (u - 1) % 2, 0:P], ps[:, 5, 0:P]).then_inc(U0.ot_ready, 1)
                    if not first:
                        if u < CT:
                            ln_stats((u,))
                        if u == 4:
                            ln_variance()
                        if u in (6, 7):
                            ln_apply(0, c - 1, (2 * u - 12, 2 * u - 11))
                v.wait_ge(U0.v_done, c * NU + NU)
                v.wait_ge(U0.o_done, c * (NU - 1) + NU - 2)
                v.tensor_copy(OT[:, (NU - 1) % 2, 0:P], ps[:, 5, 0:P]).then_inc(U0.ot_ready, 1)
                ln_sum(0, c)

            self0(0, True)
            with v.Fori(1, NC) as c:
                order.enter(c - 1, 1 + NU * 3 + LN_N)
                self0(c, False)
            order.leave(NC - 1)

            def softmax_front(U, u, n, scale=None, deep=False):
                b = 2 * (u % 2) if deep else 2
                s = ps[:, b:b + 2, 0:CT * T].rearrange("p h (t k) -> p h t k", k=T)
                e = E64[:, u % 2]
                v.wait_ge(U.s_done, n + 1)
                order.then(red(mx[:].rearrange("p (h t) -> p h t", h=2), s, AX.X, ALU.max))
                if u >= 2:
                    v.wait_ge(U.t_done, n - 1)
                tt(e, s, bc(mx[:]), ALU.subtract).then_inc(U.s_free, 1)
                if scale is not None:
                    v.wait_ge(U.s_free, n + 1)
                    tt(e, e, scale, ALU.mult).then_inc(U.sub, 1)

            def softmax_back(U, u, n, any_=None):
                e = E64[:, u % 2]
                v.wait_ge(U.exp, n + 1)
                order.then(red(sm[:].rearrange("p (h t) -> p h t", h=2), e, AX.X, ALU.add))
                order.then(v.reciprocal(rs[:], sm[:]))
                if any_ is not None:
                    order.then(tt(rs[:].rearrange("p (h t) -> p h t", h=2), rs[:].rearrange("p (h t) -> p h t", h=2),
                                  any_, ALU.mult))
                tt(e, e, bc(rs[:]), ALU.mult).then_inc(U.p_ready, 1)

            def rq_copy(n, k):
                v.wait_ge(r_T, n + k * NC + 1)
                v.tensor_copy(rq[:].rearrange("p t h -> p (t h)"), ps[:, 4, 0:CT * H]).then_inc(r_rq, 1)
                v.wait_ge(r_rq, n + k * NC + 1)

            def rq_of(u, w):
                return rq[:, :, 2 * u:2 * u + 2].rearrange("p t h -> p h t").unsqueeze(3).broadcast_to([P, 2, CT, w])

            v.wait_ge(d_const, N_CONST)
            order.then(v.tensor_copy(onesr[:], ones[:]))
            order.then(ts_(pick[:, 0:P], ones[:], 0.0, None, ALU.mult))
            order.then(ts_(pick[:, P:P + H], ones[:, 0:H], 0.0, None, ALU.mult))
            order.then(v.tensor_copy(pick[:, H - 1:H], ones[:, 0:1]))
            order.then(v.memset(eps6[:], 1e-6))
            order.then(v.memset(eps6b[:], 1e-6 * HD))
            order.then(tt(gqk_c, gq_c, gk_c, ALU.mult))
            order.then(tt(qkw_c, qw_c, kw_c, ALU.mult))
            order.then(ts_(vmaskb[:], vmask8, -1.0, 1e30, ALU.add, ALU.mult))
            order.then(red(anykey[:], vmask8, AX.X, ALU.max))
            order.then(ts_(sinkneg[:], sinkB[:], 0.0, -1.0, ALU.max, ALU.mult))
            tt(sinkexp[:], sinkB[:], sinkneg[:], ALU.add).then_inc(const_v, 1)
            v.wait_ge(const_v, 2)

            v.wait_ge(f0_cvt, 1)
            def cross0(c, ln_chunk):
                for h in range(H + 1):
                    if h < H:
                        v.wait_ge(x_qhi, c * H + h + 1)
                        v.tensor_copy(qT[:, h, :], bank(h % 2)).then_inc(x_qcp, 1)
                        tt(SQ_lo, SQ[:, h % 2, :], SQ_hi.bitcast(F32), ALU.subtract).then_inc(x_qlo, 1)
                        v.wait_ge(x_khi, c * H + h + 1)
                        tt(KSQ_lo, KSQ[:, h % 2, :], KSQ_hi.bitcast(F32), ALU.subtract).then_inc(x_klo, 1)
                    if h >= 1:
                        v.wait_ge(x_krs, c * H + h)
                        v.scalar_tensor_tensor(out=kT[:, h - 1, :], in0=bank(2 + (h - 1) % 2), scalar=gqk_c, in1=krs,
                                               op0=ALU.mult, op1=ALU.mult).then_inc(x_krdy, 1)
                    if h in (2, 3):
                        ln_stats((2 * h - 4, 2 * h - 3))
                    if h == 4:
                        ln_variance()
                    if h in (6, 7):
                        ln_apply(*ln_chunk, (2 * h - 12, 2 * h - 11))
                rq_copy(c, 0)
                for u in range(NU + 1):
                    n = c * NU + u
                    if u < NU:
                        softmax_front(U1, u, n, rq_of(u, T), deep=True)
                        softmax_back(U1, u, n)
                    if u >= 1:
                        out_copy(U1, u - 1, n - 1, c * (NU - 1) + u - 2)
                ln_sum(1, c)

            cross0(0, (0, NC - 1))
            with v.Fori(1, NC) as c:
                order.enter(c - 1, NU * 3 + LN_N)
                cross0(c, (1, c - 1))
            order.leave(NC - 1)

            def x_low(i, n):
                hi, lo = xt_parts[i]
                v.wait_ge(x_hi[i], n)
                tt(lo, XT[:], hi.bitcast(F32), ALU.subtract).then_inc(x_lo[i], 1)

            def ffn(i, L, sizes, su):
                nj = len(sizes)
                splits = NC * i

                def chunk(c, ln_chunk, more):
                    for j in range(nj + 1):
                        if j < nj:
                            m = sizes[j]
                            v.wait_ge(f_silu[i], c * nj + j + 1)
                            v.scalar_tensor_tensor(out=silu_b[0:m, j % 2, :], in0=ps[0:m, 2 + j % 2, :], scalar=su[0:m, j:j + 1],
                                                   in1=silu_b[0:m, j % 2, :], op0=ALU.mult, op1=ALU.mult).then_inc(f_hid[i], 1)
                        if j >= 1:
                            m = sizes[j - 1]
                            v.wait_ge(h_hi[i], c * nj + j)
                            tt(hid_lo[0:m, (j - 1) % 2, :], silu_b[0:m, (j - 1) % 2, :], hid_hi[0:m, (j - 1) % 2, :].bitcast(F32),
                               ALU.subtract).then_inc(h_lo[i], 1)
                        if j in (1, 2):
                            ln_stats((2 * j - 2, 2 * j - 1))
                        if j == 3:
                            ln_variance()
                        if j in (4, 5):
                            ln_apply(*ln_chunk, (2 * j - 8, 2 * j - 7))
                    if more:
                        x_low(i, c + 2 + splits)
                    ln_sum(L, c, rowsB[:, i, :])

                chunk(0, (L - 1, NC - 1), True)
                trips = NC - 1 if i == 0 else NC - 2
                with v.Fori(1, 1 + trips) as c:
                    order.enter(c - 1, 1 + LN_N)
                    chunk(c, (L, c - 1), True)
                order.leave(trips)
                if i == 1:
                    chunk(NC - 1, (L, NC - 2), False)
                ln_rest(L, NC - 1)

            ffn(0, 2, [P] * FF0, su0)

            v.wait_ge(const_a, 1)
            with v.Fori(0, NC) as c:
                order.enter(c, 4 + NU * 12 + LN_N)
                cosb = cos1[:].unsqueeze(1).broadcast_to([64, CB, T])
                sinb = sin1[:].unsqueeze(1).broadcast_to([64, CB, T])
                r3 = lambda x: x.rearrange("p (b t) -> p b t", t=T)
                v.wait_ge(l_ksq, c + 1)
                order.then(tt(r3(l1t1[0:64, :]), r3(ps[0:64, 0, :]), cosb, ALU.mult))
                order.then(tt(r3(l1t2[0:32, :]), r3(ps[32:64, 0, :]), sinb[32:64], ALU.mult))
                order.then(tt(r3(l1t2[32:64, :]), r3(ps[0:32, 0, :]), sinb[0:32], ALU.mult))
                v.tensor_copy(l1t1[64:P, :], ps[64:P, 0, :])
                order.then(tt(l1t1[0:64, :], l1t1[0:64, :], l1t2[0:64, :], ALU.add))
                v.wait_ge(l_vmm, c + 1)
                v.tensor_copy(vals[0:T, :, :], ps[0:T, 4:6, :].rearrange("p q (b n) -> p (q b) n", n=HD)).then_inc(l_v, 1)
                v.wait_ge(l_krs, c + 1)
                v.scalar_tensor_tensor(out=keysT[:, :, 0:T], in0=r3(l1t1), scalar=qkw_c, in1=r3(l1k),
                                       op0=ALU.mult, op1=ALU.mult).then_inc(l_keys, 1)
                v.wait_ge(l_ckrs, c + 1)
                v.scalar_tensor_tensor(out=ckv[:], in0=ps[0:32, 3, 0:HD], scalar=cks[:, 2:3], in1=kwB[:],
                                       op0=ALU.mult, op1=ALU.mult).then_inc(l_ckv, 1)
                v.wait_ge(l_ckT, c + 1)
                ts_(keysT[:, :, T:W1], ps[:, 3, 0:32].rearrange("p (b n) -> p b n", n=NB), qw_c, None, ALU.mult).then_inc(l_keys, 1)
                for h in range(H):
                    if h >= 2:
                        v.wait_ge(l_qrdy, c * H + h - 1)
                    v.wait_ge(l_qsq, c * H + h + 1)
                    i = h % 4
                    tt(r3(qT[0:64, h, :]), r3(ps[0:64, i, :]), cosb, ALU.mult)
                    tt(r3(SQr[h % 2][0:32, :]), r3(ps[32:64, i, :]), sinb[32:64], ALU.mult)
                    tt(r3(SQr[h % 2][32:64, :]), r3(ps[0:32, i, :]), sinb[0:32], ALU.mult).then_inc(l_qhalf, 1)
                rq_copy(c, 1)
                for u in range(NU + 1):
                    n = c * NU + u
                    if u < NU:
                        s = ps[:, 2 * (u % 2):2 * (u % 2) + 2, 0:CT * W1].rearrange("p h (t k) -> p h t k", k=W1)
                        e, sw = E[:, u % 2], E[:, u % 2, :, :, 0:T]
                        v.wait_ge(U3.s_done, n + 1)
                        if u >= 2:
                            v.wait_ge(U3.t_done, n - 1)
                        tt(e, s, rq_of(u, W1), ALU.mult).then_inc(U3.s_free, 1)
                        v.wait_ge(U3.s_free, n + 1)
                        for h in range(2):
                            order.then(tt(cb[:, h, :, 0:NB], e[:, h, :, T:W1],
                                          blockmask[:].unsqueeze(1).broadcast_to([P, CT, NB]), ALU.add))
                        order.then(v.tensor_copy(cb[:, :, :, NB:NB + 1].rearrange("p h t k -> p h (t k)"),
                                                 sinkB[:, 2 * u:2 * u + 2].unsqueeze(2).broadcast_to([P, 2, CT])))
                        order.then(red(mx[:].rearrange("p (h t) -> p h t", h=2), cb[:], AX.X, ALU.max))
                        tt(cb[:], cb[:], bc(mx[:], NB + 1), ALU.subtract).then_inc(U3.sub, 1)
                        v.wait_ge(U3.exp, 2 * n + 2)
                        for h in range(2):
                            order.then(tt(sw[:, h], sw[:, h], keep[:].unsqueeze(1).broadcast_to([P, CT, T]), ALU.mult))
                        order.then(red(sm[:].rearrange("p (h t) -> p h t", h=2), sw, AX.X, ALU.add))
                        order.then(tt(sm[:].rearrange("p (h t) -> p h t", h=2), sm[:].rearrange("p (h t) -> p h t", h=2),
                                      sinkexp[:, 2 * u:2 * u + 2].unsqueeze(2).broadcast_to([P, 2, CT]), ALU.add))
                        order.then(v.reciprocal(rs[:], sm[:]))
                        order.then(tt(sw, sw, bc(rs[:]), ALU.mult))
                        v.wait_ge(U3.cexp, n + 1)
                        order.then(red(mx[:].rearrange("p (h t) -> p h t", h=2), cb[:], AX.X, ALU.add))
                        order.then(v.reciprocal(sm[:], mx[:]))
                        tt(e[:, :, :, T:W1], cb[:, :, :, 0:NB], bc(sm[:], NB), ALU.mult).then_inc(U3.p_ready, 1)
                    if u >= 1:
                        out_copy(U3, u - 1, n - 1, c * (NU - 1) + u - 2)
                layer_norm(3, c)
            order.leave(NC)

            def cross1(c, first):
                for u in range(NU + 1):
                    n = c * NU + u
                    if u < NU:
                        softmax_front(U4, u, n)
                        softmax_back(U4, u, n, anykey[:, bass.ts(c, CT)].unsqueeze(1).broadcast_to([P, 2, CT]))
                    if u >= 1:
                        out_copy(U4, u - 1, n - 1, c * (NU - 1) + u - 2)
                    if not first:
                        if u in (1, 2):
                            ln_stats((2 * u - 2, 2 * u - 1))
                        if u == 3:
                            ln_variance()
                        if u in (5, 6):
                            ln_apply(4, c - 1, (2 * u - 10, 2 * u - 9))
                x_low(1, c + 2)
                ln_sum(4, c)

            cross1(0, True)
            with v.Fori(1, NC) as c:
                order.enter(c - 1, NU * 4 + LN_N)
                cross1(c, False)
            order.leave(NC - 1)
            ffn(1, 5, FF1_SIZES, su1)


def tables():
    import numpy as np
    f = np.float32
    pos = np.arange(T, dtype=f)
    tok = np.arange(P) % T
    key = np.arange(T)
    seen = key[None, :] <= tok[:, None]
    th0 = (f(1.0) / f(10000.0) ** (np.arange(0, 8, 2, dtype=f) / f(8))).astype(f)
    fr0 = (np.arange(H, dtype=f)[:, None] * th0[None, :]).astype(f)
    part = np.arange(D) % 16
    sign0 = np.where(part % 8 < 4, f(-1), f(1))
    th1 = (f(1.0) / f(10000.0) ** (np.arange(0, 64, 2, dtype=f) / f(64))).astype(f)
    fr1 = (th1[:, None] * pos[None, :]).astype(f)
    sign1 = np.where(np.arange(64) < 32, f(1), f(-1))
    return {
        "c_ident": np.eye(P, dtype=f),
        "c_causal": np.where(seen, f(0), f(NEG)).astype(f),
        "c_keep": seen.astype(f),
        "c_blockmask": np.where(np.arange(NB)[None, :] * 16 + 15 < tok[:, None], f(0), f(NEG)).astype(f),
        "c_cos0": np.cos(fr0)[np.arange(D) // 16, part % 4].astype(f),
        "c_sin0": (np.sin(fr0)[np.arange(D) // 16, part % 4] * sign0).astype(f),
        "c_cos1": np.cos(fr1)[np.arange(64) % 32].astype(f),
        "c_sin1": (np.sin(fr1)[np.arange(64) % 32] * sign1[:, None]).astype(f),
        "c_onehot": np.eye(H, dtype=f).reshape(-1),
        "c_headmask": (np.arange(P)[:, None] // 16 == np.arange(8)[None, :]).astype(f),
    }


def layouts(i):
    import numpy as np
    g = {k: np.asarray(v) for k, v in i.items()}
    straight = np.array([0, 2, 4, 6, 1, 3, 5, 7, 8, 10, 12, 14, 9, 11, 13, 15])
    partner = np.array([1, 3, 5, 7, 0, 2, 4, 6, 9, 11, 13, 15, 8, 10, 12, 14])
    heads = 16 * np.arange(H)[:, None]
    qT, kT = g["L0_attn_Wq"].T, g["L0_attn_Wk"].T
    up = g["L1_attn_Wq_up"]
    col = lambda x: x.reshape(-1, 1)
    row = lambda x: x.reshape(-1)
    words = lambda x: np.ascontiguousarray(x).view(np.int32)
    arrays = {
        "x": g["x"].reshape(NT, P, D),
        "ctx": g["ctx_1024"].reshape(NC, 2, 2, 2, T, P).transpose(0, 2, 4, 1, 3, 5).reshape(NC, P, 4 * P),
        "ctxT": g["ctx_1024"].reshape(B * T, P).T,
        "mask": g["mask_BxS2_bf1"].view(np.uint8),
        "a0_q": np.concatenate([qT[:, (heads + straight).ravel()], qT[:, (heads + partner).ravel()]], 0),
        "a0_k": np.tile(kT[:, straight], (1, 8)),
        "a0_v": g["L0_attn_Wv"].T,
        "a0_o": g["L0_attn_Wo"].T,
        "x0_q": g["L0_xattn_Wq"], "x0_k": g["L0_xattn_Wk"],
        "x0_vT": g["L0_xattn_Wv"].T, "x0_o": g["L0_xattn_Wo"],
        "gq": col(g["L0_xattn_gq"]), "gk": col(g["L0_xattn_gk"]),
        "f0_g": words(g["L0_ffn_w_gate"]), "f0_u": words(g["L0_ffn_w_up"]), "f0_d": words(g["L0_ffn_w_down"]),
        "f0_sg": g["L0_ffn_s_gate"].reshape(FF0, P).T, "f0_su": g["L0_ffn_s_up"].reshape(FF0, P).T, "f0_sd": row(g["L0_ffn_s_down"]),
        "l1_qc": g["L1_attn_Wq_c"], "l1_up": up,
        "l1_k": g["L1_attn_Wk"], "l1_v": g["L1_attn_Wv"],
        "l1_comp": g["L1_attn_W_comp"],
        "qw": col(g["L1_attn_q_norm_w"]), "kw": col(g["L1_attn_k_norm_w"]), "kw_row": row(g["L1_attn_k_norm_w"]),
        "sink": row(g["L1_attn_sink"]),
        "l1_gT": g["L1_attn_Wg"].transpose(0, 2, 1).reshape(4 * D, 4 * HD), "l1_o": g["L1_attn_Wo"],
        "x1_qT": g["L1_xattn_Wq"].T, "x1_kT": g["L1_xattn_Wk"].T, "x1_vT": g["L1_xattn_Wv"].T, "x1_o": g["L1_xattn_Wo"],
        "f1_g": g["L1_ffn_wq_gate"].T, "f1_u": g["L1_ffn_wq_up"].T, "f1_d": g["L1_ffn_wq_down"].T,
        "f1_sg": g["L1_ffn_s_gate"][:640].reshape(5, P).T, "f1_sg_tail": col(g["L1_ffn_s_gate"][640:]),
        "f1_su": g["L1_ffn_s_up"][:640].reshape(5, P).T, "f1_su_tail": col(g["L1_ffn_s_up"][640:]), "f1_sd": row(g["L1_ffn_s_down"]),
        **tables(),
    }
    return {"in_" + k: np.ascontiguousarray(v) for k, v in arrays.items()}


def kernel(**inputs):
    import concourse.bacc as bacc
    from concourse.bass_utils import run_bass_kernel_spmd

    nc = bacc.Bacc("TRN2", target_bir_lowering=False, num_devices=1)
    arrays = layouts(inputs)
    aps = {k[3:]: nc.dram_tensor(k, v.shape, mybir.dt.from_np(v.dtype), kind="ExternalInput").ap() for k, v in arrays.items()}
    out = nc.dram_tensor("out", (NT, P, D), F32, kind="ExternalOutput").ap()
    build(nc, aps, out)
    r = run_bass_kernel_spmd(nc, [arrays], core_ids=[0])
    return r.results[0]["out"].reshape(B, T, D)
```
